# Optimizing a Trainium2 kernel written in Bass

```python
import numpy as np
import jax
import jax.numpy as jnp

def _softmax(x, axis=-1):
    return jax.nn.softmax(x, axis=axis)

def _gelu(x):
    return jax.nn.gelu(x, approximate=True)

def _silu(x):
    return jax.nn.silu(x)

def _sigmoid(x):
    return jax.nn.sigmoid(x)

def _layernorm(x, axis=-1, eps=1e-05):
    m = jnp.mean(x, axis=axis, keepdims=True)
    v = jnp.var(x, axis=axis, keepdims=True)
    return (x - m) / jnp.sqrt(v + eps)

def _scatter_add(tgt, idx, src, axis=0):
    return tgt.at[idx].add(src)

def _segment_sum(src, seg, n):
    return jax.ops.segment_sum(src, seg, n)
kernel_name = 'mk_vit_tower_cls_d1_tok_img768_r4_6041c1'

def setup_inputs(seed: int=0):
    np.random.seed(seed)
    _w = jnp.asarray

    def _rec_inputs():
        import jax
        import jax.numpy as jnp
        _rk = jax.random.key(seed)
        x = 7.57192e-06 + 1.00007 * jax.random.normal(jax.random.fold_in(_rk, 1), (32, 3, 112, 112), jnp.float32)
        cls_tok = 0.02 * jax.random.normal(jax.random.fold_in(_rk, 5), (1, 1, 192), jnp.float32)
        return (x, cls_tok)
    x, cls_tok = _rec_inputs()

    def _L0_tok_setup():
        import jax, jax.numpy as jnp
        import numpy as np
        B, IN, IMG = (64, 3, 224)
        PATCH, LEVELS, D = (16, 4, 192)
        ISQ2 = 0.7071067811865476
        DN = ('NCHW', 'OIHW', 'NCHW')

        def conv(x, w, b=None, stride=1, pad=((0, 0), (0, 0)), groups=1):
            y = jax.lax.conv_general_dilated(x, w, (stride, stride), pad, dimension_numbers=DN, feature_group_count=groups)
            return y if b is None else y + b[None, :, None, None]

        def dwconv(x, wd, wp, bp):
            y = conv(x, wd, pad=((1, 1), (1, 1)), groups=x.shape[1])
            return conv(y, wp, bp)

        def haar_dwt2(x):
            xe, xo = (x[..., ::2], x[..., 1::2])
            lo_w, hi_w = ((xe + xo) * ISQ2, (xe - xo) * ISQ2)

            def split_h(t):
                te, to = (t[..., ::2, :], t[..., 1::2, :])
                return ((te + to) * ISQ2, (te - to) * ISQ2)
            ll, lh = split_h(lo_w)
            hl, hh = split_h(hi_w)
            return (ll, lh, hl, hh)

        def wavelet_packet(x):
            f = x
            for _ in range(LEVELS):
                b, k, h, w = f.shape
                ll, lh, hl, hh = haar_dwt2(f)
                bands = jnp.stack([ll, lh, hl, hh], axis=1)
                bands = bands.reshape(b, 4, k // IN, IN, h // 2, w // 2)
                f = jnp.transpose(bands, (0, 2, 1, 3, 4, 5)).reshape(b, 4 * k, h // 2, w // 2)
            return f

        def gelu(x):
            return jax.nn.gelu(x, approximate=False)

        def forward(x, pl_w, pl_b, pl_dw, pl_pw, pl_pwb, pg_w1, pg_b1, pg_dw, pg_pw, pg_pwb, pg_w2, pg_b2, alpha, f1_dw, f1_pw, f1_pwb, f2_dw, f2_pw, f2_pwb, f3_dw, f3_pw, f3_pwb, ln_g, ln_b, cls):
            loc = conv(x, pl_w, pl_b, stride=PATCH)
            loc = dwconv(gelu(loc), pl_dw, pl_pw, pl_pwb)
            g = wavelet_packet(x)
            g = gelu(conv(g, pg_w1, pg_b1))
            g = gelu(dwconv(g, pg_dw, pg_pw, pg_pwb))
            glob = conv(g, pg_w2, pg_b2)
            gate = 0.5 * (jnp.tanh(alpha) + 1.0)
            h = (1.0 - gate) * loc + gate * glob
            h = jax.nn.relu(dwconv(h, f1_dw, f1_pw, f1_pwb))
            h = jax.nn.relu(dwconv(h, f2_dw, f2_pw, f2_pwb))
            h = dwconv(loc + h, f3_dw, f3_pw, f3_pwb)
            t = jnp.transpose(h.reshape(h.shape[0], D, -1), (0, 2, 1))
            mu = jnp.mean(t, -1, keepdims=True)
            var = jnp.mean((t - mu) ** 2, -1, keepdims=True)
            t = (t - mu) / jnp.sqrt(var + 1e-05) * ln_g + ln_b
            cls_tok = jnp.broadcast_to(cls, (t.shape[0], 1, D))
            return jnp.concatenate([cls_tok, t], axis=1)
        key = jax.random.key(seed)
        ks = jax.random.split(key, 32)

        def rn(i, shape, s=0.02):
            return jax.random.normal(ks[i], shape, jnp.float32) * s
        KW = IN * 4 ** LEVELS
        return {'x': jax.random.normal(ks[0], (B, IN, IMG, IMG), jnp.float32), 'pl_w': rn(1, (D, IN, PATCH, PATCH)), 'pl_b': rn(2, (D,)), 'pl_dw': rn(3, (D, 1, 3, 3)), 'pl_pw': rn(4, (D, D, 1, 1)), 'pl_pwb': rn(5, (D,)), 'pg_w1': rn(6, (D, KW, 1, 1)), 'pg_b1': rn(7, (D,)), 'pg_dw': rn(8, (D, 1, 3, 3)), 'pg_pw': rn(9, (D, D, 1, 1)), 'pg_pwb': rn(10, (D,)), 'pg_w2': rn(11, (D, D, 1, 1)), 'pg_b2': rn(12, (D,)), 'alpha': jnp.zeros((1, D, 1, 1), jnp.float32), 'f1_dw': rn(13, (D, 1, 3, 3)), 'f1_pw': rn(14, (D, D, 1, 1)), 'f1_pwb': rn(15, (D,)), 'f2_dw': rn(16, (D, 1, 3, 3)), 'f2_pw': rn(17, (D, D, 1, 1)), 'f2_pwb': rn(18, (D,)), 'f3_dw': rn(19, (D, 1, 3, 3)), 'f3_pw': rn(20, (D, D, 1, 1)), 'f3_pwb': rn(21, (D,)), 'ln_g': jnp.ones((D,), jnp.float32), 'ln_b': jnp.zeros((D,), jnp.float32), 'cls': rn(22, (1, 1, D))}
    _L0_tok_all = _L0_tok_setup()
    _L0_tok_in = {k: v for k, v in _L0_tok_all.items() if k in ('pl_w', 'pl_b', 'pl_dw', 'pl_pw', 'pl_pwb', 'pg_w1', 'pg_b1', 'pg_dw', 'pg_pw', 'pg_pwb', 'pg_w2', 'pg_b2', 'alpha', 'f1_dw', 'f1_pw', 'f1_pwb', 'f2_dw', 'f2_pw', 'f2_pwb', 'f3_dw', 'f3_pw', 'f3_pwb', 'ln_g', 'ln_b', 'cls')}
    del _L0_tok_all

    def _L0_attn_setup():
        import jax, jax.numpy as jnp
        import numpy as np
        N_HEADS = 12
        key = jax.random.key(seed)
        k1, k2, k3 = jax.random.split(key, 3)
        B, S, W = (8, 256, 192)
        x = jax.random.normal(k1, (B, S, W), dtype=jnp.float32)
        w_qkv = jax.random.normal(k2, (W, 3 * W), dtype=jnp.float32) * W ** (-0.5)
        w_out = jax.random.normal(k3, (W, W), dtype=jnp.float32) * W ** (-0.5)
        return {'x': x, 'w_qkv': w_qkv, 'w_out': w_out}
    _L0_attn_all = _L0_attn_setup()
    _L0_attn_in = {k: v for k, v in _L0_attn_all.items() if k in ('w_qkv', 'w_out')}
    del _L0_attn_all

    def _L0_ffn_setup():
        import jax, jax.numpy as jnp
        import numpy as np
        GT0 = [[0, 1, 0, 0, 1, 0], [0, 1, 0, 0, 0, 1], [0, 0, 1, 0, 1, 0], [0, 0, 1, 0, 0, 1], [0, 0, 0, 1, 1, 0], [0, 0, 0, 1, 0, 1]]
        NCLS = 6
        K = 1

        def _expert_pairs():
            pairs = []
            for i in range(NCLS):
                p = [(j - 1, k - 1) for j in range(1, 6) for k in range(1, 6) if j != k and GT0[i][j] == 1 and (GT0[i][k] == 1)]
                pairs.append(p)
            return pairs
        PAIRS = _expert_pairs()
        B, P, D, H = (64, 64, 192, 768)

        def _gelu(t):
            return jax.nn.gelu(t, approximate=False)
        key = jax.random.key(seed)
        ks = jax.random.split(key, 8)
        s = 0.02
        x = jax.random.normal(ks[0], (B, NCLS + P, D), dtype=jnp.float32)
        mids = jax.random.randint(ks[1], (B,), 0, 6)
        moe0_W1 = jax.random.normal(ks[2], (D, H), dtype=jnp.float32) * s
        moe0_b1 = jnp.zeros((H,), jnp.float32)
        moe0_W2 = jax.random.normal(ks[3], (H, D), dtype=jnp.float32) * s
        moe0_b2 = jnp.zeros((D,), jnp.float32)
        A1_W = jax.random.normal(ks[4], (5, D, H), dtype=jnp.float32) * s
        A1_b = jnp.zeros((5, H), jnp.float32)
        A2_W = jax.random.normal(ks[5], (5, H, D), dtype=jnp.float32) * s
        A2_b = jnp.zeros((5, D), jnp.float32)
        G_W = jax.random.normal(ks[6], (NCLS, D, 2), dtype=jnp.float32) * s
        return {'x': x, 'moe0_W1': moe0_W1, 'moe0_b1': moe0_b1, 'moe0_W2': moe0_W2, 'moe0_b2': moe0_b2, 'A1_W': A1_W, 'A1_b': A1_b, 'A2_W': A2_W, 'A2_b': A2_b, 'G_W': G_W, 'mids': mids}
    _L0_ffn_all = _L0_ffn_setup()
    _L0_ffn_in = {k: v for k, v in _L0_ffn_all.items() if k in ('moe0_W1', 'moe0_b1', 'moe0_W2', 'moe0_b2', 'A1_W', 'A1_b', 'A2_W', 'A2_b', 'G_W', 'mids')}
    del _L0_ffn_all
    return {'x': x, 'cls_tok': cls_tok, 'L0_tok_pl_w': _L0_tok_in['pl_w'], 'L0_tok_pl_b': _L0_tok_in['pl_b'], 'L0_tok_pl_dw': _L0_tok_in['pl_dw'], 'L0_tok_pl_pw': _L0_tok_in['pl_pw'], 'L0_tok_pl_pwb': _L0_tok_in['pl_pwb'], 'L0_tok_pg_w1': _L0_tok_in['pg_w1'], 'L0_tok_pg_b1': _L0_tok_in['pg_b1'], 'L0_tok_pg_dw': _L0_tok_in['pg_dw'], 'L0_tok_pg_pw': _L0_tok_in['pg_pw'], 'L0_tok_pg_pwb': _L0_tok_in['pg_pwb'], 'L0_tok_pg_w2': _L0_tok_in['pg_w2'], 'L0_tok_pg_b2': _L0_tok_in['pg_b2'], 'L0_tok_alpha': _L0_tok_in['alpha'], 'L0_tok_f1_dw': _L0_tok_in['f1_dw'], 'L0_tok_f1_pw': _L0_tok_in['f1_pw'], 'L0_tok_f1_pwb': _L0_tok_in['f1_pwb'], 'L0_tok_f2_dw': _L0_tok_in['f2_dw'], 'L0_tok_f2_pw': _L0_tok_in['f2_pw'], 'L0_tok_f2_pwb': _L0_tok_in['f2_pwb'], 'L0_tok_f3_dw': _L0_tok_in['f3_dw'], 'L0_tok_f3_pw': _L0_tok_in['f3_pw'], 'L0_tok_f3_pwb': _L0_tok_in['f3_pwb'], 'L0_tok_ln_g': _L0_tok_in['ln_g'], 'L0_tok_ln_b': _L0_tok_in['ln_b'], 'L0_tok_cls': _L0_tok_in['cls'], 'L0_attn_w_qkv': _L0_attn_in['w_qkv'], 'L0_attn_w_out': _L0_attn_in['w_out'], 'L0_ffn_moe0_W1': _L0_ffn_in['moe0_W1'], 'L0_ffn_moe0_b1': _L0_ffn_in['moe0_b1'], 'L0_ffn_moe0_W2': _L0_ffn_in['moe0_W2'], 'L0_ffn_moe0_b2': _L0_ffn_in['moe0_b2'], 'L0_ffn_A1_W': _L0_ffn_in['A1_W'], 'L0_ffn_A1_b': _L0_ffn_in['A1_b'], 'L0_ffn_A2_W': _L0_ffn_in['A2_W'], 'L0_ffn_A2_b': _L0_ffn_in['A2_b'], 'L0_ffn_G_W': _L0_ffn_in['G_W'], 'L0_ffn_mids': _L0_ffn_in['mids']}

def reference(x, cls_tok, L0_tok_pl_w, L0_tok_pl_b, L0_tok_pl_dw, L0_tok_pl_pw, L0_tok_pl_pwb, L0_tok_pg_w1, L0_tok_pg_b1, L0_tok_pg_dw, L0_tok_pg_pw, L0_tok_pg_pwb, L0_tok_pg_w2, L0_tok_pg_b2, L0_tok_alpha, L0_tok_f1_dw, L0_tok_f1_pw, L0_tok_f1_pwb, L0_tok_f2_dw, L0_tok_f2_pw, L0_tok_f2_pwb, L0_tok_f3_dw, L0_tok_f3_pw, L0_tok_f3_pwb, L0_tok_ln_g, L0_tok_ln_b, L0_tok_cls, L0_attn_w_qkv, L0_attn_w_out, L0_ffn_moe0_W1, L0_ffn_moe0_b1, L0_ffn_moe0_W2, L0_ffn_moe0_b2, L0_ffn_A1_W, L0_ffn_A1_b, L0_ffn_A2_W, L0_ffn_A2_b, L0_ffn_G_W, L0_ffn_mids):
    import jax
    import jax.numpy as jnp

    def _L0_tok_ref(x, pl_w, pl_b, pl_dw, pl_pw, pl_pwb, pg_w1, pg_b1, pg_dw, pg_pw, pg_pwb, pg_w2, pg_b2, alpha, f1_dw, f1_pw, f1_pwb, f2_dw, f2_pw, f2_pwb, f3_dw, f3_pw, f3_pwb, ln_g, ln_b, cls):
        import jax, jax.numpy as jnp
        import numpy as np
        B, IN, IMG = (64, 3, 224)
        PATCH, LEVELS, D = (16, 4, 192)
        ISQ2 = 0.7071067811865476
        DN = ('NCHW', 'OIHW', 'NCHW')

        def conv(x, w, b=None, stride=1, pad=((0, 0), (0, 0)), groups=1):
            y = jax.lax.conv_general_dilated(x, w, (stride, stride), pad, dimension_numbers=DN, feature_group_count=groups)
            return y if b is None else y + b[None, :, None, None]

        def dwconv(x, wd, wp, bp):
            y = conv(x, wd, pad=((1, 1), (1, 1)), groups=x.shape[1])
            return conv(y, wp, bp)

        def haar_dwt2(x):
            xe, xo = (x[..., ::2], x[..., 1::2])
            lo_w, hi_w = ((xe + xo) * ISQ2, (xe - xo) * ISQ2)

            def split_h(t):
                te, to = (t[..., ::2, :], t[..., 1::2, :])
                return ((te + to) * ISQ2, (te - to) * ISQ2)
            ll, lh = split_h(lo_w)
            hl, hh = split_h(hi_w)
            return (ll, lh, hl, hh)

        def wavelet_packet(x):
            f = x
            for _ in range(LEVELS):
                b, k, h, w = f.shape
                ll, lh, hl, hh = haar_dwt2(f)
                bands = jnp.stack([ll, lh, hl, hh], axis=1)
                bands = bands.reshape(b, 4, k // IN, IN, h // 2, w // 2)
                f = jnp.transpose(bands, (0, 2, 1, 3, 4, 5)).reshape(b, 4 * k, h // 2, w // 2)
            return f

        def gelu(x):
            return jax.nn.gelu(x, approximate=False)

        def forward(x, pl_w, pl_b, pl_dw, pl_pw, pl_pwb, pg_w1, pg_b1, pg_dw, pg_pw, pg_pwb, pg_w2, pg_b2, alpha, f1_dw, f1_pw, f1_pwb, f2_dw, f2_pw, f2_pwb, f3_dw, f3_pw, f3_pwb, ln_g, ln_b, cls):
            loc = conv(x, pl_w, pl_b, stride=PATCH)
            loc = dwconv(gelu(loc), pl_dw, pl_pw, pl_pwb)
            g = wavelet_packet(x)
            g = gelu(conv(g, pg_w1, pg_b1))
            g = gelu(dwconv(g, pg_dw, pg_pw, pg_pwb))
            glob = conv(g, pg_w2, pg_b2)
            gate = 0.5 * (jnp.tanh(alpha) + 1.0)
            h = (1.0 - gate) * loc + gate * glob
            h = jax.nn.relu(dwconv(h, f1_dw, f1_pw, f1_pwb))
            h = jax.nn.relu(dwconv(h, f2_dw, f2_pw, f2_pwb))
            h = dwconv(loc + h, f3_dw, f3_pw, f3_pwb)
            t = jnp.transpose(h.reshape(h.shape[0], D, -1), (0, 2, 1))
            mu = jnp.mean(t, -1, keepdims=True)
            var = jnp.mean((t - mu) ** 2, -1, keepdims=True)
            t = (t - mu) / jnp.sqrt(var + 1e-05) * ln_g + ln_b
            cls_tok = jnp.broadcast_to(cls, (t.shape[0], 1, D))
            return jnp.concatenate([cls_tok, t], axis=1)
        return forward(x, pl_w, pl_b, pl_dw, pl_pw, pl_pwb, pg_w1, pg_b1, pg_dw, pg_pw, pg_pwb, pg_w2, pg_b2, alpha, f1_dw, f1_pw, f1_pwb, f2_dw, f2_pw, f2_pwb, f3_dw, f3_pw, f3_pwb, ln_g, ln_b, cls)

    def _L0_attn_ref(x, w_qkv, w_out):
        import jax, jax.numpy as jnp
        import numpy as np
        N_HEADS = 12
        B, S, W = x.shape
        H = N_HEADS
        D = W // H
        scale = W ** (-0.5)
        qkv = x @ w_qkv
        q, k, v = jnp.split(qkv, 3, axis=2)
        q = q.reshape(B, S, H, D)
        k = k.reshape(B, S, H, D)
        attn_score = jnp.einsum('binh,bjnh->bijn', q, k) * scale
        attn_weight = jax.nn.softmax(attn_score, axis=2)
        out = jnp.einsum('bijn,bjnh->binh', attn_weight, k)
        out = out.reshape(B, S, W)
        return out @ w_out

    def _L0_ffn_ref(x, moe0_W1, moe0_b1, moe0_W2, moe0_b2, A1_W, A1_b, A2_W, A2_b, G_W, mids):
        import jax, jax.numpy as jnp
        import numpy as np
        GT0 = [[0, 1, 0, 0, 1, 0], [0, 1, 0, 0, 0, 1], [0, 0, 1, 0, 1, 0], [0, 0, 1, 0, 0, 1], [0, 0, 0, 1, 1, 0], [0, 0, 0, 1, 0, 1]]
        NCLS = 6
        K = 1

        def _expert_pairs():
            pairs = []
            for i in range(NCLS):
                p = [(j - 1, k - 1) for j in range(1, 6) for k in range(1, 6) if j != k and GT0[i][j] == 1 and (GT0[i][k] == 1)]
                pairs.append(p)
            return pairs
        PAIRS = _expert_pairs()
        B, P, D, H = (64, 64, 192, 768)

        def _gelu(t):
            return jax.nn.gelu(t, approximate=False)
        cls_tokens = x[:, :NCLS]
        patch_tokens = x[:, NCLS:]
        patch_out = _gelu(patch_tokens @ moe0_W1 + moe0_b1) @ moe0_W2 + moe0_b2
        cls_outs = []
        for i in range(NCLS):
            tok = cls_tokens[:, i]
            eouts = [_gelu(tok @ A1_W[a] + A1_b[a]) @ A2_W[c] + A2_b[c] for a, c in PAIRS[i]]
            out = jnp.stack(eouts, axis=-1)
            gate = jax.nn.softmax(tok @ G_W[i], axis=-1)
            thr = jnp.sort(gate, axis=-1)[..., -(K + 1)]
            mask = (gate > thr[..., None]).astype(gate.dtype)
            g = gate * mask
            g = g / jnp.clip(jnp.sum(g, axis=-1, keepdims=True), 1e-06)
            cls_outs.append(jnp.sum(out * g[:, None, :], axis=-1))
        cls_out = jnp.stack(cls_outs, axis=1)
        return jnp.concatenate([cls_out, patch_out], axis=1)
    h = _L0_tok_ref(x, L0_tok_pl_w, L0_tok_pl_b, L0_tok_pl_dw, L0_tok_pl_pw, L0_tok_pl_pwb, L0_tok_pg_w1, L0_tok_pg_b1, L0_tok_pg_dw, L0_tok_pg_pw, L0_tok_pg_pwb, L0_tok_pg_w2, L0_tok_pg_b2, L0_tok_alpha, L0_tok_f1_dw, L0_tok_f1_pw, L0_tok_f1_pwb, L0_tok_f2_dw, L0_tok_f2_pw, L0_tok_f2_pwb, L0_tok_f3_dw, L0_tok_f3_pw, L0_tok_f3_pwb, L0_tok_ln_g, L0_tok_ln_b, L0_tok_cls)
    h = jnp.concatenate([jnp.broadcast_to(cls_tok, (h.shape[0], 1, h.shape[2])), h], axis=1)
    h = h + _L0_attn_ref(_layernorm(h, axis=-1), L0_attn_w_qkv, L0_attn_w_out)
    h = h + _L0_ffn_ref(_layernorm(h, axis=-1), L0_ffn_moe0_W1, L0_ffn_moe0_b1, L0_ffn_moe0_W2, L0_ffn_moe0_b2, L0_ffn_A1_W, L0_ffn_A1_b, L0_ffn_A2_W, L0_ffn_A2_b, L0_ffn_G_W, L0_ffn_mids)
    return h

_drawn_inputs = setup_inputs


def setup_inputs(seed=0):
    import zlib

    import numpy as np

    out = dict(_drawn_inputs(seed))
    spreads = {'L0_tok_alpha': (0.0, 0.8),
     'L0_tok_ln_g': (1.0, 0.2),
     'L0_tok_ln_b': (0.0, 0.1),
     'L0_ffn_moe0_b1': (0.0, 0.382),
     'L0_ffn_moe0_b2': (0.0, 0.1),
     'L0_ffn_A1_b': (0.0, 0.8),
     'L0_ffn_A2_b': (0.0, 0.332)}
    factors = {'x': 8.0,
     'cls_tok': 3.916,
     'L0_tok_pl_w': 8.0,
     'L0_tok_pl_b': 64.0,
     'L0_tok_pl_dw': 8.0,
     'L0_tok_pl_pw': 8.0,
     'L0_tok_pl_pwb': 35.36,
     'L0_tok_pg_w1': 8.0,
     'L0_tok_pg_b1': 64.0,
     'L0_tok_pg_dw': 8.0,
     'L0_tok_pg_pw': 8.0,
     'L0_tok_pg_pwb': 64.0,
     'L0_tok_pg_w2': 8.0,
     'L0_tok_pg_b2': 64.0,
     'L0_tok_f1_dw': 8.0,
     'L0_tok_f1_pw': 8.0,
     'L0_tok_f1_pwb': 64.0,
     'L0_tok_f2_dw': 8.0,
     'L0_tok_f2_pw': 8.0,
     'L0_tok_f2_pwb': 56.256,
     'L0_tok_f3_dw': 2.745,
     'L0_tok_f3_pw': 3.407,
     'L0_tok_cls': 4.256,
     'L0_ffn_A1_W': 2.97,
     'L0_ffn_A2_W': 2.901,
     'L0_ffn_G_W': 4.568}
    for name, (base, spread) in spreads.items():
        noise = np.random.default_rng([zlib.crc32(name.encode()), seed]).standard_normal(out[name].shape)
        drawn = base * np.exp(spread * noise) if base else spread * noise
        out[name] = jnp.asarray(drawn.astype(out[name].dtype))
    for name, factor in factors.items():
        out[name] = (out[name] * factor).astype(out[name].dtype)
    return out
```

```python
from contextlib import ExitStack

import numpy as np

import concourse.bass as bass
from concourse import mybir
from concourse.alu_op_type import AluOpType as ALU

F32 = mybir.dt.float32
ACT = mybir.ActivationFunctionType
AXX = mybir.AxisListType.X

B, CIN, IMG, PATCH, D = 32, 3, 112, 16, 192
G = IMG // PATCH
NTOK = G * G
S = NTOK + 2
PIX = PATCH * PATCH
KPIX = CIN * PIX
KC = KPIX // 128
DA, DB = 128, D - 128
NCH, CI = 4, 8
CT = NTOK * CI
NPAIR = NCH // 2
HD = D // 2
NH, DH = 12, 16
HP = NH // 2
NG, GI = 8, 4
NT = B // 2
ROWS = 64
NMAIN = S - 6
HID = 768
HC = HID // 128
NCLS, NEXP = 6, 5
SCALE = float(D) ** -0.5
EPS = 1e-5

VEC = {}
for _name in ("bias_loc", "bias_g", "bias_mixed", "alpha_A", "alpha_P", "plb_A", "plb_P", "pgb_A", "pgb_P",
              "b2_A", "b2_P", "f1b_A", "f1b_P", "f2b_A", "f2b_P"):
    VEC[_name] = (len(VEC), 1)
_at = len(VEC)
for _name in ("dw_loc", "dw_g", "dw_mixed", "f1_A", "f1_P", "f2_A", "f2_P", "f3_A", "f3_P"):
    VEC[_name] = (_at, 9)
    _at += 9
VEC["moe_b1"] = (_at, HC)
VEC["exp_b1"] = (_at + HC, NEXP * HC)
NVEC = _at + HC + NEXP * HC
LAYERS = ("loc", "g", "w2", "f1", "f2", "f3")
LW = 2 * D + 128


def vit_tower(nc, x, plw, w1k, had, pww, vec, bcw, cst, wqk, wout, mw1, mw2, a1, a2, gw, out_main, out_cls, h2x):
    ctx = ExitStack()
    with ctx:
        def sb(name, cols, parts=128):
            return ctx.enter_context(nc.sbuf_tensor(name, [parts, cols], F32))

        def sem(name):
            return ctx.enter_context(nc.semaphore(name))

        xreg = sb("xreg", NCH * KC * CT)
        wereg = sb("wereg", 2 * GI * HP * S)
        hadreg = sb("hadreg", CIN * 2 * D + 2 * PIX)
        gelreg = sb("gelreg", 2 * NCH * CT)
        dwreg = sb("dwreg", 2 * NCH * CT)
        mixreg = sb("mixreg", 2 * NCH * CT)
        locreg = sb("locreg", 12 * CT)
        g2reg = sb("g2reg", 6 * CT)
        cureg = sb("cureg", 6 * CT)
        tapreg = sb("tapreg", 6 * CT)
        A2 = sb("A2", HC * NEXP * D)
        MW1 = sb("MW1", 2 * HID, HD)
        MW2 = sb("MW2", HC * D)
        WQK = sb("WQK", 2 * 2 * D, HD)
        WOUT = sb("WOUT", 2 * D, HD)
        PW = sb("PW", len(LAYERS) * LW)
        V = sb("V", NVEC)
        BC = sb("BC", 7 * D)
        CST = sb("CST", 128 + HP + 1)
        GW = sb("GW", 2 * NCLS * 2, HD)

        X = xreg[:, :].rearrange("p (c k n) -> p c k n", c=NCH, k=KC)
        WE = wereg[:, 0:KC * 2 * D].rearrange("p (k n) -> p k n", k=KC)
        W1K = hadreg[:, 0:CIN * 2 * D].rearrange("p (h c o) -> p h c o", h=2, c=CIN)
        HAD = hadreg[:, CIN * 2 * D:CIN * 2 * D + 2 * PIX].rearrange("p (h x) -> p h x", h=2)
        GA = gelreg[:, :].rearrange("p (b c n) -> p b c n", b=2, c=NCH)
        DWA = dwreg[:, :].rearrange("p (b c n) -> p b c n", b=2, c=NCH)
        GM = mixreg[:, 0:NCH * CT].rearrange("p (c n) -> p c n", c=NCH)
        DWM = mixreg[:, NCH * CT:2 * NCH * CT].rearrange("p (c n) -> p c n", c=NCH)

        def six(reg, i=0):
            return reg[:, i * 6 * CT:(i + 1) * 6 * CT].rearrange("p (u n) -> p u n", u=6)

        LOC, LM = six(locreg, 0), six(locreg, 1)
        G2, CUR, TAP = six(g2reg), six(cureg), six(tapreg)
        D3A = mixreg[:, 0:B * ROWS]
        D3P = mixreg[:, B * ROWS:B * ROWS + B // 2 * ROWS]
        A1 = xreg[0:HD, 0:2 * NEXP * HID].rearrange("p (k e n) -> p k e n", k=2, e=NEXP)
        o = 2 * NEXP * HID
        T3B, XN, XN2, Y = (xreg[:, o + i * 2 * D:o + (i + 1) * 2 * D] for i in range(4))
        BD = wereg[0:HD, :].rearrange("p (k i h j) -> p k i h j", k=2, i=GI, h=HP)
        QT = hadreg[0:HD, 0:2 * GI * ROWS].rearrange("p (k i j) -> p k i j", k=2, i=GI)
        KT2 = hadreg[0:HD, 2 * GI * ROWS:6 * GI * ROWS].rearrange("p (m d j) -> p m d j", m=2 * GI, d=2)
        T3 = gelreg[:, 0:NT * D]
        H = dwreg[:, 0:NT * D]
        H2 = mixreg[:, 0:NT * D]
        H2B = locreg[:, 0:NT * D]
        HE = [g2reg[:, i * HC * 2 * HD:(i + 1) * HC * 2 * HD].rearrange("p (c r n) -> p c r n", c=HC, r=2)
              for i in range(2)]
        HIDT = cureg[:, 0:HC * GI * ROWS].rearrange("p (c i j) -> p c i j", c=HC, i=GI)
        KV = cureg[:, HC * GI * ROWS:HC * GI * ROWS + GI * 2 * HP * 17].rearrange("p (i h d) -> p i h d", i=GI, d=17)
        P = tapreg[:, 0:2 * NH * ROWS].rearrange("p (u h j) -> p u h j", u=2, h=NH)
        PT = tapreg[:, 2 * NH * ROWS:2 * NH * ROWS + HP * 128].rearrange("p (a i) -> p a i", a=HP)
        XT = sb("XT", 2 * GI * S, HD)
        X2T = sb("X2T", 2 * GI * ROWS, HD)
        TOK = sb("TOK", 2 * 2 * 3 * B, HD)
        OTOK = sb("OTOK", D)
        OT = sb("OT", 2 * 128, HD)
        HC2 = sb("HC2", 2 * D, 96)
        EU = sb("EU", 4 * D, 96)
        ER = sb("ER", 4 * D, 96)
        GT = sb("GT", 64, 96)
        ST = sb("ST", 3 * 2 * 6)
        MV = sb("MV", 3 * 2 * 2)
        VE = sb("VE", 3 * 2)
        RS = sb("RS", 4 * 2)
        MX = sb("MX", 2 * NH)
        RD = sb("RD", NH)
        TH = sb("TH", 10)
        NEG = sb("NEG", 1)
        TOKv = TOK[:, :].rearrange("p (k r a n) -> p k r a n", k=2, r=2, a=3)
        IDN = CST[:, 0:128]
        HMASK = CST[0:HD, 128:128 + HP]
        PMASK = CST[:, 128 + HP:128 + HP + 1]
        BF3, LNG, LNB, MB2, EB3, EB4, EBK = (BC[:, i * D:(i + 1) * D] for i in range(7))

        def v(name, i=0):
            return V[:, VEC[name][0] + i:VEC[name][0] + i + 1]

        PSUM = ctx.enter_context(nc.psum_tensor("PSUM", [128, 8, 512], F32))

        ld_had, ld_plw, ld_x, ld_vec, ld_cst, ld_bc, ld_pw = (
            sem("ld_had"), sem("ld_plw"), [sem(f"ld_x{c}") for c in range(NCH)], sem("ld_vec"), sem("ld_cst"),
            sem("ld_bc"), sem("ld_pw"))
        ld_attn, ld_moe, ld_a1, ld_a2, ld_gw = sem("ld_attn"), sem("ld_moe"), sem("ld_a1"), sem("ld_a2"), sem("ld_gw")
        acc_done = sem("acc_done")
        acc_read = sem("acc_read")
        centre = sem("centre")
        tap = sem("tap")
        fused = sem("fused")
        tanh_done, gate_step = sem("tanh_done"), sem("gate_step")
        d3_zero, d3_ready, t3_ready = sem("d3_zero"), sem("d3_ready"), sem("t3_ready")
        consts = sem("consts")
        passed = sem("passed")
        pads_zero = sem("pads_zero")
        biased, scaled, h_ready, norm3 = sem("biased"), sem("scaled"), sem("h_ready"), sem("norm3")
        stats = [sem(f"stats{i}") for i in range(3)]
        meanvar = [sem(f"meanvar{i}") for i in range(3)]
        var_eps = [sem(f"var_eps{i}") for i in range(3)]
        rstd = [sem(f"rstd{i}") for i in range(3)]
        rstd_masked = sem("rstd_masked")
        xn_ready, xn2_ready = sem("xn_ready"), sem("xn2_ready")
        t1_done, xt_ready, q_done, q_ready, k_done, k_ready = (
            sem("t1_done"), sem("xt_ready"), sem("q_done"), sem("q_ready"), sem("k_done"), sem("k_ready"))
        bd_ready, kt_done, kv_ready, s_done, smax, d_ready, p_ready = (
            sem("bd_ready"), sem("kt_done"), sem("kv_ready"), sem("s_done"), sem("smax"), sem("d_ready"), sem("p_ready"))
        pt_done, pt_lo, pt_hi, av_done, rden, o_ready = (
            sem("pt_done"), sem("pt_lo"), sem("pt_hi"), sem("av_done"), sem("rden"), sem("o_ready"))
        ot_done, ot_ready, proj_done, h2_ready, h2b_ready = (
            sem("ot_done"), sem("ot_ready"), sem("proj_done"), sem("h2_ready"), sem("h2b_ready"))
        t2_done, x2_ready, tok_ready = sem("t2_done"), sem("x2_ready"), sem("tok_ready")
        f1_done, gelu_done, f2_done, y_ready, y_stored = (
            sem("f1_done"), sem("gelu_done"), sem("f2_done"), sem("y_ready"), sem("y_stored"))
        h2x_stored, hc_loaded, gate_done, gate_max, gate_exp, gate_dve = (
            sem("h2x_stored"), sem("hc_loaded"), sem("gate_done"), sem("gate_max"), sem("gate_exp"), sem("gate_dve"))
        e1_done, e1_read, e2_done, e_mix, cls_stored = (
            sem("e1_done"), sem("e1_read"), sem("e2_done"), sem("e_mix"), sem("cls_stored"))
        block = ctx.enter_context(nc.Block())

        STEPS = [("w", 0), ("e", 0), ("e", 1), ("e", 2), ("loc", 0), ("g", 0), ("w2", 0), ("e", 3), ("f1", 0),
                 ("loc", 1), ("g", 1), ("w2", 1), ("f2", 0), ("f1", 1), ("f3", 0), ("f2", 1), ("f3", 1)]
        UNITS = {"w": 4, "e": 3, "loc": 3, "g": 3, "w2": 3, "f1": 3, "f2": 3, "f3": 4}
        first_unit, _n = {}, 0
        for st in STEPS:
            first_unit[st] = _n
            _n += UNITS[st[0]]
        NUNITS = _n
        DW = [("dw", 0), ("dw", 1), ("dw", 2), ("f1", 0), ("dw", 3), ("f2", 0), ("f3", 0), ("f1", 1), ("f2", 1), ("f3", 1)]
        dw_at = {b: i for i, b in enumerate(DW)}
        NTAPS = 24

        def taps_done(b):
            return NTAPS * (dw_at[b] + 1)

        def batch_units(b):
            kind, i = b
            if kind == "dw":
                return [(GA[:, 0, i, :], DWA[:, 0, i, :], "dw_loc"), (GA[:, 1, i, :], DWA[:, 1, i, :], "dw_g"),
                        (GM[:, i, :], DWM[:, i, :], "dw_mixed")]
            return [(CUR[:, u, :], TAP[:, u, :], kind + ("_P" if u >= 4 else "_A")) for u in (2 * i, 2 * i + 1, 4 + i)]

        def units_of_pair(i):
            return (2 * i, 2 * i + 1, 4 + i)

        def bank(n, cols, parts=slice(0, 128)):
            return PSUM[parts, n % 8, 0:cols]

        def times(g, k, c=0):
            return k * g + c

        def wait(eng, s, value):
            if not isinstance(value, int) or value > 0:
                eng.wait_ge(s, value)

        @block.sync
        def _(sp):
            sp.dma_start(HAD, had).then_inc(ld_had, 16)
            sp.dma_start(W1K, w1k).then_inc(ld_had, 16)
            sp.dma_start(WE[:, :, 0:DA], plw[:, :, 0:DA]).then_inc(ld_plw, 16)
            sp.dma_start(WE[:, :, 2 * DA:2 * DA + DB], plw[:, :, DA:D]).then_inc(ld_plw, 16)
            sp.dma_start(X[:, 0, :, :], x[:, 0, :, :]).then_inc(ld_x[0], 16)
            sp.dma_start(V[:, :], vec).then_inc(ld_vec, 16)
            for c in range(1, NCH):
                sp.dma_start(X[:, c, :, :], x[:, c, :, :]).then_inc(ld_x[c], 16)
            sp.dma_start(PW[:, :], pww).then_inc(ld_pw, 16)
            sp.dma_start(CST[:, :], cst).then_inc(ld_cst, 16)
            sp.dma_start(BC[:, :], bcw).then_inc(ld_bc, 16)
            sp.dma_start(WQK[:, :], wqk).then_inc(ld_attn, 16)
            sp.dma_start(WOUT[:, :], wout).then_inc(ld_attn, 16)
            sp.dma_start(MW1[:, :], mw1).then_inc(ld_moe, 16)
            sp.dma_start(MW2[:, :], mw2).then_inc(ld_moe, 16)
            sp.dma_start(A2[:, :], a2).then_inc(ld_a2, 16)
            sp.dma_start(GW[:, :], gw).then_inc(ld_gw, 16)
            sp.wait_ge(acc_done, first_unit[("e", NCH - 1)] + 3)
            sp.dma_start(A1[:, :, :, :], a1).then_inc(ld_a1, 16)

            def store(g):
                wait(sp, y_ready, times(g, 1, 1))
                sp.dma_start(out_main[:, bass.ds(times(g, 2 * D), 2 * D)], Y).then_inc(y_stored, 16)

            with sp.Fori(0, NG - 1) as g:
                store(g)
            sp.wait_ge(h2_ready, NT)
            for e in range(2):
                sp.dma_start(h2x[:, e, :, :], H2[ROWS * e + NMAIN:ROWS * e + S, :].rearrange("p (t c) -> p t c", c=D)).then_inc(h2x_stored, 16)
            sp.wait_ge(h2x_stored, 32)
            for a in range(3):
                for r in range(2):
                    row = (2 * a + r - 2) % NCLS
                    sp.dma_start(HC2[B * a:B * a + B, r * D:(r + 1) * D], h2x[row, :, :, :].rearrange("e t c -> (e t) c")).then_inc(hc_loaded, 16)
            store(NG - 1)
            sp.wait_ge(e_mix, 8)
            sp.dma_start(out_cls, ER[:, 2 * D:4 * D]).then_inc(cls_stored, 16)
            sp.wait_ge(cls_stored, 16)
            sp.wait_ge(y_stored, 16 * NG)

        @block.tensor
        def _(pe):
            def mm(out, lhsT, rhs, start, stop):
                return nc.tensor.matmul(out, lhsT, rhs, start=start, stop=stop)

            def free_bank(n):
                if n >= 8:
                    pe.wait_ge(acc_read, n - 7)

            def haar_weights():
                pe.wait_ge(ld_had, 32)
                for j, (m, c0, nco) in enumerate(((0, 0, 2), (0, 2, 1), (1, 0, 2), (1, 2, 1))):
                    for h in range(2):
                        last = mm(bank(j, nco * D), HAD[:, h, m * 128:(m + 1) * 128],
                                  W1K[:, h, c0:c0 + nco, :], h == 0, h == 1)
                    last.then_inc(acc_done, 1)

            def embed(c):
                n = first_unit[("e", c)]
                pe.wait_ge(ld_x[c], 16)
                if c == 0:
                    pe.wait_ge(ld_plw, 32)
                for j, w0 in enumerate((0, DA, 2 * DA)):
                    if c == 0 and j == 1:
                        pe.wait_ge(acc_read, 4)
                    free_bank(n + j)
                    for k in range(KC):
                        last = mm(bank(n + j, CT), WE[:, k, w0:w0 + 128], X[:, c, k, :], k == 0, k == KC - 1)
                    last.then_inc(acc_done, 1)

            def pointwise(layer, i):
                w = LAYERS.index(layer) * LW
                wa, wb, wd = PW[:, w:w + D], PW[:, w + D:w + 2 * D], PW[:, w + 2 * D:w + 2 * D + 128]
                n = first_unit[(layer, i)]
                if layer in ("loc", "g"):
                    pe.wait_ge(tap, taps_done(("dw", 2 * i + 1)))
                    b = ("loc", "g").index(layer)
                    half = slice(DB * b, DB * b + DB)
                    a_in = [DWA[:, b, 2 * i + j, :] for j in range(2)]
                    b_in = [(half, DWM[half, 2 * i + j, :]) for j in range(2)]
                else:
                    if layer == "w2":
                        pe.wait_ge(acc_read, first_unit[("g", i)] + 3)
                        src = G2
                    else:
                        pe.wait_ge(tap, taps_done((layer, i)))
                        src = TAP
                    a_in = [src[:, 2 * i + j, :] for j in range(2)]
                    b_in = [(slice(DB * j, DB * j + DB), src[DB * j:DB * j + DB, 4 + i, :]) for j in range(2)]
                for j in range(2):
                    free_bank(n + j)
                    half, rhs = b_in[j]
                    mm(bank(n + j, CT), wa[:, 0:DA], a_in[j], True, False)
                    mm(bank(n + j, CT), wb[half, 0:DA], rhs, False, True).then_inc(acc_done, 1)
                free_bank(n + 2)
                outs = [PSUM[DB * j:DB * j + DB, (n + 2) % 8, 0:CT] for j in range(2)]
                if layer in ("loc", "g"):
                    for j in range(2):
                        mm(outs[j], wa[:, DA:D], a_in[j], True, False)
                    for j in range(2):
                        half, rhs = b_in[j]
                        last = mm(outs[j], wb[half, DA:D], rhs, False, True)
                else:
                    mm(bank(n + 2, CT), wd, src[:, 4 + i, :], True, False)
                    for j in range(2):
                        last = mm(outs[j], wa[:, DA:D], a_in[j], False, True)
                last.then_inc(acc_done, 1)

            def f3_tiles(i):
                w = LAYERS.index("f3") * LW
                wa, wb = PW[:, w:w + D], PW[:, w + D:w + 2 * D]
                n = first_unit[("f3", i)]
                for q in range(4):
                    free_bank(n + q)
                    pe.wait_ge(d3_ready, 2 * i + q // 2 + 1)
                    for u in range(2):
                        t = 8 * i + 2 * q + u
                        half = slice(DB * (q // 2), DB * (q // 2) + DB)
                        at = (8 * i + 2 * (t % 4)) * ROWS
                        out = PSUM[:, (n + q) % 8, u * D:(u + 1) * D]
                        mm(out, D3A[:, 2 * t * ROWS:(2 * t + 2) * ROWS], wa, True, False)
                        last = mm(out, D3P[half, at:at + 2 * ROWS], wb[half, :], False, True)
                    last.then_inc(acc_done, 1)

            for kind, i in STEPS:
                if kind == "w":
                    haar_weights()
                elif kind == "e":
                    embed(i)
                elif kind == "f3":
                    f3_tiles(i)
                else:
                    if (kind, i) == ("loc", 0):
                        pe.wait_ge(ld_pw, 16)
                    pointwise(kind, i)

            def halves(n, cols):
                return PSUM[0:HD, n, 0:2 * cols].rearrange("p (k n) -> p k n", k=2)

            def transpose_in(src, n):
                out = halves(n, 2 * 128)
                for u in range(2):
                    for k in range(2):
                        last = nc.tensor.transpose(out[:, k, u * 128:(u + 1) * 128],
                                                   src[:, u * D + k * HD:u * D + (k + 1) * HD], IDN)
                return last

            def t1(g):
                wait(pe, xn_ready, times(g, 2, 2))
                wait(pe, ot_ready, times(g, 2))
                transpose_in(XN, 0).then_inc(t1_done, 1)

            def t2(g):
                wait(pe, xn2_ready, times(g, 2, 2))
                transpose_in(XN2, 1).then_inc(t2_done, 1)

            def qk(g):
                wait(pe, xt_ready, times(g, 1, 1))
                for which, n, done in ((0, 0, q_done), (1, 1, k_done)):
                    if which == 1:
                        wait(pe, x2_ready, times(g, 1))
                    out = halves(n, GI * S)
                    for m in range(2):
                        for k in range(2):
                            last = mm(out[:, m, :], WQK[:, (k * 4 + which * 2 + m) * HD:(k * 4 + which * 2 + m + 1) * HD],
                                      XT[:, k * GI * S:(k + 1) * GI * S], k == 0, k == 1)
                    last.then_inc(done, 1)

            def kt(g):
                wait(pe, q_ready, times(g, 1, 1))
                wait(pe, k_ready, times(g, 1, 1))
                for n in range(2):
                    for i in range(2):
                        for k in range(2):
                            last = nc.tensor.transpose(PSUM[:, n, i * D + k * HD:i * D + (k + 1) * HD],
                                                       KT2[:, k * GI + 2 * n + i, :, :], IDN[0:HD, 0:HD])
                    last.then_inc(kt_done, 1)

            def scores(g, u):
                wait(pe, d_ready, times(g, 2, u))
                if u == 0:
                    wait(pe, bd_ready, times(g, 1, 1))
                for k in range(2):
                    for e in range(2):
                        last = mm(PSUM[ROWS * e:ROWS * e + ROWS, 2 + k, 0:HP * S], QT[:, k, 2 * u + e, :],
                                  BD[:, k, 2 * u + e, :, :], True, True)
                last.then_inc(s_done, 1)

            def transpose_probs(g, u):
                wait(pe, p_ready, times(g, 2, u + 1))
                wait(pe, pt_lo, times(g, 2, u))
                wait(pe, pt_hi, times(g, 2, u))
                for a in range(HP):
                    last = nc.tensor.transpose(PSUM[:, 4 + a // 3, (a % 3) * 128:(a % 3 + 1) * 128],
                                               P[:, u, 2 * a:2 * a + 2, :], IDN)
                last.then_inc(pt_done, 1)

            def attend(g, u):
                wait(pe, pt_lo, times(g, 2, u + 1))
                wait(pe, pt_hi, times(g, 2, u + 1))
                if u == 0:
                    wait(pe, kv_ready, times(g, 2, 2))
                else:
                    wait(pe, o_ready, times(g, 2, 1))
                for a in range(HP):
                    for e in range(2):
                        last = mm(PSUM[ROWS * e:ROWS * e + ROWS, 0, a * 34:(a + 1) * 34],
                                  PT[:, a, ROWS * e:ROWS * e + ROWS], KV[:, 2 * u + e, 2 * a:2 * a + 2, :], True, True)
                last.then_inc(av_done, 1)

            def transpose_out(g, u):
                wait(pe, o_ready, times(g, 2, u + 1))
                n = 1 - u
                for k in range(2):
                    last = nc.tensor.transpose(PSUM[0:HD, n, k * 128:(k + 1) * 128], OTOK[:, k * HD:(k + 1) * HD], IDN)
                last.then_inc(ot_done, 1)

            def project(g, u):
                wait(pe, ot_ready, times(g, 2, u + 1))
                if u == 1:
                    wait(pe, h2_ready, times(g, 2, 1))
                for k in range(2):
                    last = mm(PSUM[:, 1, 0:D], OT[:, k * 128:(k + 1) * 128], WOUT[:, k * D:(k + 1) * D], k == 0, k == 1)
                last.then_inc(proj_done, 1)

            def ffn_up(g, j):
                if j == 0:
                    wait(pe, x2_ready, times(g, 1, 1))
                    wait(pe, gelu_done, times(g, 3))
                elif j == 1:
                    wait(pe, y_ready, times(g, 1))
                else:
                    wait(pe, gelu_done, times(g, 3, 1))
                x2 = X2T[:, :].rearrange("p (k i j) -> p k i j", k=2, i=GI)
                for c in (2 * j, 2 * j + 1):
                    for k in range(2):
                        last = mm(PSUM[:, 6 + j % 2, (c % 2) * GI * NMAIN:(c % 2 + 1) * GI * NMAIN],
                                  MW1[:, k * HID + c * 128:k * HID + (c + 1) * 128], x2[:, k, :, 0:NMAIN],
                                  k == 0, k == 1)
                last.then_inc(f1_done, 1)

            def ffn_down(g, u):
                if u == 0:
                    wait(pe, gelu_done, times(g, 3, 3))
                for c in range(HC):
                    last = mm(PSUM[:, 7, u * D:(u + 1) * D], HIDT[:, c, 2 * u:2 * u + 2, :],
                              MW2[:, c * D:(c + 1) * D], c == 0, c == HC - 1)
                if u == 1:
                    last.then_inc(f2_done, 1)

            def body(g, ffn):
                t1(g)
                if ffn:
                    t2(g - 1)
                qk(g)
                if ffn:
                    ffn_up(g - 1, 0)
                kt(g)
                if ffn:
                    ffn_up(g - 1, 1)
                scores(g, 0)
                if ffn:
                    ffn_up(g - 1, 2)
                scores(g, 1)
                if ffn:
                    ffn_down(g - 1, 0)
                transpose_probs(g, 0)
                if ffn:
                    ffn_down(g - 1, 1)
                attend(g, 0)
                transpose_probs(g, 1)
                transpose_out(g, 0)
                attend(g, 1)
                project(g, 0)
                transpose_out(g, 1)
                project(g, 1)

            pe.wait_ge(ld_cst, 16)
            pe.wait_ge(ld_attn, 32)
            pe.wait_ge(ld_moe, 32)
            pe.wait_ge(acc_read, NUNITS)
            pe.wait_ge(pads_zero, 2)
            body(0, False)
            body(1, True)
            with pe.Fori(2, NG) as g:
                body(g, True)
            t2(NG - 1)

            pe.wait_ge(tok_ready, NG)
            pe.wait_ge(ld_gw, 16)
            gwv = GW[:, :].rearrange("p (k r a n) -> p k r a n", k=2, r=2, a=3)
            for r in range(2):
                for a in range(3):
                    for k in range(2):
                        last = mm(PSUM[B * a:B * a + B, 0, 2 * r:2 * r + 2], TOKv[:, k, r, a, :], gwv[:, k, r, a, :],
                                  k == 0, k == 1)
            last.then_inc(gate_done, 1)
            for j in range(3):
                ffn_up(NG - 1, j)
            pe.wait_ge(ld_a1, 16)
            for n, (a, c0, c1) in enumerate(((0, 0, 6), (1, 0, 6), (2, 0, 6), (3, 0, 3), (3, 3, 6), (4, 0, 3), (4, 3, 6))):
                w = 64 if a < 3 else 96
                nb = 1 + n if n < 5 else n - 4
                if n >= 5:
                    pe.wait_ge(e1_read, n - 4)
                for c in range(c0, c1):
                    for k in range(2):
                        rhs = TOKv[:, k, :, a, :] if a < 3 else TOKv[:, k, a - 3, :, :]
                        last = mm(PSUM[:, nb, (c - c0) * w:(c - c0 + 1) * w],
                                  A1[:, k, a, c * 128:(c + 1) * 128], rhs, k == 0, k == 1)
                last.then_inc(e1_done, 1)
                if n == 2:
                    ffn_down(NG - 1, 0)
                    ffn_down(NG - 1, 1)
            pe.wait_ge(ld_a2, 16)
            pe.wait_ge(e1_read, 3)
            a2v = A2[:, :].rearrange("p (c e n) -> p c e n", c=HC, e=NEXP)
            pe.wait_ge(gate_max, 1)
            for r in range(2):
                for c in range(HC):
                    last = mm(PSUM[0:96, 0, r * D:(r + 1) * D], HE[0][:, c, r, :], a2v[:, c, 3 + r, :], c == 0, c == HC - 1)
            last.then_inc(e2_done, 1)
            pe.wait_ge(e1_read, 7)
            for r in range(2):
                for c in range(HC):
                    for a in range(3):
                        last = mm(PSUM[B * a:B * a + B, 3, r * D:(r + 1) * D], HE[1][:, c, r, B * a:B * a + B],
                                  a2v[:, c, a, :], c == 0, c == HC - 1)
            last.then_inc(e2_done, 1)

        @block.scalar
        def _(act):
            def read(n, done=1):
                act.wait_ge(acc_done, n + 1)

            def centre_taps(b):
                for src, dst, f in batch_units(b):
                    nc.scalar.activation(dst, src, ACT.Copy, scale=v(f, 4)).then_inc(centre, 1)

            def haar_evict():
                for j, (m, c0, nco) in enumerate(((0, 0, 2), (0, 2, 1), (1, 0, 2), (1, 2, 1))):
                    read(j)
                    src = bank(j, nco * D).rearrange("p (c o) -> p c o", o=D)
                    dst = WE[:, 2 * c0 + m:2 * (c0 + nco - 1) + m + 1:2, :]
                    nc.scalar.activation(dst[:, :, DA:2 * DA], src[:, :, 0:DA], ACT.Copy)
                    nc.scalar.activation(dst[:, :, 2 * DA + DB:], src[:, :, DA:D], ACT.Copy).then_inc(acc_read, 1)

            def embed_evict(c):
                n = first_unit[("e", c)]
                for j, (dst, bias) in enumerate(((GA[:, 0, c, :], "bias_loc"), (GA[:, 1, c, :], "bias_g"),
                                                 (GM[:, c, :], "bias_mixed"))):
                    read(n + j)
                    nc.scalar.activation(dst, bank(n + j, CT), ACT.Gelu, bias=v(bias)).then_inc(acc_read, 1)
                act.wait_ge(acc_read, n + 3)
                centre_taps(("dw", c))

            def pointwise_evict(layer, i):
                n = first_unit[(layer, i)]
                for j, u in enumerate(units_of_pair(i)):
                    part = "_P" if j == 2 else "_A"
                    p = (j == 2)
                    read(n + j)
                    src = bank(n + j, CT)
                    if layer == "loc":
                        nc.scalar.activation(LOC[:, u, :], src, ACT.Identity, bias=v("plb" + part))
                        if i == 0 and j == 0:
                            act.wait_ge(gate_step, 8)
                        nc.scalar.activation(LM[:, u, :], src, ACT.Identity, bias=TH[:, 8 + p:9 + p],
                                             scale=TH[:, 4 + p:5 + p]).then_inc(acc_read, 1)
                    elif layer == "g":
                        nc.scalar.activation(G2[:, u, :], src, ACT.Gelu, bias=v("pgb" + part)).then_inc(acc_read, 1)
                    elif layer == "w2":
                        nc.scalar.activation(CUR[:, u, :], src, ACT.Copy, scale=TH[:, 2 + p:3 + p]).then_inc(acc_read, 1)
                    else:
                        nc.scalar.activation(CUR[:, u, :], src, ACT.Relu, bias=v(layer + "b" + part)).then_inc(acc_read, 1)

            nfused = {("w2", 0): 3, ("w2", 1): 6, ("f2", 0): 9, ("f2", 1): 12}

            def d3(i):
                act.wait_ge(tap, taps_done(("f3", i)))
                act.wait_ge(d3_zero, 1)
                for j in range(2):
                    c = 2 * i + j
                    todo = [(TAP[:, c, :], D3A[:, c * CI * ROWS:(c + 1) * CI * ROWS])]
                    if j == 0:
                        todo.append((TAP[:, 4 + i, :], D3P[:, i * CI * ROWS:(i + 1) * CI * ROWS]))
                    for src, dst in todo:
                        s = src.rearrange("p (t i) -> p i t", i=CI)
                        d = dst.rearrange("p (i r) -> p i r", r=ROWS)
                        nc.scalar.activation(d[:, :, 0:NMAIN], s[:, :, 4:NTOK], ACT.Copy)
                        last = nc.scalar.activation(d[:, :, NMAIN:NTOK], s[:, :, 0:4], ACT.Copy)
                    last.then_inc(d3_ready, 1)

            def f3_evict(i):
                n = first_unit[("f3", i)]
                for q in range(4):
                    read(n + q)
                    nc.scalar.activation(T3[:, (4 * i + q) * 2 * D:(4 * i + q + 1) * 2 * D], bank(n + q, 2 * D),
                                         ACT.Copy).then_inc(acc_read, 1)

            act.wait_ge(ld_vec, 16)
            a0 = VEC["alpha_A"][0]
            nc.scalar.activation(TH[:, 0:2], V[:, a0:a0 + 2], ACT.Tanh).then_inc(tanh_done, 1)
            act.wait_ge(ld_plw, 32)
            haar_evict()
            embed_evict(0)
            embed_evict(1)
            embed_evict(2)
            pointwise_evict("loc", 0)
            pointwise_evict("g", 0)
            pointwise_evict("w2", 0)
            act.wait_ge(fused, nfused[("w2", 0)])
            centre_taps(("f1", 0))
            embed_evict(3)
            pointwise_evict("f1", 0)
            act.wait_ge(acc_read, first_unit[("f1", 0)] + 3)
            centre_taps(("f2", 0))
            pointwise_evict("loc", 1)
            pointwise_evict("g", 1)
            pointwise_evict("w2", 1)
            pointwise_evict("f2", 0)
            act.wait_ge(fused, nfused[("f2", 0)])
            centre_taps(("f3", 0))
            act.wait_ge(fused, nfused[("f2", 0)])
            centre_taps(("f1", 1))
            pointwise_evict("f1", 1)
            act.wait_ge(acc_read, first_unit[("f1", 1)] + 3)
            centre_taps(("f2", 1))
            d3(0)
            f3_evict(0)
            pointwise_evict("f2", 1)
            act.wait_ge(fused, nfused[("f2", 1)])
            centre_taps(("f3", 1))
            d3(1)
            f3_evict(1)

            def halves(n, cols):
                return PSUM[0:HD, n, 0:2 * cols].rearrange("p (k n) -> p k n", k=2)

            def xt(g):
                wait(act, t1_done, times(g, 1, 1))
                src = PSUM[0:HD, 0, :].rearrange("p (m j) -> p m j", j=ROWS)
                wait(act, k_done, times(g, 1))
                nc.scalar.activation(XT[:, :].rearrange("p (m j) -> p m j", j=S), src[:, :, 0:S], ACT.Copy).then_inc(xt_ready, 1)

            def x2t(g):
                wait(act, t2_done, times(g, 1, 1))
                wait(act, tok_ready, times(g, 1))
                wait(act, f1_done, times(g, 3))
                nc.scalar.activation(X2T[:, :], PSUM[0:HD, 1, :], ACT.Copy).then_inc(x2_ready, 1)

            def qkt(g):
                wait(act, q_done, times(g, 1, 1))
                wait(act, s_done, times(g, 2))
                nc.scalar.activation(QT[:, :, :, 0:S].rearrange("p k i j -> p (k i) j"),
                                     PSUM[0:HD, 0, 0:2 * GI * S].rearrange("p (m j) -> p m j", j=S), ACT.Copy).then_inc(q_ready, 1)
                wait(act, k_done, times(g, 1, 1))
                wait(act, kt_done, times(g, 2))
                wait(act, bd_ready, times(g, 1))
                src = PSUM[0:HD, 1, 0:2 * GI * S].rearrange("p (m o j) -> p m o j", o=1, j=S)
                nc.scalar.activation(KT2[:, :, :, 0:S], src.to_broadcast([HD, 2 * GI, 2, S]), ACT.Copy).then_inc(k_ready, 1)

            def kv(g):
                for n in range(2):
                    wait(act, kt_done, times(g, 2, n + 1))
                    wait(act, av_done, times(g, 2))
                    for r in range(2):
                        half = slice(ROWS * r, ROWS * r + ROWS)
                        for i in range(2):
                            src = PSUM[half, n, i * D:(i + 1) * D].rearrange("p (a d) -> p a d", d=2 * DH)
                            dst = KV[half, 2 * n + i, r:NH:2, 0:DH]
                            last = nc.scalar.activation(dst, src[:, :, r * DH:(r + 1) * DH], ACT.Copy)
                    last.then_inc(kv_ready, 1)

            def exps(g, u):
                wait(act, d_ready, times(g, 2, u + 1))
                nc.scalar.activation(P[:, u, :, 0:S], P[:, u, :, 0:S], ACT.Exp, scale=SCALE).then_inc(p_ready, 1)

            def probs_lo(g, u):
                wait(act, pt_done, times(g, 2, u + 1))
                wait(act, av_done, times(g, 2, u))
                nc.scalar.activation(PT[:, 0:3, :].rearrange("p a i -> p (a i)"), PSUM[:, 4, 0:384], ACT.Copy).then_inc(pt_lo, 1)

            def ot(g, u):
                wait(act, ot_done, times(g, 2, u + 1))
                wait(act, proj_done, times(g, 2, u))
                nc.scalar.activation(OT[:, :], PSUM[0:HD, 1 - u, 0:256], ACT.Copy).then_inc(ot_ready, 1)

            def gelus(g, j):
                wait(act, f1_done, times(g, 3, j + 1))
                wait(act, f2_done, times(g, 1))
                for c in (2 * j, 2 * j + 1):
                    src = PSUM[:, 6 + j % 2, (c % 2) * GI * NMAIN:(c % 2 + 1) * GI * NMAIN].rearrange("p (i j) -> p i j", j=NMAIN)
                    last = nc.scalar.activation(HIDT[:, c, :, 0:NMAIN], src, ACT.Gelu, bias=v("moe_b1", c))
                last.then_inc(gelu_done, 1)

            def body(g, ffn):
                xt(g)
                if ffn:
                    x2t(g - 1)
                qkt(g)
                if ffn:
                    gelus(g - 1, 0)
                kv(g)
                if ffn:
                    gelus(g - 1, 1)
                    gelus(g - 1, 2)
                exps(g, 0)
                exps(g, 1)
                probs_lo(g, 0)
                probs_lo(g, 1)
                ot(g, 0)
                ot(g, 1)

            act.wait_ge(pads_zero, 2)
            body(0, False)
            body(1, True)
            with act.Fori(2, NG) as g:
                body(g, True)
            x2t(NG - 1)
            act.wait_ge(gate_max, 2)
            nc.scalar.activation(GT[:, 4:8], GT[:, 4:8], ACT.Exp).then_inc(gate_exp, 1)
            for j in range(3):
                gelus(NG - 1, j)
            for n, (a, c0, c1) in enumerate(((0, 0, 6), (1, 0, 6), (2, 0, 6), (3, 0, 3), (3, 3, 6), (4, 0, 3), (4, 3, 6))):
                act.wait_ge(e1_done, n + 1)
                nb = 1 + n if n < 5 else n - 4
                w = 64 if a < 3 else 96
                for c in range(c0, c1):
                    src = PSUM[:, nb, (c - c0) * w:(c - c0 + 1) * w]
                    if a < 3:
                        src = src.rearrange("p (r n) -> p r n", r=2)
                        dst = HE[0][:, c, :, B * a:B * a + B]
                    else:
                        dst = HE[1][:, c, a - 3, :]
                    last = nc.scalar.activation(dst, src, ACT.Gelu, bias=v("exp_b1", a * HC + c))
                last.then_inc(e1_read, 1)

        @block.vector
        def _(dve):
            steps = [0]

            def step(ins):
                steps[0] += 1
                ins.then_inc(gate_step, 1)
                dve.wait_ge(gate_step, steps[0])

            dve.wait_ge(tanh_done, 1)
            dve.wait_ge(ld_vec, 16)
            p0, q0 = VEC["plb_A"][0], VEC["b2_A"][0]
            step(nc.vector.tensor_scalar(TH[:, 2:4], TH[:, 0:2], 1.0, 0.5, ALU.add, ALU.mult))
            step(nc.vector.tensor_scalar(TH[:, 4:6], TH[:, 2:4], -1.0, 1.0, ALU.mult, ALU.add))
            step(nc.vector.tensor_tensor(TH[:, 6:8], TH[:, 2:4], V[:, q0:q0 + 2], ALU.mult))
            step(nc.vector.tensor_tensor(TH[:, 8:10], TH[:, 4:6], V[:, p0:p0 + 2], ALU.mult))
            step(nc.vector.tensor_tensor(TH[:, 8:10], TH[:, 8:10], TH[:, 6:8], ALU.add))
            step(nc.vector.memset(NEG[:, :], -0.5))
            step(nc.vector.tensor_copy(TH[:, 0:2], TH[:, 2:4]))
            step(nc.vector.tensor_copy(TH[:, 6:8], TH[:, 4:6]))

            SHIFTS = [(dy, dx) for dy in (-1, 0, 1) for dx in (-1, 0, 1) if (dy, dx) != (0, 0)]

            def shifted(ap, dy, dx, inp):
                ys = slice(max(0, dy), G + min(0, dy)) if inp else slice(max(0, -dy), G - max(0, dy))
                lo = max(0, dx) if inp else max(0, -dx)
                n = G - abs(dx)
                return ap.rearrange("p (y x) -> p y x", y=G)[:, ys, lo * CI:(lo + n) * CI]

            def taps(b):
                k = dw_at[b]
                dve.wait_ge(centre, 3 * (k + 1))
                for j, (dy, dx) in enumerate(SHIFTS):
                    for i, (src, dst, f) in enumerate(batch_units(b)):
                        if j:
                            dve.wait_ge(tap, NTAPS * k + 3 * (j - 1) + i + 1)
                        acc = shifted(dst, dy, dx, False)
                        nc.vector.scalar_tensor_tensor(out=acc, in0=shifted(src, dy, dx, True),
                                                       scalar=v(f, (dy + 1) * 3 + dx + 1), in1=acc,
                                                       op0=ALU.mult, op1=ALU.add).then_inc(tap, 1)

            def fuse(layer, i, other):
                n = first_unit[(layer, i)]
                for j, u in enumerate(units_of_pair(i)):
                    dve.wait_ge(acc_read, n + j + 1)
                    nc.vector.tensor_tensor(CUR[:, u, :], CUR[:, u, :], other[:, u, :], ALU.add).then_inc(fused, 1)

            taps(("dw", 0))
            taps(("dw", 1))
            taps(("dw", 2))
            fuse("w2", 0, LM)
            taps(("f1", 0))
            taps(("dw", 3))
            taps(("f2", 0))
            fuse("w2", 1, LM)
            fuse("f2", 0, LOC)
            taps(("f3", 0))
            taps(("f1", 1))
            taps(("f2", 1))
            fuse("f2", 1, LOC)
            taps(("f3", 1))

            def wait_bn(s, value):
                wait(dve, s, value)
                if not isinstance(value, int):
                    dve.sem_inc(passed, 1)

            def statistics(i, src, u):
                nc.vector.bn_stats(ST[:, (2 * i + u) * 6:(2 * i + u + 1) * 6], src).then_inc(stats[i], 1)

            def aggregate(i, u):
                return nc.vector.bn_aggr(MV[:, (2 * i + u) * 2:(2 * i + u + 1) * 2], ST[:, (2 * i + u) * 6:(2 * i + u + 1) * 6])

            def add_eps(i, u0, n):
                var = MV[:, (2 * i + u0) * 2:(2 * i + u0 + n) * 2].rearrange("p (u m) -> p u m", m=2)[:, :, 1]
                return nc.vector.tensor_scalar(VE[:, 2 * i + u0:2 * i + u0 + n], var, EPS, None, ALU.add)

            def mean(i, u):
                return MV[:, (2 * i + u) * 2:(2 * i + u) * 2 + 1]

            def tokens(g):
                wait(dve, acc_read, NUNITS)
                t3 = T3[:, bass.ds(times(g, 2 * D), 2 * D)].rearrange("p (u c) -> p u c", u=2)
                b3 = T3B.rearrange("p (u c) -> p u c", u=2)

                def both(row):
                    return row.rearrange("p (o c) -> p o c", o=1).to_broadcast([128, 2, D])

                nc.vector.tensor_tensor(b3, t3, both(BF3), ALU.add).then_inc(biased, 1)
                wait(dve, biased, times(g, 1, 1))
                for u in range(2):
                    statistics(0, T3B[:, u * D:(u + 1) * D], u)
                for u in range(2):
                    wait_bn(stats[0], times(g, 2, u + 1))
                    aggregate(0, u).then_inc(meanvar[0], 1)
                wait(dve, meanvar[0], times(g, 2, 2))
                add_eps(0, 0, 2).then_inc(var_eps[0], 1)
                wait(dve, rstd_masked, times(g, 1, 1))
                for u in range(2):
                    nc.vector.tensor_scalar(T3B[:, u * D:(u + 1) * D], T3B[:, u * D:(u + 1) * D], mean(0, u),
                                            RS[:, 6 + u:7 + u], ALU.subtract, ALU.mult).then_inc(norm3, 1)
                wait(dve, norm3, times(g, 2, 2))
                nc.vector.tensor_tensor(b3, b3, both(LNG), ALU.mult).then_inc(scaled, 1)
                wait(dve, scaled, times(g, 1, 1))
                h = H[:, bass.ds(times(g, 2 * D), 2 * D)]
                nc.vector.tensor_tensor(h.rearrange("p (u c) -> p u c", u=2), b3, both(LNB), ALU.add).then_inc(h_ready, 1)
                wait_bn(h_ready, times(g, 1, 1))
                for u in range(2):
                    statistics(1, H[:, bass.ds(times(g, 2 * D, u * D), D)], u)
                for u in range(2):
                    wait_bn(stats[1], times(g, 2, u + 1))
                    aggregate(1, u).then_inc(meanvar[1], 1)
                wait(dve, meanvar[1], times(g, 2, 2))
                add_eps(1, 0, 2).then_inc(var_eps[1], 1)
                wait(dve, rstd[1], times(g, 1, 1))
                wait(dve, t1_done, times(g, 1))
                for u in range(2):
                    nc.vector.tensor_scalar(XN[:, u * D:(u + 1) * D], H[:, bass.ds(times(g, 2 * D, u * D), D)], mean(1, u),
                                            RS[:, 2 + u:3 + u], ALU.subtract, ALU.mult).then_inc(xn_ready, 1)

            def block_diagonal(g):
                wait(dve, k_ready, times(g, 1, 1))
                wait(dve, s_done, times(g, 2))
                for k in range(2):
                    for h in range(HP):
                        last = nc.vector.tensor_scalar(BD[:, k, :, h, :], KT2[:, k * GI:(k + 1) * GI, 0, 0:S],
                                                       HMASK[:, h:h + 1], None, ALU.mult)
                last.then_inc(bd_ready, 1)

            def minus_max(g, u):
                wait(dve, s_done, times(g, 2, u + 1))
                s = PSUM[:, 2:4, 0:HP * S].rearrange("p k (h j) -> p k h j", j=S)
                mx = MX[:, u * NH:(u + 1) * NH].rearrange("p (k h) -> p k h", k=2)
                nc.vector.tensor_reduce(mx, s, AXX, ALU.max).then_inc(smax, 1)
                wait(dve, smax, times(g, 2, u + 1))
                wait(dve, pt_done, times(g, 2, u - 1))
                for k in range(2):
                    m = mx[:, k, :].rearrange("p (h o) -> p h o", o=1).to_broadcast([128, HP, S])
                    last = nc.vector.tensor_tensor(P[:, u, k * HP:(k + 1) * HP, 0:S], s[:, k, :, :], m, ALU.subtract)
                last.then_inc(d_ready, 1)

            def probs_hi(g, u):
                wait(dve, pt_done, times(g, 2, u + 1))
                wait(dve, av_done, times(g, 2, u))
                nc.vector.tensor_copy(PT[:, 3:6, :].rearrange("p a i -> p (a i)"), PSUM[:, 5, 0:384]).then_inc(pt_hi, 1)

            def normalise(g, u):
                wait(dve, av_done, times(g, 2, u + 1))
                av = PSUM[:, 0, 0:NH * 17].rearrange("p (h d) -> p h d", d=17)
                nc.vector.reciprocal(RD[:, :], av[:, :, DH]).then_inc(rden, 1)
                wait(dve, rden, times(g, 2, u + 1))
                wait(dve, ot_done, times(g, 2, u))
                r = RD[:, :].rearrange("p (h o) -> p h o", o=1).to_broadcast([128, NH, DH])
                nc.vector.tensor_tensor(OTOK[:, :].rearrange("p (h d) -> p h d", d=DH), av[:, :, 0:DH], r, ALU.mult).then_inc(o_ready, 1)

            def residual(g, u):
                wait(dve, proj_done, times(g, 2, u + 1))
                at = bass.ds(times(g, 2 * D, u * D), D)
                nc.vector.tensor_tensor(H2[:, at], PSUM[:, 1, 0:D], H[:, at], ALU.add).then_inc(h2_ready, 1)
                wait_bn(h2_ready, times(g, 2, u + 1))
                statistics(2, H2[:, at], u)
                wait_bn(stats[2], times(g, 2, u + 1))
                aggregate(2, u).then_inc(meanvar[2], 1)
                wait(dve, meanvar[2], times(g, 2, u + 1))
                add_eps(2, u, 1).then_inc(var_eps[2], 1)

            def norm2(g, u):
                wait(dve, rstd[2], times(g, 2, u + 1))
                wait(dve, t2_done, times(g, 1))
                at = bass.ds(times(g, 2 * D, u * D), D)
                nc.vector.tensor_scalar(XN2[:, u * D:(u + 1) * D], H2[:, at], mean(2, u), RS[:, 4 + u:5 + u],
                                        ALU.subtract, ALU.mult).then_inc(xn2_ready, 1)

            def ffn_out(g):
                wait(dve, f2_done, times(g, 1, 1))
                wait(dve, h2b_ready, times(g, 1, 1))
                wait(dve, y_stored, times(g, 16))
                nc.vector.tensor_tensor(Y, PSUM[:, 7, 0:2 * D], H2B[:, bass.ds(times(g, 2 * D), 2 * D)], ALU.add).then_inc(y_ready, 1)

            def body(g, ffn, ahead):
                block_diagonal(g)
                minus_max(g, 0)
                minus_max(g, 1)
                probs_hi(g, 0)
                if ffn:
                    ffn_out(g - 1)
                normalise(g, 0)
                probs_hi(g, 1)
                normalise(g, 1)
                residual(g, 0)
                residual(g, 1)
                norm2(g, 0)
                norm2(g, 1)
                if ahead:
                    tokens(g + 1)

            dve.wait_ge(ld_bc, 16)
            dve.wait_ge(ld_cst, 16)
            tokens(0)
            dve.wait_ge(pads_zero, 2)
            body(0, False, True)
            body(1, True, True)
            with dve.Fori(2, NG - 1) as g:
                body(g, True, True)
            body(NG - 1, True, False)

            dve.wait_ge(gate_done, 1)
            lg = PSUM[0:96, 0, 0:4].rearrange("p (r n) -> p r n", r=2)

            def pairs(at):
                return GT[:, at:at + 4].rearrange("p (r n) -> p r n", r=2)

            def one(at):
                return GT[:, at:at + 2].rearrange("p (r o) -> p r o", o=1).to_broadcast([96, 2, 2])

            nc.vector.tensor_reduce(GT[:, 0:2], lg, AXX, ALU.max).then_inc(gate_dve, 1)
            dve.wait_ge(gate_dve, 1)
            nc.vector.tensor_tensor(pairs(4), lg, one(0), ALU.subtract).then_inc(gate_max, 2)
            dve.wait_ge(gate_exp, 1)
            chain = [1]

            def link(ins):
                chain[0] += 1
                ins.then_inc(gate_dve, 1)
                dve.wait_ge(gate_dve, chain[0])

            link(nc.vector.tensor_reduce(GT[:, 8:10], pairs(4), AXX, ALU.add))
            link(nc.vector.reciprocal(GT[:, 10:12], GT[:, 8:10]))
            link(nc.vector.tensor_tensor(pairs(12), pairs(4), one(10), ALU.mult))
            link(nc.vector.tensor_reduce(GT[:, 16:18], pairs(12), AXX, ALU.min))
            link(nc.vector.tensor_tensor(pairs(20), pairs(12), one(16), ALU.is_gt))
            link(nc.vector.tensor_tensor(pairs(24), pairs(20), pairs(12), ALU.mult))
            link(nc.vector.tensor_reduce(GT[:, 28:30], pairs(24), AXX, ALU.add))
            link(nc.vector.tensor_scalar(GT[:, 30:32], GT[:, 28:30], 1e-6, None, ALU.max))
            link(nc.vector.reciprocal(GT[:, 32:34], GT[:, 30:32]))
            link(nc.vector.tensor_tensor(pairs(36), pairs(24), one(32), ALU.mult))
            ffn_out(NG - 1)
            dve.wait_ge(e2_done, 2)
            dve.wait_ge(hc_loaded, 16 * NCLS)
            for r in range(2):
                cols = slice(r * D, (r + 1) * D)
                nc.vector.tensor_tensor(EU[:, cols], PSUM[0:96, 0, cols], (EB3, EB4)[r][0:96, :], ALU.add).then_inc(e_mix, 1)
                nc.vector.tensor_tensor(EU[:, 2 * D + r * D:2 * D + (r + 1) * D], PSUM[0:96, 3, cols], EBK[0:96, :], ALU.add).then_inc(e_mix, 1)
            for r in range(2):
                cols = slice(r * D, (r + 1) * D)
                dve.wait_ge(e_mix, 4)
                nc.vector.scalar_tensor_tensor(out=ER[:, cols], in0=EU[:, cols], scalar=GT[:, 36 + 2 * r:37 + 2 * r],
                                               in1=HC2[:, cols], op0=ALU.mult, op1=ALU.add).then_inc(e_mix, 1)
            for r in range(2):
                cols = slice(r * D, (r + 1) * D)
                dve.wait_ge(e_mix, 5 + r)
                nc.vector.scalar_tensor_tensor(out=ER[:, 2 * D + r * D:2 * D + (r + 1) * D], in0=EU[:, 2 * D + r * D:2 * D + (r + 1) * D],
                                               scalar=GT[:, 37 + 2 * r:38 + 2 * r], in1=ER[:, cols],
                                               op0=ALU.mult, op1=ALU.add).then_inc(e_mix, 1)

        @block.gpsimd
        def _(gp):
            gp.wait_ge(acc_done, first_unit[("g", 1)] + 3)
            gp.memset(mixreg[:, 0:(B + B // 2) * ROWS], 0.0).then_inc(d3_zero, 1)
            gp.wait_ge(acc_done, NUNITS)
            gp.memset(QT[:, :, :, S:ROWS], 0.0)
            gp.memset(KT2[:, :, :, S:ROWS], 0.0)
            gp.memset(P[:, :, :, S:ROWS], 0.0)
            gp.memset(HIDT[:, :, :, NMAIN:ROWS], 0.0)
            gp.memset(KV, 0.0).then_inc(consts, 1)
            gp.wait_ge(consts, 1)
            for r in range(2):
                gp.memset(KV[ROWS * r:ROWS * r + ROWS, :, r:NH:2, DH:DH + 1], 1.0).then_inc(pads_zero, 1)
                gp.wait_ge(pads_zero, r + 1)

            def power(i, at, n):
                return gp.tensor_tensor(RS[:, at:at + n], VE[:, 2 * i + at % 2:2 * i + at % 2 + n],
                                        NEG[:, :].to_broadcast([128, n]), ALU.pow)

            def norms(g):
                wait(gp, var_eps[0], times(g, 1, 1))
                power(0, 0, 2).then_inc(rstd[0], 1)
                wait(gp, rstd[0], times(g, 1, 1))
                gp.tensor_tensor(RS[:, 6:8], RS[:, 0:2], PMASK.to_broadcast([128, 2]), ALU.mult).then_inc(rstd_masked, 1)
                wait(gp, var_eps[1], times(g, 1, 1))
                power(1, 2, 2).then_inc(rstd[1], 1)

            def norm2(g):
                for u in range(2):
                    wait(gp, var_eps[2], times(g, 2, u + 1))
                    gp.tensor_tensor(RS[:, 4 + u:5 + u], VE[:, 4 + u:5 + u], NEG[:, :], ALU.pow).then_inc(rstd[2], 1)
                at = bass.ds(times(g, 2 * D), 2 * D)
                gp.tensor_tensor(H2B[:, at].rearrange("p (u c) -> p u c", u=2), H2[:, at].rearrange("p (u c) -> p u c", u=2),
                                 MB2.rearrange("p (o c) -> p o c", o=1).to_broadcast([128, 2, D]), ALU.add).then_inc(h2b_ready, 1)

            def class_tokens(g):
                wait(gp, x2_ready, times(g, 1, 1))
                x2 = X2T[:, :].rearrange("p (k u e j) -> p k u e j", k=2, u=2, e=2)
                for k in range(2):
                    for r in range(2):
                        for e in range(2):
                            dst = TOKv[:, k, r, :, bass.ds(times(g, 2, 16 * e), 2)]
                            gp.tensor_copy(dst[:, 1:3, :], x2[:, k, :, e, NMAIN + r:NMAIN + 4:2].rearrange("p u a -> p a u"))
                            last = gp.tensor_copy(dst[:, 0, :], x2[:, k, :, e, NTOK + r])
                last.then_inc(tok_ready, 1)

            gp.wait_ge(ld_cst, 16)
            gp.wait_ge(ld_bc, 16)
            gp.wait_ge(gate_step, 6)
            norms(0)

            def body(g, ffn, ahead):
                if ffn:
                    class_tokens(g - 1)
                norm2(g)
                if ahead:
                    norms(g + 1)

            body(0, False, True)
            with gp.Fori(1, NG - 1) as g:
                body(g, True, True)
            body(NG - 1, True, False)
            class_tokens(NG - 1)


def _haar():
    y, x = np.meshgrid(np.arange(PATCH), np.arange(PATCH), indexing="ij")
    m = np.ones((PIX, PATCH, PATCH), np.float32)
    for band in range(PIX):
        for level in range(4):
            d = (band >> (2 * (3 - level))) & 3
            if d & 2:
                m[band] *= 1 - 2 * ((x >> level) & 1)
            if d & 1:
                m[band] *= 1 - 2 * ((y >> level) & 1)
    return (m / 16.0).reshape(PIX, PIX).astype(np.float32)


def kernel(**inputs):
    import concourse.bacc as bacc
    from concourse.bass_utils import run_bass_kernel_spmd as run

    a = {k: np.asarray(w) for k, w in inputs.items()}
    t = {k[len("L0_tok_"):]: w for k, w in a.items() if k.startswith("L0_tok_")}
    f = {k[len("L0_ffn_"):]: w for k, w in a.items() if k.startswith("L0_ffn_")}
    z = np.zeros
    f32 = np.float32

    def rows(m, k):
        return m.reshape(k, m.shape[0] // k, -1).transpose(1, 0, 2)

    x = a["x"].reshape(NCH, CI, CIN, G, PATCH, G, PATCH).transpose(2, 4, 6, 0, 3, 5, 1)
    x = x.reshape(KC, 128, NCH, CT).transpose(1, 2, 0, 3)
    plw = rows(t["pl_w"].reshape(D, KPIX).T, KC)
    w1k = t["pg_w1"].reshape(D, PIX, CIN).transpose(1, 2, 0).reshape(2, 128, CIN, D).transpose(1, 0, 2, 3)
    had = rows(_haar(), 2)
    blocks = []
    for name in ("pl_pw", "pg_pw", "pg_w2", "f1_pw", "f2_pw", "f3_pw"):
        w = t[name].reshape(D, D).T
        bd = z((128, 128), f32)
        bd[:DB, :DB] = w[DA:, DA:]
        bd[DB:, DB:] = w[DA:, DA:]
        blocks += [w[:DA], np.concatenate([w[DA:], w[DA:]]), bd]
    pww = np.concatenate(blocks, 1)

    def part_a(w):
        return w.reshape(D, -1)[:DA]

    def part_p(w):
        return np.concatenate([w.reshape(D, -1)[DA:]] * 2)

    def mixed(p, q):
        return np.concatenate([p.reshape(D, -1)[DA:], q.reshape(D, -1)[DA:]])

    vec = np.concatenate([
        part_a(t["pl_b"]), part_a(t["pg_b1"]), mixed(t["pl_b"], t["pg_b1"]), part_a(t["alpha"]), part_p(t["alpha"]),
        part_a(t["pl_pwb"]), part_p(t["pl_pwb"]), part_a(t["pg_pwb"]), part_p(t["pg_pwb"]),
        part_a(t["pg_b2"]), part_p(t["pg_b2"]), part_a(t["f1_pwb"]), part_p(t["f1_pwb"]),
        part_a(t["f2_pwb"]), part_p(t["f2_pwb"]),
        part_a(t["pl_dw"]), part_a(t["pg_dw"]), mixed(t["pl_dw"], t["pg_dw"]),
        part_a(t["f1_dw"]), part_p(t["f1_dw"]), part_a(t["f2_dw"]), part_p(t["f2_dw"]),
        part_a(t["f3_dw"]), part_p(t["f3_dw"]),
        f["moe0_b1"].reshape(HC, 128).T, f["A1_b"].reshape(NEXP * HC, 128).T], 1)

    def wide(row, n=128):
        return np.broadcast_to(row.reshape(1, D), (n, D))

    lnb = z((128, D), f32)
    for e in range(2):
        lnb[ROWS * e:ROWS * e + NTOK] = wide(t["ln_b"], NTOK)
        lnb[ROWS * e + NTOK] = a["cls_tok"].reshape(D)
        lnb[ROWS * e + NTOK + 1] = t["cls"].reshape(D)
    ebk = np.concatenate([wide(f["A2_b"][k], B) for k in range(3)] + [z((128 - 3 * B, D), f32)])
    bcw = np.concatenate([wide(t["f3_pwb"]), wide(t["ln_g"]), lnb, wide(f["moe0_b2"]), wide(f["A2_b"][3]),
                          wide(f["A2_b"][4]), ebk], 1)
    cst = z((128, 128 + HP + 1), f32)
    cst[:, :128] = np.eye(128)
    for h in range(HP):
        cst[h * DH:(h + 1) * DH, 128 + h] = 1.0
    for e in range(2):
        cst[ROWS * e:ROWS * e + NTOK, 128 + HP] = 1.0
    wqk = rows(a["L0_attn_w_qkv"][:, :2 * D], 2)
    wout = rows(a["L0_attn_w_out"], 2)
    mw1 = rows(f["moe0_W1"], 2)
    mw2 = rows(f["moe0_W2"], HC)
    a1 = f["A1_W"].reshape(NEXP, 2, HD, HID).transpose(2, 1, 0, 3)
    a2 = f["A2_W"].reshape(NEXP, HC, 128, D).transpose(2, 1, 0, 3)
    gw = f["G_W"].reshape(3, 2, 2, HD, 2).transpose(3, 2, 1, 0, 4)

    arrays = {
        "x": x, "plw": plw, "w1k": w1k, "had": had, "pww": pww, "vec": vec, "bcw": bcw, "cst": cst,
        "wqk": wqk.reshape(HD, -1), "wout": wout.reshape(HD, -1), "mw1": mw1.reshape(HD, -1), "mw2": mw2.reshape(128, -1),
        "a1": a1, "a2": a2.reshape(128, -1), "gw": gw.reshape(HD, -1)}
    arrays = {k: np.ascontiguousarray(w) for k, w in arrays.items()}

    nc = bacc.Bacc("TRN2", target_bir_lowering=False, num_devices=1)
    args = [nc.dram_tensor(k, w.shape, mybir.dt.from_np(w.dtype), kind="ExternalInput").ap() for k, w in arrays.items()]
    args.append(nc.dram_tensor("out_main", (128, NT * D), F32, kind="ExternalOutput").ap())
    args.append(nc.dram_tensor("out_cls", (96, 2 * D), F32, kind="ExternalOutput").ap())
    args.append(nc.dram_tensor("h2x", (NCLS, 2, NT, D), F32, kind="Internal").ap())
    vit_tower(nc, *args)
    r = run(nc, [arrays], core_ids=[0]).results[0]
    main = np.asarray(r["out_main"]).reshape(2, ROWS, NT, D)[:, :NMAIN].transpose(2, 0, 1, 3).reshape(B, NMAIN, D)
    cls = np.asarray(r["out_cls"]).reshape(3, 2, NT, 2, D).transpose(2, 1, 0, 3, 4).reshape(B, NCLS, D)
    return np.concatenate([cls, main], 1)
```

```python
from contextlib import ExitStack

import numpy as np

import concourse.bass as bass
from concourse import mybir
from concourse.alu_op_type import AluOpType as ALU

F32 = mybir.dt.float32
ACT = mybir.ActivationFunctionType
AXX = mybir.AxisListType.X

B, CIN, IMG, PATCH, D = 32, 3, 112, 16, 192
G = IMG // PATCH
NTOK = G * G
S = NTOK + 2
PIX = PATCH * PATCH
KPIX = CIN * PIX
KC = KPIX // 128
DA, DB = 128, D - 128
NCH, CI = 4, 8
CT = NTOK * CI
NPAIR = NCH // 2
HD = D // 2
NH, DH = 12, 16
HP = NH // 2
NG, GI = 8, 4
NT = B // 2
ROWS = 64
NMAIN = S - 6
HID = 768
HC = HID // 128
NCLS, NEXP = 6, 5
SCALE = float(D) ** -0.5
EPS = 1e-5

VEC = {}
for _name in ("bias_loc", "bias_g", "bias_mixed", "alpha_A", "alpha_P", "plb_A", "plb_P", "pgb_A", "pgb_P",
              "b2_A", "b2_P", "f1b_A", "f1b_P", "f2b_A", "f2b_P"):
    VEC[_name] = (len(VEC), 1)
_at = len(VEC)
for _name in ("dw_loc", "dw_g", "dw_mixed", "f1_A", "f1_P", "f2_A", "f2_P", "f3_A", "f3_P"):
    VEC[_name] = (_at, 9)
    _at += 9
VEC["moe_b1"] = (_at, HC)
VEC["exp_b1"] = (_at + HC, NEXP * HC)
NVEC = _at + HC + NEXP * HC
LAYERS = ("loc", "g", "w2", "f1", "f2", "f3")
LW = 2 * D + 128


def vit_tower(nc, x, plw, w1k, had, pww, vec, bcw, cst, wqk, wout, mw1, mw2, a1, a2, gw, out_main, out_cls, h2x):
    ctx = ExitStack()
    with ctx:
        def sb(name, cols, parts=128):
            return ctx.enter_context(nc.sbuf_tensor(name, [parts, cols], F32))

        def sem(name):
            return ctx.enter_context(nc.semaphore(name))

        xreg = sb("xreg", NCH * KC * CT)
        wereg = sb("wereg", 2 * GI * HP * S)
        hadreg = sb("hadreg", CIN * 2 * D + 2 * PIX)
        gelreg = sb("gelreg", 2 * NCH * CT)
        dwreg = sb("dwreg", 2 * NCH * CT)
        mixreg = sb("mixreg", 2 * NCH * CT)
        locreg = sb("locreg", 12 * CT)
        g2reg = sb("g2reg", 6 * CT)
        cureg = sb("cureg", 6 * CT)
        tapreg = sb("tapreg", 6 * CT)
        A2 = sb("A2", HC * NEXP * D)
        MW1 = sb("MW1", 2 * HID, HD)
        MW2 = sb("MW2", HC * D)
        WQK = sb("WQK", 2 * 2 * D, HD)
        WOUT = sb("WOUT", 2 * D, HD)
        PW = sb("PW", len(LAYERS) * LW)
        V = sb("V", NVEC)
        BC = sb("BC", 7 * D)
        CST = sb("CST", 128 + HP + 1)
        GW = sb("GW", 2 * NCLS * 2, HD)

        X = xreg[:, :].rearrange("p (c k n) -> p c k n", c=NCH, k=KC)
        WE = wereg[:, 0:KC * 2 * D].rearrange("p (k n) -> p k n", k=KC)
        W1K = hadreg[:, 0:CIN * 2 * D].rearrange("p (h c o) -> p h c o", h=2, c=CIN)
        HAD = hadreg[:, CIN * 2 * D:CIN * 2 * D + 2 * PIX].rearrange("p (h x) -> p h x", h=2)
        GA = gelreg[:, :].rearrange("p (b c n) -> p b c n", b=2, c=NCH)
        DWA = dwreg[:, :].rearrange("p (b c n) -> p b c n", b=2, c=NCH)
        GM = mixreg[:, 0:NCH * CT].rearrange("p (c n) -> p c n", c=NCH)
        DWM = mixreg[:, NCH * CT:2 * NCH * CT].rearrange("p (c n) -> p c n", c=NCH)

        def six(reg, i=0):
            return reg[:, i * 6 * CT:(i + 1) * 6 * CT].rearrange("p (u n) -> p u n", u=6)

        LOC, LM = six(locreg, 0), six(locreg, 1)
        G2, CUR, TAP = six(g2reg), six(cureg), six(tapreg)
        D3A = mixreg[:, 0:B * ROWS]
        D3P = mixreg[:, B * ROWS:B * ROWS + B // 2 * ROWS]
        DG = xreg[:, 0:3 * 9 * 128].rearrange("p (f t n) -> p f t n", f=3, t=9)
        A1 = xreg[0:HD, 0:2 * NEXP * HID].rearrange("p (k e n) -> p k e n", k=2, e=NEXP)
        o = 2 * NEXP * HID
        T3B, XN, XN2, Y = (xreg[:, o + i * 2 * D:o + (i + 1) * 2 * D] for i in range(4))
        BD = wereg[0:HD, :].rearrange("p (k i h j) -> p k i h j", k=2, i=GI, h=HP)
        QT = hadreg[0:HD, 0:2 * GI * ROWS].rearrange("p (k i j) -> p k i j", k=2, i=GI)
        KT2 = hadreg[0:HD, 2 * GI * ROWS:6 * GI * ROWS].rearrange("p (m d j) -> p m d j", m=2 * GI, d=2)
        T3 = gelreg[:, 0:NT * D]
        H = dwreg[:, 0:NT * D]
        H2 = mixreg[:, 0:NT * D]
        H2B = H
        HE = [g2reg[:, i * HC * 2 * HD:(i + 1) * HC * 2 * HD].rearrange("p (c r n) -> p c r n", c=HC, r=2)
              for i in range(2)]
        low = locreg[:, 6 * CT:12 * CT]
        HIDT = low[:, 0:HC * GI * ROWS].rearrange("p (c i j) -> p c i j", c=HC, i=GI)
        KV = low[:, HC * GI * ROWS:HC * GI * ROWS + GI * 2 * HP * 17].rearrange("p (i h d) -> p i h d", i=GI, d=17)
        P = g2reg[:, 0:2 * NH * ROWS].rearrange("p (u h j) -> p u h j", u=2, h=NH)
        PT = g2reg[:, 2 * NH * ROWS:2 * NH * ROWS + HP * 128].rearrange("p (a i) -> p a i", a=HP)
        XT = sb("XT", 2 * GI * S, HD)
        X2T = sb("X2T", 2 * GI * ROWS, HD)
        TOK = sb("TOK", 2 * 2 * 3 * B, HD)
        OTOK = sb("OTOK", D)
        OT = sb("OT", 2 * 128, HD)
        HC2 = sb("HC2", 2 * D, 96)
        EU = sb("EU", 4 * D, 96)
        ER = sb("ER", 4 * D, 96)
        GT = sb("GT", 64, 96)
        ST = sb("ST", 3 * 2 * 6)
        MV = sb("MV", 3 * 2 * 2)
        VE = sb("VE", 3 * 2)
        RS = sb("RS", 4 * 2)
        MX = sb("MX", 2 * NH)
        RD = sb("RD", NH)
        TH = sb("TH", 10)
        NEG = sb("NEG", 1)
        TOKv = TOK[:, :].rearrange("p (k r a n) -> p k r a n", k=2, r=2, a=3)
        IDN = CST[:, 0:128]
        HMASK = CST[0:HD, 128:128 + HP]
        PMASK = CST[:, 128 + HP:128 + HP + 1]
        BF3, LNG, LNB, MB2, EB3, EB4, EBK = (BC[:, i * D:(i + 1) * D] for i in range(7))

        def v(name, i=0):
            return V[:, VEC[name][0] + i:VEC[name][0] + i + 1]

        PSUM = ctx.enter_context(nc.psum_tensor("PSUM", [128, 8, 512], F32))

        ld_had, ld_plw, ld_x, ld_vec, ld_cst, ld_bc, ld_pw = (
            sem("ld_had"), sem("ld_plw"), [sem(f"ld_x{c}") for c in range(NCH)], sem("ld_vec"), sem("ld_cst"),
            sem("ld_bc"), sem("ld_pw"))
        ld_attn, ld_moe, ld_a1, ld_a2, ld_gw = sem("ld_attn"), sem("ld_moe"), sem("ld_a1"), sem("ld_a2"), sem("ld_gw")
        acc_done = sem("acc_done")
        acc_read = sem("acc_read")
        centre = sem("centre")
        tap = sem("tap")
        fused = sem("fused")
        tanh_done, gate_step = sem("tanh_done"), sem("gate_step")
        d3_zero, d3_ready, t3_ready = sem("d3_zero"), sem("d3_ready"), sem("t3_ready")
        consts = sem("consts")
        dg_ready = sem("dg_ready")
        passed = sem("passed")
        pads_zero = sem("pads_zero")
        biased, scaled, h_ready, norm3 = sem("biased"), sem("scaled"), sem("h_ready"), sem("norm3")
        stats = [sem(f"stats{i}") for i in range(3)]
        meanvar = [sem(f"meanvar{i}") for i in range(3)]
        var_eps = [sem(f"var_eps{i}") for i in range(3)]
        rstd = [sem(f"rstd{i}") for i in range(3)]
        rstd_masked = sem("rstd_masked")
        xn_ready, xn2_ready = sem("xn_ready"), sem("xn2_ready")
        t1_done, xt_ready, q_done, q_ready, k_done, k_ready = (
            sem("t1_done"), sem("xt_ready"), sem("q_done"), sem("q_ready"), sem("k_done"), sem("k_ready"))
        bd_ready, kt_done, kv_ready, s_done, smax, d_ready, p_ready = (
            sem("bd_ready"), sem("kt_done"), sem("kv_ready"), sem("s_done"), sem("smax"), sem("d_ready"), sem("p_ready"))
        pt_done, pt_lo, pt_hi, av_done, rden, o_ready = (
            sem("pt_done"), sem("pt_lo"), sem("pt_hi"), sem("av_done"), sem("rden"), sem("o_ready"))
        ot_done, ot_ready, proj_done, h2_ready, h2b_ready = (
            sem("ot_done"), sem("ot_ready"), sem("proj_done"), sem("h2_ready"), sem("h2b_ready"))
        t2_done, x2_ready, tok_ready = sem("t2_done"), sem("x2_ready"), sem("tok_ready")
        f1_done, gelu_done, f2_done, y_ready, y_free = (
            sem("f1_done"), sem("gelu_done"), sem("f2_done"), sem("y_ready"), sem("y_free"))
        h2x_stored, hc_loaded, gate_done, gate_max, gate_exp, gate_dve = (
            sem("h2x_stored"), sem("hc_loaded"), sem("gate_done"), sem("gate_max"), sem("gate_exp"), sem("gate_dve"))
        e1_done, e1_read, e2_done, e_mix, cls_stored = (
            sem("e1_done"), sem("e1_read"), sem("e2_done"), sem("e_mix"), sem("cls_stored"))
        block = ctx.enter_context(nc.Block())

        STEPS = [("w", 0), ("e", 0), ("e", 1), ("e", 2), ("e", 3), ("loc", 0), ("g", 0), ("w2", 0),
                 ("loc", 1), ("g", 1), ("w2", 1), ("f1", 0), ("p1", 1), ("f1", 1), ("p2", 0), ("f2", 0),
                 ("p2", 1), ("f2", 1), ("p3", 0), ("f3", 0), ("p3", 1), ("f3", 1)]
        UNITS = {"w": 4, "e": 3, "loc": 3, "g": 3, "w2": 3, "f1": 3, "f2": 3, "f3": 4, "p1": 1, "p2": 1, "p3": 1}
        first_unit, _n = {}, 0
        for st in STEPS:
            first_unit[st] = _n
            _n += UNITS[st[0]]
        NUNITS = _n
        LAST = first_unit[STEPS[-1]]
        LAST_BANKS = (2, 3, 6, 7)
        DW = [("dw", 0), ("dw", 1), ("dw", 2), ("dw", 3), ("f1", 0), ("f1", 1), ("f2", 0), ("f2", 1), ("f3", 0), ("f3", 1)]
        dw_at = {b: i for i, b in enumerate(DW)}

        def on_pe(b):
            return ("p" + b[0][1:], b[1]) in STEPS

        def batch_units(b):
            kind, i = b
            if kind == "dw":
                return [(GA[:, 0, i, :], DWA[:, 0, i, :], "dw_loc"), (GA[:, 1, i, :], DWA[:, 1, i, :], "dw_g"),
                        (GM[:, i, :], DWM[:, i, :], "dw_mixed")]
            units = (2 * i, 2 * i + 1) if on_pe(b) else (2 * i, 2 * i + 1, 4 + i)
            return [(CUR[:, u, :], TAP[:, u, :], kind + ("_P" if u >= 4 else "_A")) for u in units]

        def centres_done(b):
            return sum(len(batch_units(c)) for c in DW[:dw_at[b] + 1])

        def taps_done(b):
            return 8 * centres_done(b)

        SHIFTS = [(dy, dx) for dy in (-1, 0, 1) for dx in (-1, 0, 1) if (dy, dx) != (0, 0)]

        def shifted(ap, dy, dx, inp):
            ys = slice(max(0, dy), G + min(0, dy)) if inp else slice(max(0, -dy), G - max(0, dy))
            lo = max(0, dx) if inp else max(0, -dx)
            n = G - abs(dx)
            return ap.rearrange("p (y x) -> p y x", y=G)[:, ys, lo * CI:(lo + n) * CI]

        nfused = {("w2", 0): 3, ("w2", 1): 6, ("f2", 0): 9, ("f2", 1): 12}

        def units_of_pair(i):
            return (2 * i, 2 * i + 1, 4 + i)

        def bank_of(n):
            return n % 8 if n < LAST else LAST_BANKS[n - LAST]

        def bank(n, cols, parts=slice(0, 128)):
            return PSUM[parts, bank_of(n), 0:cols]

        def times(g, k, c=0):
            return k * g + c

        def wait(eng, s, value):
            if not isinstance(value, int) or value > 0:
                eng.wait_ge(s, value)

        @block.sync
        def _(sp):
            sp.dma_start(HAD, had).then_inc(ld_had, 16)
            sp.dma_start(W1K, w1k).then_inc(ld_had, 16)
            sp.dma_start(WE[:, :, 0:DA], plw[:, :, 0:DA]).then_inc(ld_plw, 16)
            sp.dma_start(WE[:, :, 2 * DA:2 * DA + DB], plw[:, :, DA:D]).then_inc(ld_plw, 16)
            sp.dma_start(X[:, 0, :, :], x[:, 0, :, :]).then_inc(ld_x[0], 16)
            sp.dma_start(V[:, :], vec).then_inc(ld_vec, 16)
            for c in range(1, NCH):
                sp.dma_start(X[:, c, :, :], x[:, c, :, :]).then_inc(ld_x[c], 16)
            sp.dma_start(PW[:, :], pww).then_inc(ld_pw, 16)
            sp.dma_start(CST[:, :], cst).then_inc(ld_cst, 16)
            sp.dma_start(BC[:, :], bcw).then_inc(ld_bc, 16)
            sp.dma_start(WQK[:, :], wqk).then_inc(ld_attn, 16)
            sp.dma_start(WOUT[:, :], wout).then_inc(ld_attn, 16)
            sp.dma_start(MW1[:, :], mw1).then_inc(ld_moe, 16)
            sp.dma_start(MW2[:, :], mw2).then_inc(ld_moe, 16)
            sp.dma_start(A2[:, :], a2).then_inc(ld_a2, 16)
            sp.dma_start(GW[:, :], gw).then_inc(ld_gw, 16)
            sp.wait_ge(acc_done, first_unit[("p3", NPAIR - 1)] + 1)
            sp.dma_start(A1[:, :, :, :], a1).then_inc(ld_a1, 16)

            def store(g):
                wait(sp, y_ready, times(g, 1, 1))
                sp.dma_start(out_main[:, bass.ds(times(g, 2 * D), 2 * D)], Y).then_inc(y_free, 16)

            with sp.Fori(0, NG - 1) as g:
                store(g)
            sp.wait_ge(h2_ready, NT)
            for e in range(2):
                sp.dma_start(h2x[:, e, :, :], H2[ROWS * e + NMAIN:ROWS * e + S, :].rearrange("p (t c) -> p t c", c=D)).then_inc(h2x_stored, 16)
            sp.wait_ge(h2x_stored, 32)
            for a in range(3):
                for r in range(2):
                    row = (2 * a + r - 2) % NCLS
                    sp.dma_start(HC2[B * a:B * a + B, r * D:(r + 1) * D], h2x[row, :, :, :].rearrange("e t c -> (e t) c")).then_inc(hc_loaded, 16)
            store(NG - 1)
            sp.wait_ge(e_mix, 8)
            sp.dma_start(out_cls, ER[:, 2 * D:4 * D]).then_inc(cls_stored, 16)
            sp.wait_ge(cls_stored, 16)
            sp.wait_ge(y_free, 16 * (NG + 1))

        @block.tensor
        def _(pe):
            def mm(out, lhsT, rhs, start, stop):
                return nc.tensor.matmul(out, lhsT, rhs, start=start, stop=stop)

            def free_bank(n):
                if 8 <= n < LAST:
                    pe.wait_ge(acc_read, n - 7)

            def haar_weights():
                pe.wait_ge(ld_had, 32)
                for j, (m, c0, nco) in enumerate(((0, 0, 2), (0, 2, 1), (1, 0, 2), (1, 2, 1))):
                    for h in range(2):
                        last = mm(bank(j, nco * D), HAD[:, h, m * 128:(m + 1) * 128],
                                  W1K[:, h, c0:c0 + nco, :], h == 0, h == 1)
                    last.then_inc(acc_done, 1)

            def embed(c):
                n = first_unit[("e", c)]
                pe.wait_ge(ld_x[c], 16)
                if c == 0:
                    pe.wait_ge(ld_plw, 32)
                for j, w0 in enumerate((0, DA, 2 * DA)):
                    if c == 0 and j == 1:
                        pe.wait_ge(acc_read, 4)
                    free_bank(n + j)
                    for k in range(KC):
                        last = mm(bank(n + j, CT), WE[:, k, w0:w0 + 128], X[:, c, k, :], k == 0, k == KC - 1)
                    last.then_inc(acc_done, 1)

            def pointwise(layer, i):
                w = LAYERS.index(layer) * LW
                wa, wb, wd = PW[:, w:w + D], PW[:, w + D:w + 2 * D], PW[:, w + 2 * D:w + 2 * D + 128]
                n = first_unit[(layer, i)]
                if layer in ("loc", "g"):
                    pe.wait_ge(tap, taps_done(("dw", 2 * i + 1)))
                    b = ("loc", "g").index(layer)
                    half = slice(DB * b, DB * b + DB)
                    a_in = [DWA[:, b, 2 * i + j, :] for j in range(2)]
                    b_in = [(half, DWM[half, 2 * i + j, :]) for j in range(2)]
                else:
                    if layer == "w2":
                        pe.wait_ge(acc_read, first_unit[("g", i)] + 3)
                        src = G2
                    else:
                        pe.wait_ge(tap, taps_done((layer, i)))
                        if on_pe((layer, i)):
                            pe.wait_ge(acc_read, first_unit[("p" + layer[1], i)] + 1)
                        src = TAP
                    a_in = [src[:, 2 * i + j, :] for j in range(2)]
                    b_in = [(slice(DB * j, DB * j + DB), src[DB * j:DB * j + DB, 4 + i, :]) for j in range(2)]
                for j in range(2):
                    free_bank(n + j)
                    half, rhs = b_in[j]
                    mm(bank(n + j, CT), wa[:, 0:DA], a_in[j], True, False)
                    mm(bank(n + j, CT), wb[half, 0:DA], rhs, False, True).then_inc(acc_done, 1)
                free_bank(n + 2)
                outs = [PSUM[DB * j:DB * j + DB, bank_of(n + 2), 0:CT] for j in range(2)]
                if layer in ("loc", "g"):
                    for j in range(2):
                        mm(outs[j], wa[:, DA:D], a_in[j], True, False)
                    for j in range(2):
                        half, rhs = b_in[j]
                        last = mm(outs[j], wb[half, DA:D], rhs, False, True)
                else:
                    mm(bank(n + 2, CT), wd, src[:, 4 + i, :], True, False)
                    for j in range(2):
                        last = mm(outs[j], wa[:, DA:D], a_in[j], False, True)
                last.then_inc(acc_done, 1)

            def depthwise(layer, i):
                n = first_unit[("p%d" % layer, i)]
                free_bank(n)
                pe.wait_ge(dg_ready, layer)
                if layer == 2:
                    pe.wait_ge(acc_read, first_unit[("f1", i)] + 3)
                else:
                    pe.wait_ge(fused, nfused[("w2" if layer == 1 else "f2", i)])
                src, acc = CUR[:, 4 + i, :], bank(n, CT)
                mm(acc, DG[:, layer - 1, 4, :], src, True, False)
                for j, (dy, dx) in enumerate(SHIFTS):
                    last = mm(shifted(acc, dy, dx, False), DG[:, layer - 1, (dy + 1) * 3 + dx + 1, :],
                              shifted(src, dy, dx, True), False, j == len(SHIFTS) - 1)
                last.then_inc(acc_done, 1)

            def f3_tiles(i):
                w = LAYERS.index("f3") * LW
                wa, wb = PW[:, w:w + D], PW[:, w + D:w + 2 * D]
                n = first_unit[("f3", i)]
                for q in range(4):
                    free_bank(n + q)
                    pe.wait_ge(d3_ready, 2 * i + q // 2 + 1)
                    if on_pe(("f3", i)):
                        pe.wait_ge(acc_read, first_unit[("p3", i)] + 1)
                    for u in range(2):
                        t = 8 * i + 2 * q + u
                        half = slice(DB * (q // 2), DB * (q // 2) + DB)
                        at = (8 * i + 2 * (t % 4)) * ROWS
                        out = PSUM[:, bank_of(n + q), u * D:(u + 1) * D]
                        mm(out, D3A[:, 2 * t * ROWS:(2 * t + 2) * ROWS], wa, True, False)
                        last = mm(out, D3P[half, at:at + 2 * ROWS], wb[half, :], False, True)
                    last.then_inc(acc_done, 1)

            def step(kind, i):
                if kind == "w":
                    haar_weights()
                elif kind == "e":
                    embed(i)
                elif kind == "f3":
                    f3_tiles(i)
                elif kind[0] == "p":
                    depthwise(int(kind[1]), i)
                else:
                    if (kind, i) == ("loc", 0):
                        pe.wait_ge(ld_pw, 16)
                    pointwise(kind, i)

            for st in STEPS[:-1]:
                step(*st)

            def halves(n, cols):
                return PSUM[0:HD, n, 0:2 * cols].rearrange("p (k n) -> p k n", k=2)

            def transpose_in(src, n):
                out = halves(n, 2 * 128)
                for u in range(2):
                    for k in range(2):
                        last = nc.tensor.transpose(out[:, k, u * 128:(u + 1) * 128],
                                                   src[:, u * D + k * HD:u * D + (k + 1) * HD], IDN)
                return last

            def t1(g):
                wait(pe, xn_ready, times(g, 2, 2))
                if not isinstance(g, int) or g > 1:
                    wait(pe, h2_ready, times(g, 2, -2))
                transpose_in(XN, 1).then_inc(t1_done, 1)

            def t2(g):
                wait(pe, xn2_ready, times(g, 2, 2))
                transpose_in(XN2, 0).then_inc(t2_done, 1)

            def q_or_k(g, which):
                wait(pe, xt_ready, times(g, 1, 1))
                if which == 0 and (not isinstance(g, int) or g > 1):
                    wait(pe, x2_ready, times(g, 1, -1))
                out = halves(which, GI * S)
                for m in range(2):
                    for k in range(2):
                        last = mm(out[:, m, :], WQK[:, (k * 4 + which * 2 + m) * HD:(k * 4 + which * 2 + m + 1) * HD],
                                  XT[:, k * GI * S:(k + 1) * GI * S], k == 0, k == 1)
                last.then_inc((q_done, k_done)[which], 1)

            def kt(g):
                wait(pe, k_ready, times(g, 1, 1))
                wait(pe, pt_lo, times(g, 2))
                wait(pe, pt_hi, times(g, 2))
                for n in range(2):
                    for i in range(2):
                        for k in range(2):
                            last = nc.tensor.transpose(PSUM[:, 4 + n, i * D + k * HD:i * D + (k + 1) * HD],
                                                       KT2[:, k * GI + 2 * n + i, :, :], IDN[0:HD, 0:HD])
                    last.then_inc(kt_done, 1)

            def scores(g, u):
                wait(pe, d_ready, times(g, 2, u))
                if u == 0:
                    wait(pe, bd_ready, times(g, 1, 1))
                for k in range(2):
                    for e in range(2):
                        last = mm(PSUM[ROWS * e:ROWS * e + ROWS, 2 + k, 0:HP * S], QT[:, k, 2 * u + e, :],
                                  BD[:, k, 2 * u + e, :, :], True, True)
                last.then_inc(s_done, 1)

            def transpose_probs(g, u):
                wait(pe, p_ready, times(g, 2, u + 1))
                if u == 0:
                    wait(pe, kv_ready, times(g, 2, 2))
                else:
                    wait(pe, pt_lo, times(g, 2, 1))
                    wait(pe, pt_hi, times(g, 2, 1))
                for a in range(HP):
                    last = nc.tensor.transpose(PSUM[:, 4 + a // 3, (a % 3) * 128:(a % 3 + 1) * 128],
                                               P[:, u, 2 * a:2 * a + 2, :], IDN)
                last.then_inc(pt_done, 1)

            def attend(g, u, ahead):
                wait(pe, pt_lo, times(g, 2, u + 1))
                wait(pe, pt_hi, times(g, 2, u + 1))
                if u == 0 and ahead:
                    wait(pe, q_ready, times(g, 1, 2))
                elif u == 0:
                    wait(pe, x2_ready, times(g, 1))
                else:
                    wait(pe, o_ready, times(g, 2, 1))
                for a in range(HP):
                    for e in range(2):
                        last = mm(PSUM[ROWS * e:ROWS * e + ROWS, 0, a * 34:(a + 1) * 34],
                                  PT[:, a, ROWS * e:ROWS * e + ROWS], KV[:, 2 * u + e, 2 * a:2 * a + 2, :], True, True)
                last.then_inc(av_done, 1)

            def transpose_out(g, u, ahead):
                wait(pe, o_ready, times(g, 2, u + 1))
                if u == 0 and ahead:
                    wait(pe, k_ready, times(g, 1, 2))
                n = 1 - u
                for k in range(2):
                    last = nc.tensor.transpose(PSUM[0:HD, n, k * 128:(k + 1) * 128], OTOK[:, k * HD:(k + 1) * HD], IDN)
                last.then_inc(ot_done, 1)

            def project(g, u):
                wait(pe, ot_ready, times(g, 2, u + 1))
                if u == 1:
                    wait(pe, h2_ready, times(g, 2, 1))
                for k in range(2):
                    last = mm(PSUM[:, 1, 0:D], OT[:, k * 128:(k + 1) * 128], WOUT[:, k * D:(k + 1) * D], k == 0, k == 1)
                last.then_inc(proj_done, 1)

            def ffn_up(g, j):
                if j == 0:
                    wait(pe, x2_ready, times(g, 1, 1))
                    wait(pe, gelu_done, times(g, 3))
                elif j == 1:
                    wait(pe, y_ready, times(g, 1))
                else:
                    wait(pe, gelu_done, times(g, 3, 1))
                x2 = X2T[:, :].rearrange("p (k i j) -> p k i j", k=2, i=GI)
                for c in (2 * j, 2 * j + 1):
                    for k in range(2):
                        last = mm(PSUM[:, 6 + j % 2, (c % 2) * GI * NMAIN:(c % 2 + 1) * GI * NMAIN],
                                  MW1[:, k * HID + c * 128:k * HID + (c + 1) * 128], x2[:, k, :, 0:NMAIN],
                                  k == 0, k == 1)
                last.then_inc(f1_done, 1)

            def ffn_down(g, u):
                if u == 0:
                    wait(pe, gelu_done, times(g, 3, 3))
                for c in range(HC):
                    last = mm(PSUM[:, 7, u * D:(u + 1) * D], HIDT[:, c, 2 * u:2 * u + 2, :],
                              MW2[:, c * D:(c + 1) * D], c == 0, c == HC - 1)
                if u == 1:
                    last.then_inc(f2_done, 1)

            def body(g, ahead, ffn):
                scores(g, 0)
                if ffn:
                    t2(g - 1)
                if ahead:
                    t1(g + 1)
                if ffn:
                    ffn_up(g - 1, 0)
                scores(g, 1)
                if ahead:
                    q_or_k(g + 1, 0)
                if ffn:
                    ffn_up(g - 1, 1)
                transpose_probs(g, 0)
                if ahead:
                    q_or_k(g + 1, 1)
                attend(g, 0, ahead)
                transpose_probs(g, 1)
                if ffn:
                    ffn_up(g - 1, 2)
                transpose_out(g, 0, ahead)
                attend(g, 1, ahead)
                if ahead:
                    kt(g + 1)
                project(g, 0)
                transpose_out(g, 1, ahead)
                if ffn:
                    ffn_down(g - 1, 0)
                project(g, 1)
                if ffn:
                    ffn_down(g - 1, 1)

            pe.wait_ge(ld_cst, 16)
            pe.wait_ge(ld_attn, 32)
            pe.wait_ge(ld_moe, 32)
            pe.wait_ge(acc_read, LAST)
            t1(0)
            q_or_k(0, 0)
            q_or_k(0, 1)
            step(*STEPS[-1])
            kt(0)
            pe.wait_ge(pads_zero, 2)
            pe.wait_ge(acc_read, NUNITS)
            body(0, True, False)
            body(1, True, True)
            with pe.Fori(2, NG - 1) as g:
                body(g, True, True)
            body(NG - 1, False, True)
            t2(NG - 1)

            pe.wait_ge(tok_ready, NG)
            pe.wait_ge(ld_gw, 16)
            gwv = GW[:, :].rearrange("p (k r a n) -> p k r a n", k=2, r=2, a=3)
            for r in range(2):
                for a in range(3):
                    for k in range(2):
                        last = mm(PSUM[B * a:B * a + B, 0, 2 * r:2 * r + 2], TOKv[:, k, r, a, :], gwv[:, k, r, a, :],
                                  k == 0, k == 1)
            last.then_inc(gate_done, 1)
            for j in range(3):
                ffn_up(NG - 1, j)
            pe.wait_ge(ld_a1, 16)
            for n, (a, c0, c1) in enumerate(((0, 0, 6), (1, 0, 6), (2, 0, 6), (3, 0, 3), (3, 3, 6), (4, 0, 3), (4, 3, 6))):
                w = 64 if a < 3 else 96
                nb = 1 + n if n < 5 else n - 4
                if n >= 5:
                    pe.wait_ge(e1_read, n - 4)
                for c in range(c0, c1):
                    for k in range(2):
                        rhs = TOKv[:, k, :, a, :] if a < 3 else TOKv[:, k, a - 3, :, :]
                        last = mm(PSUM[:, nb, (c - c0) * w:(c - c0 + 1) * w],
                                  A1[:, k, a, c * 128:(c + 1) * 128], rhs, k == 0, k == 1)
                last.then_inc(e1_done, 1)
                if n == 2:
                    ffn_down(NG - 1, 0)
                    ffn_down(NG - 1, 1)
            pe.wait_ge(ld_a2, 16)
            pe.wait_ge(e1_read, 3)
            a2v = A2[:, :].rearrange("p (c e n) -> p c e n", c=HC, e=NEXP)
            pe.wait_ge(gate_max, 1)
            for r in range(2):
                for c in range(HC):
                    last = mm(PSUM[0:96, 0, r * D:(r + 1) * D], HE[0][:, c, r, :], a2v[:, c, 3 + r, :], c == 0, c == HC - 1)
            last.then_inc(e2_done, 1)
            pe.wait_ge(e1_read, 7)
            for r in range(2):
                for c in range(HC):
                    for a in range(3):
                        last = mm(PSUM[B * a:B * a + B, 3, r * D:(r + 1) * D], HE[1][:, c, r, B * a:B * a + B],
                                  a2v[:, c, a, :], c == 0, c == HC - 1)
            last.then_inc(e2_done, 1)

        @block.scalar
        def _(act):
            def read(n, done=1):
                act.wait_ge(acc_done, n + 1)

            def centre_taps(b):
                for src, dst, f in batch_units(b):
                    nc.scalar.activation(dst, src, ACT.Copy, scale=v(f, 4)).then_inc(centre, 1)

            def haar_evict():
                for j, (m, c0, nco) in enumerate(((0, 0, 2), (0, 2, 1), (1, 0, 2), (1, 2, 1))):
                    read(j)
                    src = bank(j, nco * D).rearrange("p (c o) -> p c o", o=D)
                    dst = WE[:, 2 * c0 + m:2 * (c0 + nco - 1) + m + 1:2, :]
                    nc.scalar.activation(dst[:, :, DA:2 * DA], src[:, :, 0:DA], ACT.Copy)
                    nc.scalar.activation(dst[:, :, 2 * DA + DB:], src[:, :, DA:D], ACT.Copy).then_inc(acc_read, 1)

            def embed_evict(c):
                n = first_unit[("e", c)]
                for j, (dst, bias) in enumerate(((GA[:, 0, c, :], "bias_loc"), (GA[:, 1, c, :], "bias_g"),
                                                 (GM[:, c, :], "bias_mixed"))):
                    read(n + j)
                    nc.scalar.activation(dst, bank(n + j, CT), ACT.Gelu, bias=v(bias)).then_inc(acc_read, 1)
                act.wait_ge(acc_read, n + 3)
                centre_taps(("dw", c))

            def pointwise_evict(layer, i):
                n = first_unit[(layer, i)]
                for j, u in enumerate(units_of_pair(i)):
                    part = "_P" if j == 2 else "_A"
                    p = (j == 2)
                    read(n + j)
                    src = bank(n + j, CT)
                    if layer == "loc":
                        nc.scalar.activation(LOC[:, u, :], src, ACT.Identity, bias=v("plb" + part))
                        if i == 0 and j == 0:
                            act.wait_ge(gate_step, 8)
                        nc.scalar.activation(LM[:, u, :], src, ACT.Identity, bias=TH[:, 8 + p:9 + p],
                                             scale=TH[:, 4 + p:5 + p]).then_inc(acc_read, 1)
                    elif layer == "g":
                        nc.scalar.activation(G2[:, u, :], src, ACT.Gelu, bias=v("pgb" + part)).then_inc(acc_read, 1)
                    elif layer == "w2":
                        nc.scalar.activation(CUR[:, u, :], src, ACT.Copy, scale=TH[:, 2 + p:3 + p]).then_inc(acc_read, 1)
                    else:
                        nc.scalar.activation(CUR[:, u, :], src, ACT.Relu, bias=v(layer + "b" + part)).then_inc(acc_read, 1)


            def by_image(src, dst):
                s = src.rearrange("p (t i) -> p i t", i=CI)
                d = dst.rearrange("p (i r) -> p i r", r=ROWS)
                nc.scalar.activation(d[:, :, 0:NMAIN], s[:, :, 4:NTOK], ACT.Copy)
                return nc.scalar.activation(d[:, :, NMAIN:NTOK], s[:, :, 0:4], ACT.Copy)

            def d3(i):
                act.wait_ge(tap, taps_done(("f3", i)))
                act.wait_ge(d3_zero, 1)
                for j in range(2):
                    c = 2 * i + j
                    by_image(TAP[:, c, :], D3A[:, c * CI * ROWS:(c + 1) * CI * ROWS]).then_inc(d3_ready, 1)

            def depthwise_evict(layer, i):
                n = first_unit[("p%d" % layer, i)]
                read(n)
                if layer == 3:
                    act.wait_ge(d3_zero, 1)
                    by_image(bank(n, CT), D3P[:, i * CI * ROWS:(i + 1) * CI * ROWS]).then_inc(acc_read, 1)
                else:
                    nc.scalar.activation(TAP[:, 4 + i, :], bank(n, CT), ACT.Copy).then_inc(acc_read, 1)

            def f3_evict(i):
                n = first_unit[("f3", i)]
                for q in range(4):
                    read(n + q)
                    nc.scalar.activation(T3[:, (4 * i + q) * 2 * D:(4 * i + q + 1) * 2 * D], bank(n + q, 2 * D),
                                         ACT.Copy).then_inc(acc_read, 1)

            act.wait_ge(ld_vec, 16)
            a0 = VEC["alpha_A"][0]
            nc.scalar.activation(TH[:, 0:2], V[:, a0:a0 + 2], ACT.Tanh).then_inc(tanh_done, 1)
            act.wait_ge(ld_plw, 32)
            haar_evict()
            for c in range(NCH):
                embed_evict(c)
            for i in range(NPAIR):
                pointwise_evict("loc", i)
                pointwise_evict("g", i)
                pointwise_evict("w2", i)
                act.wait_ge(fused, nfused[("w2", i)])
                centre_taps(("f1", i))
            for i in range(NPAIR):
                if on_pe(("f1", i)):
                    depthwise_evict(1, i)
                pointwise_evict("f1", i)
                act.wait_ge(acc_read, first_unit[("f1", i)] + 3)
                centre_taps(("f2", i))
            depthwise_evict(2, 0)
            pointwise_evict("f2", 0)
            depthwise_evict(2, 1)
            act.wait_ge(fused, nfused[("f2", 0)])
            centre_taps(("f3", 0))
            pointwise_evict("f2", 1)
            act.wait_ge(fused, nfused[("f2", 1)])
            centre_taps(("f3", 1))
            depthwise_evict(3, 0)
            d3(0)
            f3_evict(0)
            depthwise_evict(3, 1)

            def halves(n, cols):
                return PSUM[0:HD, n, 0:2 * cols].rearrange("p (k n) -> p k n", k=2)

            def xt(g):
                wait(act, t1_done, times(g, 1, 1))
                src = PSUM[0:HD, 1, :].rearrange("p (m j) -> p m j", j=ROWS)
                wait(act, k_done, times(g, 1))
                nc.scalar.activation(XT[:, :].rearrange("p (m j) -> p m j", j=S), src[:, :, 0:S], ACT.Copy).then_inc(xt_ready, 1)

            def x2t(g):
                wait(act, t2_done, times(g, 1, 1))
                wait(act, tok_ready, times(g, 1))
                wait(act, f1_done, times(g, 3))
                nc.scalar.activation(X2T[:, :], PSUM[0:HD, 0, :], ACT.Copy).then_inc(x2_ready, 1)

            def qt(g):
                wait(act, q_done, times(g, 1, 1))
                wait(act, s_done, times(g, 2))
                nc.scalar.activation(QT[:, :, :, 0:S].rearrange("p k i j -> p (k i) j"),
                                     PSUM[0:HD, 0, 0:2 * GI * S].rearrange("p (m j) -> p m j", j=S), ACT.Copy).then_inc(q_ready, 1)

            def kt2(g):
                wait(act, k_done, times(g, 1, 1))
                wait(act, kt_done, times(g, 2))
                wait(act, bd_ready, times(g, 1))
                src = PSUM[0:HD, 1, 0:2 * GI * S].rearrange("p (m o j) -> p m o j", o=1, j=S)
                nc.scalar.activation(KT2[:, :, :, 0:S], src.to_broadcast([HD, 2 * GI, 2, S]), ACT.Copy).then_inc(k_ready, 1)

            def kv(g):
                for n in range(2):
                    wait(act, kt_done, times(g, 2, n + 1))
                    wait(act, av_done, times(g, 2))
                    for r in range(2):
                        half = slice(ROWS * r, ROWS * r + ROWS)
                        for i in range(2):
                            src = PSUM[half, 4 + n, i * D:(i + 1) * D].rearrange("p (a d) -> p a d", d=2 * DH)
                            dst = KV[half, 2 * n + i, r:NH:2, 0:DH]
                            last = nc.scalar.activation(dst, src[:, :, r * DH:(r + 1) * DH], ACT.Copy)
                    last.then_inc(kv_ready, 1)

            def exps(g, u):
                wait(act, d_ready, times(g, 2, u + 1))
                nc.scalar.activation(P[:, u, :, 0:S], P[:, u, :, 0:S], ACT.Exp, scale=SCALE).then_inc(p_ready, 1)

            def probs_lo(g, u):
                wait(act, pt_done, times(g, 2, u + 1))
                wait(act, av_done, times(g, 2, u))
                nc.scalar.activation(PT[:, 0:3, :].rearrange("p a i -> p (a i)"), PSUM[:, 4, 0:384], ACT.Copy).then_inc(pt_lo, 1)

            def ot(g, u):
                wait(act, ot_done, times(g, 2, u + 1))
                wait(act, proj_done, times(g, 2, u))
                nc.scalar.activation(OT[:, :], PSUM[0:HD, 1 - u, 0:256], ACT.Copy).then_inc(ot_ready, 1)

            def gelus(g, j):
                wait(act, f1_done, times(g, 3, j + 1))
                wait(act, f2_done, times(g, 1))
                for c in (2 * j, 2 * j + 1):
                    src = PSUM[:, 6 + j % 2, (c % 2) * GI * NMAIN:(c % 2 + 1) * GI * NMAIN].rearrange("p (i j) -> p i j", j=NMAIN)
                    last = nc.scalar.activation(HIDT[:, c, :, 0:NMAIN], src, ACT.Gelu, bias=v("moe_b1", c))
                last.then_inc(gelu_done, 1)

            def body(g, ahead, ffn):
                if ffn:
                    x2t(g - 1)
                if ahead:
                    xt(g + 1)
                exps(g, 0)
                if ahead:
                    qt(g + 1)
                exps(g, 1)
                probs_lo(g, 0)
                if ahead:
                    kt2(g + 1)
                if ffn:
                    gelus(g - 1, 0)
                    gelus(g - 1, 1)
                probs_lo(g, 1)
                if ffn:
                    gelus(g - 1, 2)
                ot(g, 0)
                if ahead:
                    kv(g + 1)
                ot(g, 1)

            act.wait_ge(pads_zero, 2)
            xt(0)
            qt(0)
            kt2(0)
            d3(1)
            f3_evict(1)
            kv(0)
            body(0, True, False)
            body(1, True, True)
            with act.Fori(2, NG - 1) as g:
                body(g, True, True)
            body(NG - 1, False, True)
            x2t(NG - 1)
            act.wait_ge(gate_max, 2)
            nc.scalar.activation(GT[:, 4:8], GT[:, 4:8], ACT.Exp).then_inc(gate_exp, 1)
            for j in range(3):
                gelus(NG - 1, j)
            for n, (a, c0, c1) in enumerate(((0, 0, 6), (1, 0, 6), (2, 0, 6), (3, 0, 3), (3, 3, 6), (4, 0, 3), (4, 3, 6))):
                act.wait_ge(e1_done, n + 1)
                nb = 1 + n if n < 5 else n - 4
                w = 64 if a < 3 else 96
                for c in range(c0, c1):
                    src = PSUM[:, nb, (c - c0) * w:(c - c0 + 1) * w]
                    if a < 3:
                        src = src.rearrange("p (r n) -> p r n", r=2)
                        dst = HE[0][:, c, :, B * a:B * a + B]
                    else:
                        dst = HE[1][:, c, a - 3, :]
                    last = nc.scalar.activation(dst, src, ACT.Gelu, bias=v("exp_b1", a * HC + c))
                last.then_inc(e1_read, 1)

        @block.vector
        def _(dve):
            steps = [0]

            def step(ins):
                steps[0] += 1
                ins.then_inc(gate_step, 1)
                dve.wait_ge(gate_step, steps[0])

            dve.sem_inc(y_free, 16)
            dve.wait_ge(tanh_done, 1)
            dve.wait_ge(ld_vec, 16)
            p0, q0 = VEC["plb_A"][0], VEC["b2_A"][0]
            step(nc.vector.tensor_scalar(TH[:, 2:4], TH[:, 0:2], 1.0, 0.5, ALU.add, ALU.mult))
            step(nc.vector.tensor_scalar(TH[:, 4:6], TH[:, 2:4], -1.0, 1.0, ALU.mult, ALU.add))
            step(nc.vector.tensor_tensor(TH[:, 6:8], TH[:, 2:4], V[:, q0:q0 + 2], ALU.mult))
            step(nc.vector.tensor_tensor(TH[:, 8:10], TH[:, 4:6], V[:, p0:p0 + 2], ALU.mult))
            step(nc.vector.tensor_tensor(TH[:, 8:10], TH[:, 8:10], TH[:, 6:8], ALU.add))
            step(nc.vector.memset(NEG[:, :], -0.5))
            step(nc.vector.tensor_copy(TH[:, 0:2], TH[:, 2:4]))
            step(nc.vector.tensor_copy(TH[:, 6:8], TH[:, 4:6]))

            def taps(b, j0=0, j1=len(SHIFTS)):
                units = batch_units(b)
                before = taps_done(b) - 8 * len(units)
                if j0 == 0:
                    dve.wait_ge(centre, centres_done(b))
                for j in range(j0, j1):
                    dy, dx = SHIFTS[j]
                    for i, (src, dst, f) in enumerate(units):
                        if j:
                            dve.wait_ge(tap, before + len(units) * (j - 1) + i + 1)
                        acc = shifted(dst, dy, dx, False)
                        nc.vector.scalar_tensor_tensor(out=acc, in0=shifted(src, dy, dx, True),
                                                       scalar=v(f, (dy + 1) * 3 + dx + 1), in1=acc,
                                                       op0=ALU.mult, op1=ALU.add).then_inc(tap, 1)

            def fuse(layer, i, other):
                n = first_unit[(layer, i)]
                for j, u in enumerate(units_of_pair(i)):
                    dve.wait_ge(acc_read, n + j + 1)
                    nc.vector.tensor_tensor(CUR[:, u, :], CUR[:, u, :], other[:, u, :], ALU.add).then_inc(fused, 1)

            for c in range(NCH):
                taps(("dw", c))
            for i in range(NPAIR):
                fuse("w2", i, LM)
                taps(("f1", i))
            for i in range(NPAIR):
                taps(("f2", i))
            fuse("f2", 0, LOC)
            taps(("f3", 0))
            fuse("f2", 1, LOC)

            def wait_bn(s, value):
                wait(dve, s, value)
                if not isinstance(value, int):
                    dve.sem_inc(passed, 1)

            def statistics(i, src, u):
                nc.vector.bn_stats(ST[:, (2 * i + u) * 6:(2 * i + u + 1) * 6], src).then_inc(stats[i], 1)

            def aggregate(i, u):
                return nc.vector.bn_aggr(MV[:, (2 * i + u) * 2:(2 * i + u + 1) * 2], ST[:, (2 * i + u) * 6:(2 * i + u + 1) * 6])

            def add_eps(i, u0, n):
                var = MV[:, (2 * i + u0) * 2:(2 * i + u0 + n) * 2].rearrange("p (u m) -> p u m", m=2)[:, :, 1]
                return nc.vector.tensor_scalar(VE[:, 2 * i + u0:2 * i + u0 + n], var, EPS, None, ALU.add)

            def mean(i, u):
                return MV[:, (2 * i + u) * 2:(2 * i + u) * 2 + 1]

            def both(row):
                return row.rearrange("p (o c) -> p o c", o=1).to_broadcast([128, 2, D])

            T3B2 = T3B.rearrange("p (u c) -> p u c", u=2)

            def tokens_a(g):
                t3 = T3[:, bass.ds(times(g, 2 * D), 2 * D)].rearrange("p (u c) -> p u c", u=2)
                nc.vector.tensor_tensor(T3B2, t3, both(BF3), ALU.add).then_inc(biased, 1)
                wait_bn(biased, times(g, 1, 1))
                for u in range(2):
                    statistics(0, T3B[:, u * D:(u + 1) * D], u)
                for u in range(2):
                    wait_bn(stats[0], times(g, 2, u + 1))
                    aggregate(0, u).then_inc(meanvar[0], 1)
                wait(dve, meanvar[0], times(g, 2, 2))
                add_eps(0, 0, 2).then_inc(var_eps[0], 1)

            def tokens_b(g):
                wait(dve, rstd_masked, times(g, 1, 1))
                for u in range(2):
                    nc.vector.tensor_scalar(T3B[:, u * D:(u + 1) * D], T3B[:, u * D:(u + 1) * D], mean(0, u),
                                            RS[:, 6 + u:7 + u], ALU.subtract, ALU.mult).then_inc(norm3, 1)
                wait(dve, norm3, times(g, 2, 2))
                nc.vector.tensor_tensor(T3B2, T3B2, both(LNG), ALU.mult).then_inc(scaled, 1)
                wait(dve, scaled, times(g, 1, 1))
                h = H[:, bass.ds(times(g, 2 * D), 2 * D)]
                nc.vector.tensor_tensor(h.rearrange("p (u c) -> p u c", u=2), T3B2, both(LNB), ALU.add).then_inc(h_ready, 1)

            def tokens_c(g):
                wait_bn(h_ready, times(g, 1, 1))
                for u in range(2):
                    statistics(1, H[:, bass.ds(times(g, 2 * D, u * D), D)], u)
                for u in range(2):
                    wait_bn(stats[1], times(g, 2, u + 1))
                    aggregate(1, u).then_inc(meanvar[1], 1)
                wait(dve, meanvar[1], times(g, 2, 2))
                add_eps(1, 0, 2).then_inc(var_eps[1], 1)

            def tokens_d(g):
                wait(dve, rstd[1], times(g, 1, 1))
                wait(dve, t1_done, times(g, 1))
                for u in range(2):
                    nc.vector.tensor_scalar(XN[:, u * D:(u + 1) * D], H[:, bass.ds(times(g, 2 * D, u * D), D)], mean(1, u),
                                            RS[:, 2 + u:3 + u], ALU.subtract, ALU.mult).then_inc(xn_ready, 1)

            def tokens(g):
                tokens_a(g)
                tokens_b(g)
                tokens_c(g)
                tokens_d(g)

            def block_diagonal(g, k):
                if k == 0:
                    wait(dve, k_ready, times(g, 1, 1))
                    wait(dve, s_done, times(g, 2))
                for h in range(HP):
                    last = nc.vector.tensor_scalar(BD[:, k, :, h, :], KT2[:, k * GI:(k + 1) * GI, 0, 0:S],
                                                   HMASK[:, h:h + 1], None, ALU.mult)
                if k == 1:
                    last.then_inc(bd_ready, 1)

            def minus_max(g, u):
                wait(dve, s_done, times(g, 2, u + 1))
                s = PSUM[:, 2:4, 0:HP * S].rearrange("p k (h j) -> p k h j", j=S)
                mx = MX[:, u * NH:(u + 1) * NH].rearrange("p (k h) -> p k h", k=2)
                nc.vector.tensor_reduce(mx, s, AXX, ALU.max).then_inc(smax, 1)
                wait(dve, smax, times(g, 2, u + 1))
                wait(dve, pt_done, times(g, 2, u - 1))
                for k in range(2):
                    m = mx[:, k, :].rearrange("p (h o) -> p h o", o=1).to_broadcast([128, HP, S])
                    last = nc.vector.tensor_tensor(P[:, u, k * HP:(k + 1) * HP, 0:S], s[:, k, :, :], m, ALU.subtract)
                last.then_inc(d_ready, 1)

            def probs_hi(g, u):
                wait(dve, pt_done, times(g, 2, u + 1))
                wait(dve, av_done, times(g, 2, u))
                nc.vector.tensor_copy(PT[:, 3:6, :].rearrange("p a i -> p (a i)"), PSUM[:, 5, 0:384]).then_inc(pt_hi, 1)

            def normalise(g, u):
                wait(dve, av_done, times(g, 2, u + 1))
                av = PSUM[:, 0, 0:NH * 17].rearrange("p (h d) -> p h d", d=17)
                nc.vector.reciprocal(RD[:, :], av[:, :, DH]).then_inc(rden, 1)
                wait(dve, rden, times(g, 2, u + 1))
                wait(dve, ot_done, times(g, 2, u))
                r = RD[:, :].rearrange("p (h o) -> p h o", o=1).to_broadcast([128, NH, DH])
                nc.vector.tensor_tensor(OTOK[:, :].rearrange("p (h d) -> p h d", d=DH), av[:, :, 0:DH], r, ALU.mult).then_inc(o_ready, 1)

            def residual(g, u):
                wait(dve, proj_done, times(g, 2, u + 1))
                at = bass.ds(times(g, 2 * D, u * D), D)
                nc.vector.tensor_tensor(H2[:, at], PSUM[:, 1, 0:D], H[:, at], ALU.add).then_inc(h2_ready, 1)
                wait_bn(h2_ready, times(g, 2, u + 1))
                statistics(2, H2[:, at], u)
                wait_bn(stats[2], times(g, 2, u + 1))
                aggregate(2, u).then_inc(meanvar[2], 1)
                wait(dve, meanvar[2], times(g, 2, u + 1))
                add_eps(2, u, 1).then_inc(var_eps[2], 1)

            def norm2(g, u):
                wait(dve, rstd[2], times(g, 2, u + 1))
                wait(dve, t2_done, times(g, 1))
                at = bass.ds(times(g, 2 * D, u * D), D)
                nc.vector.tensor_scalar(XN2[:, u * D:(u + 1) * D], H2[:, at], mean(2, u), RS[:, 4 + u:5 + u],
                                        ALU.subtract, ALU.mult).then_inc(xn2_ready, 1)

            def ffn_out(g):
                wait(dve, f2_done, times(g, 1, 1))
                wait(dve, h2b_ready, times(g, 1, 1))
                wait(dve, y_free, times(g, 16, 16))
                nc.vector.tensor_tensor(Y, PSUM[:, 7, 0:2 * D], H2B[:, bass.ds(times(g, 2 * D), 2 * D)], ALU.add).then_inc(y_ready, 1)

            def body(g, two_ahead, ahead, out):
                minus_max(g, 0)
                if out:
                    ffn_out(g - 2)
                if two_ahead:
                    tokens_a(g + 2)
                minus_max(g, 1)
                if two_ahead:
                    tokens_b(g + 2)
                probs_hi(g, 0)
                if two_ahead:
                    tokens_c(g + 2)
                normalise(g, 0)
                probs_hi(g, 1)
                if ahead:
                    block_diagonal(g + 1, 0)
                normalise(g, 1)
                if ahead:
                    block_diagonal(g + 1, 1)
                if two_ahead:
                    tokens_d(g + 2)
                residual(g, 0)
                residual(g, 1)
                norm2(g, 0)
                norm2(g, 1)

            dve.wait_ge(ld_bc, 16)
            dve.wait_ge(ld_cst, 16)
            taps(("f3", 1))
            dve.wait_ge(acc_read, first_unit[("f3", 0)] + 2)
            tokens_a(0)
            tokens_b(0)
            tokens_c(0)
            tokens_a(1)
            tokens_d(0)
            tokens_b(1)
            tokens_c(1)
            dve.wait_ge(pads_zero, 2)
            block_diagonal(0, 0)
            block_diagonal(0, 1)
            tokens_d(1)
            dve.wait_ge(acc_read, NUNITS)
            body(0, True, True, False)
            body(1, True, True, False)
            with dve.Fori(2, NG - 2) as g:
                body(g, True, True, True)
            body(NG - 2, False, True, True)
            body(NG - 1, False, False, True)
            ffn_out(NG - 2)

            dve.wait_ge(gate_done, 1)
            lg = PSUM[0:96, 0, 0:4].rearrange("p (r n) -> p r n", r=2)

            def pairs(at):
                return GT[:, at:at + 4].rearrange("p (r n) -> p r n", r=2)

            def one(at):
                return GT[:, at:at + 2].rearrange("p (r o) -> p r o", o=1).to_broadcast([96, 2, 2])

            nc.vector.tensor_reduce(GT[:, 0:2], lg, AXX, ALU.max).then_inc(gate_dve, 1)
            dve.wait_ge(gate_dve, 1)
            nc.vector.tensor_tensor(pairs(4), lg, one(0), ALU.subtract).then_inc(gate_max, 2)
            dve.wait_ge(gate_exp, 1)
            chain = [1]

            def link(ins):
                chain[0] += 1
                ins.then_inc(gate_dve, 1)
                dve.wait_ge(gate_dve, chain[0])

            link(nc.vector.tensor_reduce(GT[:, 8:10], pairs(4), AXX, ALU.add))
            link(nc.vector.reciprocal(GT[:, 10:12], GT[:, 8:10]))
            link(nc.vector.tensor_tensor(pairs(12), pairs(4), one(10), ALU.mult))
            link(nc.vector.tensor_reduce(GT[:, 16:18], pairs(12), AXX, ALU.min))
            link(nc.vector.tensor_tensor(pairs(20), pairs(12), one(16), ALU.is_gt))
            link(nc.vector.tensor_tensor(pairs(24), pairs(20), pairs(12), ALU.mult))
            link(nc.vector.tensor_reduce(GT[:, 28:30], pairs(24), AXX, ALU.add))
            link(nc.vector.tensor_scalar(GT[:, 30:32], GT[:, 28:30], 1e-6, None, ALU.max))
            link(nc.vector.reciprocal(GT[:, 32:34], GT[:, 30:32]))
            link(nc.vector.tensor_tensor(pairs(36), pairs(24), one(32), ALU.mult))
            ffn_out(NG - 1)
            dve.wait_ge(e2_done, 2)
            dve.wait_ge(hc_loaded, 16 * NCLS)
            for r in range(2):
                cols = slice(r * D, (r + 1) * D)
                nc.vector.tensor_tensor(EU[:, cols], PSUM[0:96, 0, cols], (EB3, EB4)[r][0:96, :], ALU.add).then_inc(e_mix, 1)
                nc.vector.tensor_tensor(EU[:, 2 * D + r * D:2 * D + (r + 1) * D], PSUM[0:96, 3, cols], EBK[0:96, :], ALU.add).then_inc(e_mix, 1)
            for r in range(2):
                cols = slice(r * D, (r + 1) * D)
                dve.wait_ge(e_mix, 4)
                nc.vector.scalar_tensor_tensor(out=ER[:, cols], in0=EU[:, cols], scalar=GT[:, 36 + 2 * r:37 + 2 * r],
                                               in1=HC2[:, cols], op0=ALU.mult, op1=ALU.add).then_inc(e_mix, 1)
            for r in range(2):
                cols = slice(r * D, (r + 1) * D)
                dve.wait_ge(e_mix, 5 + r)
                nc.vector.scalar_tensor_tensor(out=ER[:, 2 * D + r * D:2 * D + (r + 1) * D], in0=EU[:, 2 * D + r * D:2 * D + (r + 1) * D],
                                               scalar=GT[:, 37 + 2 * r:38 + 2 * r], in1=ER[:, cols],
                                               op0=ALU.mult, op1=ALU.add).then_inc(e_mix, 1)

        @block.gpsimd
        def _(gp):
            gp.wait_ge(acc_done, first_unit[("e", NCH - 1)] + 3)
            gp.wait_ge(ld_vec, 16)
            gp.wait_ge(ld_cst, 16)
            for k, f in enumerate(("f1_P", "f2_P", "f3_P")):
                w = V[:, VEC[f][0]:VEC[f][0] + 9].rearrange("p (t o) -> p t o", o=1).to_broadcast([128, 9, 128])
                gp.tensor_tensor(DG[:, k, :, :], IDN.rearrange("p (o n) -> p o n", o=1).to_broadcast([128, 9, 128]), w,
                                 ALU.mult).then_inc(dg_ready, 1)
            gp.wait_ge(acc_done, first_unit[("g", 1)] + 3)
            gp.memset(mixreg[:, 0:(B + B // 2) * ROWS], 0.0).then_inc(d3_zero, 1)
            gp.wait_ge(acc_done, first_unit[("w2", 1)] + 3)
            gp.wait_ge(fused, 6)
            gp.memset(QT[:, :, :, S:ROWS], 0.0)
            gp.memset(KT2[:, :, :, S:ROWS], 0.0)
            gp.memset(P[:, :, :, S:ROWS], 0.0)
            gp.memset(HIDT[:, :, :, NMAIN:ROWS], 0.0)
            gp.memset(KV, 0.0).then_inc(consts, 1)
            gp.wait_ge(consts, 1)
            for r in range(2):
                gp.memset(KV[ROWS * r:ROWS * r + ROWS, :, r:NH:2, DH:DH + 1], 1.0).then_inc(pads_zero, 1)
                gp.wait_ge(pads_zero, r + 1)

            def power(i, at, n):
                return gp.tensor_tensor(RS[:, at:at + n], VE[:, 2 * i + at % 2:2 * i + at % 2 + n],
                                        NEG[:, :].to_broadcast([128, n]), ALU.pow)

            def norms(g):
                wait(gp, var_eps[0], times(g, 1, 1))
                power(0, 0, 2).then_inc(rstd[0], 1)
                wait(gp, rstd[0], times(g, 1, 1))
                gp.tensor_tensor(RS[:, 6:8], RS[:, 0:2], PMASK.to_broadcast([128, 2]), ALU.mult).then_inc(rstd_masked, 1)
                wait(gp, var_eps[1], times(g, 1, 1))
                power(1, 2, 2).then_inc(rstd[1], 1)

            def norm2(g):
                for u in range(2):
                    wait(gp, var_eps[2], times(g, 2, u + 1))
                    gp.tensor_tensor(RS[:, 4 + u:5 + u], VE[:, 4 + u:5 + u], NEG[:, :], ALU.pow).then_inc(rstd[2], 1)
                at = bass.ds(times(g, 2 * D), 2 * D)
                gp.tensor_tensor(H2B[:, at].rearrange("p (u c) -> p u c", u=2), H2[:, at].rearrange("p (u c) -> p u c", u=2),
                                 MB2.rearrange("p (o c) -> p o c", o=1).to_broadcast([128, 2, D]), ALU.add).then_inc(h2b_ready, 1)

            def class_tokens(g):
                wait(gp, x2_ready, times(g, 1, 1))
                x2 = X2T[:, :].rearrange("p (k u e j) -> p k u e j", k=2, u=2, e=2)
                for k in range(2):
                    for r in range(2):
                        for e in range(2):
                            dst = TOKv[:, k, r, :, bass.ds(times(g, 2, 16 * e), 2)]
                            gp.tensor_copy(dst[:, 1:3, :], x2[:, k, :, e, NMAIN + r:NMAIN + 4:2].rearrange("p u a -> p a u"))
                            last = gp.tensor_copy(dst[:, 0, :], x2[:, k, :, e, NTOK + r])
                last.then_inc(tok_ready, 1)

            gp.wait_ge(ld_cst, 16)
            gp.wait_ge(ld_bc, 16)
            gp.wait_ge(gate_step, 6)
            norms(0)
            norms(1)

            def body(g, ffn, two_ahead):
                if ffn:
                    class_tokens(g - 1)
                if two_ahead:
                    norms(g + 2)
                norm2(g)

            body(0, False, True)
            with gp.Fori(1, NG - 2) as g:
                body(g, True, True)
            body(NG - 2, True, False)
            body(NG - 1, True, False)
            class_tokens(NG - 1)


def _haar():
    y, x = np.meshgrid(np.arange(PATCH), np.arange(PATCH), indexing="ij")
    m = np.ones((PIX, PATCH, PATCH), np.float32)
    for band in range(PIX):
        for level in range(4):
            d = (band >> (2 * (3 - level))) & 3
            if d & 2:
                m[band] *= 1 - 2 * ((x >> level) & 1)
            if d & 1:
                m[band] *= 1 - 2 * ((y >> level) & 1)
    return (m / 16.0).reshape(PIX, PIX).astype(np.float32)


def kernel(**inputs):
    import concourse.bacc as bacc
    from concourse.bass_utils import run_bass_kernel_spmd as run

    a = {k: np.asarray(w) for k, w in inputs.items()}
    t = {k[len("L0_tok_"):]: w for k, w in a.items() if k.startswith("L0_tok_")}
    f = {k[len("L0_ffn_"):]: w for k, w in a.items() if k.startswith("L0_ffn_")}
    z = np.zeros
    f32 = np.float32

    def rows(m, k):
        return m.reshape(k, m.shape[0] // k, -1).transpose(1, 0, 2)

    x = a["x"].reshape(NCH, CI, CIN, G, PATCH, G, PATCH).transpose(2, 4, 6, 0, 3, 5, 1)
    x = x.reshape(KC, 128, NCH, CT).transpose(1, 2, 0, 3)
    plw = rows(t["pl_w"].reshape(D, KPIX).T, KC)
    w1k = t["pg_w1"].reshape(D, PIX, CIN).transpose(1, 2, 0).reshape(2, 128, CIN, D).transpose(1, 0, 2, 3)
    had = rows(_haar(), 2)
    blocks = []
    for name in ("pl_pw", "pg_pw", "pg_w2", "f1_pw", "f2_pw", "f3_pw"):
        w = t[name].reshape(D, D).T
        bd = z((128, 128), f32)
        bd[:DB, :DB] = w[DA:, DA:]
        bd[DB:, DB:] = w[DA:, DA:]
        blocks += [w[:DA], np.concatenate([w[DA:], w[DA:]]), bd]
    pww = np.concatenate(blocks, 1)

    def part_a(w):
        return w.reshape(D, -1)[:DA]

    def part_p(w):
        return np.concatenate([w.reshape(D, -1)[DA:]] * 2)

    def mixed(p, q):
        return np.concatenate([p.reshape(D, -1)[DA:], q.reshape(D, -1)[DA:]])

    vec = np.concatenate([
        part_a(t["pl_b"]), part_a(t["pg_b1"]), mixed(t["pl_b"], t["pg_b1"]), part_a(t["alpha"]), part_p(t["alpha"]),
        part_a(t["pl_pwb"]), part_p(t["pl_pwb"]), part_a(t["pg_pwb"]), part_p(t["pg_pwb"]),
        part_a(t["pg_b2"]), part_p(t["pg_b2"]), part_a(t["f1_pwb"]), part_p(t["f1_pwb"]),
        part_a(t["f2_pwb"]), part_p(t["f2_pwb"]),
        part_a(t["pl_dw"]), part_a(t["pg_dw"]), mixed(t["pl_dw"], t["pg_dw"]),
        part_a(t["f1_dw"]), part_p(t["f1_dw"]), part_a(t["f2_dw"]), part_p(t["f2_dw"]),
        part_a(t["f3_dw"]), part_p(t["f3_dw"]),
        f["moe0_b1"].reshape(HC, 128).T, f["A1_b"].reshape(NEXP * HC, 128).T], 1)

    def wide(row, n=128):
        return np.broadcast_to(row.reshape(1, D), (n, D))

    lnb = z((128, D), f32)
    for e in range(2):
        lnb[ROWS * e:ROWS * e + NTOK] = wide(t["ln_b"], NTOK)
        lnb[ROWS * e + NTOK] = a["cls_tok"].reshape(D)
        lnb[ROWS * e + NTOK + 1] = t["cls"].reshape(D)
    ebk = np.concatenate([wide(f["A2_b"][k], B) for k in range(3)] + [z((128 - 3 * B, D), f32)])
    bcw = np.concatenate([wide(t["f3_pwb"]), wide(t["ln_g"]), lnb, wide(f["moe0_b2"]), wide(f["A2_b"][3]),
                          wide(f["A2_b"][4]), ebk], 1)
    cst = z((128, 128 + HP + 1), f32)
    cst[:, :128] = np.eye(128)
    for h in range(HP):
        cst[h * DH:(h + 1) * DH, 128 + h] = 1.0
    for e in range(2):
        cst[ROWS * e:ROWS * e + NTOK, 128 + HP] = 1.0
    wqk = rows(a["L0_attn_w_qkv"][:, :2 * D], 2)
    wout = rows(a["L0_attn_w_out"], 2)
    mw1 = rows(f["moe0_W1"], 2)
    mw2 = rows(f["moe0_W2"], HC)
    a1 = f["A1_W"].reshape(NEXP, 2, HD, HID).transpose(2, 1, 0, 3)
    a2 = f["A2_W"].reshape(NEXP, HC, 128, D).transpose(2, 1, 0, 3)
    gw = f["G_W"].reshape(3, 2, 2, HD, 2).transpose(3, 2, 1, 0, 4)

    arrays = {
        "x": x, "plw": plw, "w1k": w1k, "had": had, "pww": pww, "vec": vec, "bcw": bcw, "cst": cst,
        "wqk": wqk.reshape(HD, -1), "wout": wout.reshape(HD, -1), "mw1": mw1.reshape(HD, -1), "mw2": mw2.reshape(128, -1),
        "a1": a1, "a2": a2.reshape(128, -1), "gw": gw.reshape(HD, -1)}
    arrays = {k: np.ascontiguousarray(w) for k, w in arrays.items()}

    nc = bacc.Bacc("TRN2", target_bir_lowering=False, num_devices=1)
    args = [nc.dram_tensor(k, w.shape, mybir.dt.from_np(w.dtype), kind="ExternalInput").ap() for k, w in arrays.items()]
    args.append(nc.dram_tensor("out_main", (128, NT * D), F32, kind="ExternalOutput").ap())
    args.append(nc.dram_tensor("out_cls", (96, 2 * D), F32, kind="ExternalOutput").ap())
    args.append(nc.dram_tensor("h2x", (NCLS, 2, NT, D), F32, kind="Internal").ap())
    vit_tower(nc, *args)
    r = run(nc, [arrays], core_ids=[0]).results[0]
    main = np.asarray(r["out_main"]).reshape(2, ROWS, NT, D)[:, :NMAIN].transpose(2, 0, 1, 3).reshape(B, NMAIN, D)
    cls = np.asarray(r["out_cls"]).reshape(3, 2, NT, 2, D).transpose(2, 1, 0, 3, 4).reshape(B, NCLS, D)
    return np.concatenate([cls, main], 1)
```

```python
from contextlib import ExitStack

import numpy as np

import concourse.bass as bass
from concourse import mybir
from concourse.alu_op_type import AluOpType as ALU

F32 = mybir.dt.float32
ACT = mybir.ActivationFunctionType
AXX = mybir.AxisListType.X

B, CIN, IMG, PATCH, D = 32, 3, 112, 16, 192
G = IMG // PATCH
NTOK = G * G
S = NTOK + 2
PIX = PATCH * PATCH
KPIX = CIN * PIX
KC = KPIX // 128
DA, DB = 128, D - 128
NCH, CI = 4, 8
CT = NTOK * CI
NPAIR = NCH // 2
HD = D // 2
NH, DH = 12, 16
HP = NH // 2
QK_PARTS = ((DA, DA // DH, 0), (DB, DB // DH, DA // DH))
HMAX = DA // DH
NG, GI = 8, 4
NT = B // 2
ROWS = 64
NMAIN = S - 6
HID = 768
HC = HID // 128
NCLS, NEXP = 6, 5
SCALE = float(D) ** -0.5
EPS = 1e-5

VEC = {}
for _name in ("bias_loc", "bias_g", "bias_mixed", "alpha_A", "alpha_P", "plb_A", "plb_P", "pgb_A", "pgb_P",
              "b2_A", "b2_P", "f1b_A", "f1b_P", "f2b_A", "f2b_P"):
    VEC[_name] = (len(VEC), 1)
_at = len(VEC)
for _name in ("dw_loc", "dw_g", "dw_mixed", "f1_A", "f1_P", "f2_A", "f2_P", "f3_A", "f3_P"):
    VEC[_name] = (_at, 9)
    _at += 9
VEC["moe_b1"] = (_at, HC)
VEC["exp_b1"] = (_at + HC, NEXP * HC)
NVEC = _at + HC + NEXP * HC
LAYERS = ("loc", "g", "w2", "f1", "f2", "f3")
LW = 2 * D + 128


def vit_tower(nc, x, plw, w1k, had, pww, vec, bcw, cst, wqk, wout, mw1, mw2, a1, a2, gw, out_main, out_cls, h2x):
    ctx = ExitStack()
    with ctx:
        def sb(name, cols, parts=128):
            return ctx.enter_context(nc.sbuf_tensor(name, [parts, cols], F32))

        def sem(name):
            return ctx.enter_context(nc.semaphore(name))

        xreg = sb("xreg", NCH * KC * CT)
        wereg = sb("wereg", GI * NH * S)
        hadreg = sb("hadreg", CIN * 2 * D + 2 * PIX)
        gelreg = sb("gelreg", 2 * NCH * CT)
        dwreg = sb("dwreg", 2 * NCH * CT)
        mixreg = sb("mixreg", 2 * NCH * CT)
        locreg = sb("locreg", 12 * CT)
        g2reg = sb("g2reg", 6 * CT)
        cureg = sb("cureg", 6 * CT)
        tapreg = sb("tapreg", 6 * CT)
        A2 = sb("A2", HC * NEXP * D)
        MW1 = sb("MW1", 2 * HID, HD)
        MW2 = sb("MW2", HC * D)
        WQK = sb("WQK", 2 * 2 * D, HD)
        WOUT = sb("WOUT", 2 * D, HD)
        PW = sb("PW", len(LAYERS) * LW)
        V = sb("V", NVEC)
        BC = sb("BC", 7 * D)
        CST = sb("CST", 128 + HMAX + 1)
        GW = sb("GW", 2 * NCLS * 2, HD)

        X = xreg[:, :].rearrange("p (c k n) -> p c k n", c=NCH, k=KC)
        WE = wereg[:, 0:KC * 2 * D].rearrange("p (k n) -> p k n", k=KC)
        W1K = hadreg[:, 0:CIN * 2 * D].rearrange("p (h c o) -> p h c o", h=2, c=CIN)
        HAD = hadreg[:, CIN * 2 * D:CIN * 2 * D + 2 * PIX].rearrange("p (h x) -> p h x", h=2)
        GA = gelreg[:, :].rearrange("p (b c n) -> p b c n", b=2, c=NCH)
        DWA = dwreg[:, :].rearrange("p (b c n) -> p b c n", b=2, c=NCH)
        GM = mixreg[:, 0:NCH * CT].rearrange("p (c n) -> p c n", c=NCH)
        DWM = mixreg[:, NCH * CT:2 * NCH * CT].rearrange("p (c n) -> p c n", c=NCH)

        def six(reg, i=0):
            return reg[:, i * 6 * CT:(i + 1) * 6 * CT].rearrange("p (u n) -> p u n", u=6)

        LOC, LM = six(locreg, 0), six(locreg, 1)
        G2, CUR, TAP = six(g2reg), six(cureg), six(tapreg)
        D3A = mixreg[:, 0:B * ROWS]
        D3P = mixreg[:, B * ROWS:B * ROWS + B // 2 * ROWS]
        DG = A2[:, 0:3 * 9 * 128].rearrange("p (f t n) -> p f t n", f=3, t=9)
        A1 = xreg[0:HD, 0:2 * NEXP * HID].rearrange("p (k e n) -> p k e n", k=2, e=NEXP)
        o = 2 * NEXP * HID
        T3B, XN, XN2, Y = (xreg[:, o + i * 2 * D:o + (i + 1) * 2 * D] for i in range(4))
        BD = [wereg[0:n, GI * S * h0:GI * S * (h0 + nh)].rearrange("p (i h j) -> p i h j", i=GI, h=nh)
              for n, nh, h0 in QK_PARTS]
        QT = hadreg[:, 0:2 * GI * ROWS].rearrange("p (k i j) -> p k i j", k=2, i=GI)
        KT2 = hadreg[:, 2 * GI * ROWS:6 * GI * ROWS].rearrange("p (m d j) -> p m d j", m=2 * GI, d=2)
        T3 = gelreg[:, 0:NT * D]
        H = dwreg[:, 0:NT * D]
        H2 = mixreg[:, 0:NT * D]
        H2B = H
        HE = [g2reg[:, i * HC * 2 * HD:(i + 1) * HC * 2 * HD].rearrange("p (c r n) -> p c r n", c=HC, r=2)
              for i in range(2)]
        low = locreg[:, 6 * CT:12 * CT]
        HIDT = low[:, 0:HC * GI * ROWS].rearrange("p (c i j) -> p c i j", c=HC, i=GI)
        KV = low[:, HC * GI * ROWS:HC * GI * ROWS + GI * 2 * HP * 17].rearrange("p (i h d) -> p i h d", i=GI, d=17)
        P = g2reg[:, 0:2 * NH * ROWS].rearrange("p (u h j) -> p u h j", u=2, h=NH)
        PT = g2reg[:, 2 * NH * ROWS:2 * NH * ROWS + HP * 128].rearrange("p (a i) -> p a i", a=HP)
        XT = sb("XT", 2 * GI * S, HD)
        X2T = sb("X2T", 2 * GI * ROWS, HD)
        TOK = sb("TOK", 2 * 2 * 3 * B, HD)
        OTOK = sb("OTOK", D)
        OT = sb("OT", 2 * 128, HD)
        HC2 = sb("HC2", 2 * D, 96)
        EU = sb("EU", 4 * D, 96)
        ER = sb("ER", 4 * D, 96)
        GT = sb("GT", 64, 96)
        ST = sb("ST", 3 * 2 * 6)
        MV = sb("MV", 3 * 2 * 2)
        VE = sb("VE", 3 * 2)
        RS = sb("RS", 4 * 2)
        MX = sb("MX", 2 * NH)
        RD = sb("RD", NH)
        TH = sb("TH", 10)
        NEG = sb("NEG", 1)
        NIL = sb("NIL", 3)
        TOKv = TOK[:, :].rearrange("p (k r a n) -> p k r a n", k=2, r=2, a=3)
        IDN = CST[:, 0:128]
        HMASK = CST[:, 128:128 + HMAX]
        PMASK = CST[:, 128 + HMAX:128 + HMAX + 1]
        BF3, LNG, LNB, MB2, EB3, EB4, EBK = (BC[:, i * D:(i + 1) * D] for i in range(7))

        def v(name, i=0):
            return V[:, VEC[name][0] + i:VEC[name][0] + i + 1]

        PSUM = ctx.enter_context(nc.psum_tensor("PSUM", [128, 8, 512], F32))

        ld_haar, ld_third, ld_plw, ld_plw_b, ld_x_first, ld_x, ld_vec, ld_cst, ld_bc, ld_pw = (
            sem("ld_haar"), sem("ld_third"), sem("ld_plw"), sem("ld_plw_b"), sem("ld_x_first"), [sem(f"ld_x{c}") for c in range(NCH)], sem("ld_vec"), sem("ld_cst"),
            sem("ld_bc"), sem("ld_pw"))
        ld_attn, ld_moe, ld_a1, ld_a2, ld_gw = sem("ld_attn"), sem("ld_moe"), sem("ld_a1"), sem("ld_a2"), sem("ld_gw")
        acc_done = sem("acc_done")
        acc_read = sem("acc_read")
        centre = sem("centre")
        tap = sem("tap")
        fused = sem("fused")
        tanh_done, gate_step = sem("tanh_done"), sem("gate_step")
        d3_zero, d3_ready = sem("d3_zero"), sem("d3_ready")
        consts = sem("consts")
        warm = sem("warm")
        dg_ready = sem("dg_ready")
        passed = sem("passed")
        pads_zero = sem("pads_zero")
        biased, h_ready, norm3 = sem("biased"), sem("h_ready"), sem("norm3")
        stats = [sem(f"stats{i}") for i in range(3)]
        meanvar = [sem(f"meanvar{i}") for i in range(3)]
        var_eps = [sem(f"var_eps{i}") for i in range(3)]
        rstd = [sem(f"rstd{i}") for i in range(3)]
        rstd_masked = sem("rstd_masked")
        xn_ready, xn2_ready = sem("xn_ready"), sem("xn2_ready")
        t1_done, xt_ready, q_done, q_ready, k_done, k_ready = (
            sem("t1_done"), sem("xt_ready"), sem("q_done"), sem("q_ready"), sem("k_done"), sem("k_ready"))
        bd_ready, kt_done, kv_ready, s_done, smax, d_ready, p_ready = (
            sem("bd_ready"), sem("kt_done"), sem("kv_ready"), sem("s_done"), sem("smax"), sem("d_ready"), sem("p_ready"))
        pt_done, pt_lo, pt_hi, av_done, rden, o_ready = (
            sem("pt_done"), sem("pt_lo"), sem("pt_hi"), sem("av_done"), sem("rden"), sem("o_ready"))
        ot_done, ot_ready, proj_done, h2_ready, h2b_ready = (
            sem("ot_done"), sem("ot_ready"), sem("proj_done"), sem("h2_ready"), sem("h2b_ready"))
        t2_done, x2_ready, tok_ready = sem("t2_done"), sem("x2_ready"), sem("tok_ready")
        f1_done, gelu_done, f2_done, y_ready, y_free = (
            sem("f1_done"), sem("gelu_done"), sem("f2_done"), sem("y_ready"), sem("y_free"))
        h2x_stored, hc_loaded, gate_done, gate_max, gate_exp, gate_dve = (
            sem("h2x_stored"), sem("hc_loaded"), sem("gate_done"), sem("gate_max"), sem("gate_exp"), sem("gate_dve"))
        e1_done, e1_read, e2_done, e_mix, cls_stored = (
            sem("e1_done"), sem("e1_read"), sem("e2_done"), sem("e_mix"), sem("cls_stored"))
        block = ctx.enter_context(nc.Block())

        STEPS = [("w", 0), ("e", 0), ("e", 1), ("e", 2), ("e", 3), ("g", 0), ("loc", 0), ("w2", 0),
                 ("g", 1), ("loc", 1), ("w2", 1), ("f1", 0), ("p1", 1), ("f1", 1), ("p2", 0), ("f2", 0),
                 ("p2", 1), ("f2", 1), ("p3", 0), ("f3", 0), ("p3", 1), ("f3", 1)]
        HAAR_UNITS = ((0, 0, 2), (1, 0, 2), (0, 2, 1), (1, 2, 1))
        UNITS = {"w": 4, "e": 3, "loc": 3, "g": 3, "w2": 3, "f1": 3, "f2": 3, "f3": 4, "p1": 1, "p2": 1, "p3": 1}
        first_unit, _n = {}, 0
        for st in STEPS:
            first_unit[st] = _n
            _n += UNITS[st[0]]
        NUNITS = _n
        LAST = first_unit[STEPS[-1]]
        LAST_BANKS = (6, 7, 6, 7)
        DW = [("dw", 0), ("dw", 1), ("dw", 2), ("dw", 3), ("f1", 0), ("f1", 1), ("f2", 0), ("f2", 1), ("f3", 0), ("f3", 1)]
        dw_at = {b: i for i, b in enumerate(DW)}

        def on_pe(b):
            return ("p" + b[0][1:], b[1]) in STEPS

        def batch_units(b):
            kind, i = b
            if kind == "dw":
                return [(GA[:, 0, i, :], DWA[:, 0, i, :], "dw_loc"), (GA[:, 1, i, :], DWA[:, 1, i, :], "dw_g"),
                        (GM[:, i, :], DWM[:, i, :], "dw_mixed")]
            units = (2 * i, 2 * i + 1) if on_pe(b) else (2 * i, 2 * i + 1, 4 + i)
            return [(CUR[:, u, :], TAP[:, u, :], kind + ("_P" if u >= 4 else "_A")) for u in units]

        def centres_done(b):
            return sum(len(batch_units(c)) for c in DW[:dw_at[b] + 1])

        def taps_done(b):
            return 8 * centres_done(b)

        SHIFTS = [(dy, dx) for dy in (-1, 0, 1) for dx in (-1, 0, 1) if (dy, dx) != (0, 0)]

        def shifted(ap, dy, dx, inp):
            ys = slice(max(0, dy), G + min(0, dy)) if inp else slice(max(0, -dy), G - max(0, dy))
            lo = max(0, dx) if inp else max(0, -dx)
            n = G - abs(dx)
            return ap.rearrange("p (y x) -> p y x", y=G)[:, ys, lo * CI:(lo + n) * CI]

        nfused = {("w2", 0): 3, ("w2", 1): 6, ("f2", 0): 9, ("f2", 1): 12}

        def units_of_pair(i):
            return (2 * i, 2 * i + 1, 4 + i)

        def bank_of(n):
            return n % 8 if n < LAST else LAST_BANKS[n - LAST]

        def bank(n, cols, parts=slice(0, 128)):
            return PSUM[parts, bank_of(n), 0:cols]

        def times(g, k, c=0):
            return k * g + c

        def wait(eng, s, value):
            if not isinstance(value, int) or value > 0:
                eng.wait_ge(s, value)

        @block.sync
        def _(sp):
            sp.dma_start(HAD, had).then_inc(ld_haar, 16)
            sp.dma_start(W1K[:, :, 0:2, :], w1k[:, :, 0:2, :]).then_inc(ld_haar, 16)
            sp.dma_start(W1K[:, :, 2:3, :], w1k[:, :, 2:3, :]).then_inc(ld_third, 16)
            sp.dma_start(WE[:, :, 0:DA], plw[:, :, 0:DA]).then_inc(ld_plw, 16)
            sp.dma_start(X[:, 0, 0:KC // 2, :], x[:, 0, 0:KC // 2, :]).then_inc(ld_x_first, 16)
            sp.dma_start(X[:, 0, KC // 2:, :], x[:, 0, KC // 2:, :]).then_inc(ld_x[0], 16)
            sp.dma_start(WE[:, :, 2 * DA:2 * DA + DB], plw[:, :, DA:D]).then_inc(ld_plw_b, 16)
            sp.dma_start(V[:, :], vec).then_inc(ld_vec, 16)
            sp.dma_start(CST[:, :], cst).then_inc(ld_cst, 16)
            for c in range(1, NCH):
                sp.dma_start(X[:, c, :, :], x[:, c, :, :]).then_inc(ld_x[c], 16)
            sp.dma_start(PW[:, :], pww).then_inc(ld_pw, 16)
            sp.dma_start(BC[:, :], bcw).then_inc(ld_bc, 16)
            sp.dma_start(WQK[:, :], wqk).then_inc(ld_attn, 16)
            sp.dma_start(WOUT[:, :], wout).then_inc(ld_attn, 16)
            sp.dma_start(MW1[:, :], mw1).then_inc(ld_moe, 16)
            sp.dma_start(MW2[:, :], mw2).then_inc(ld_moe, 16)
            sp.dma_start(GW[:, :], gw).then_inc(ld_gw, 16)
            sp.wait_ge(acc_done, first_unit[("e", NCH - 1)] + 3)
            sp.dma_start(A1[:, :, :, :], a1).then_inc(ld_a1, 16)
            sp.wait_ge(acc_done, first_unit[("p3", NPAIR - 1)] + 1)
            sp.dma_start(A2[:, :], a2).then_inc(ld_a2, 16)

            def store(g):
                wait(sp, y_ready, times(g, 1, 1))
                sp.dma_start(out_main[:, bass.ds(times(g, 2 * D), 2 * D)], Y).then_inc(y_free, 16)

            with sp.Fori(0, NG - 1) as g:
                store(g)
            sp.wait_ge(h2_ready, NT)
            for e in range(2):
                sp.dma_start(h2x[:, e, :, :], H2[ROWS * e + NMAIN:ROWS * e + S, :].rearrange("p (t c) -> p t c", c=D)).then_inc(h2x_stored, 16)
            sp.wait_ge(h2x_stored, 32)
            for a in range(3):
                for r in range(2):
                    row = (2 * a + r - 2) % NCLS
                    sp.dma_start(HC2[B * a:B * a + B, r * D:(r + 1) * D], h2x[row, :, :, :].rearrange("e t c -> (e t) c")).then_inc(hc_loaded, 16)
            store(NG - 1)
            sp.wait_ge(e_mix, 8)
            sp.dma_start(out_cls, ER[:, 2 * D:4 * D]).then_inc(cls_stored, 16)
            sp.wait_ge(cls_stored, 16)
            sp.wait_ge(y_free, 16 * (NG + 1))

        @block.tensor
        def _(pe):
            def mm(out, lhsT, rhs, start, stop):
                return nc.tensor.matmul(out, lhsT, rhs, start=start, stop=stop)

            def free_bank(n):
                if 8 <= n < LAST:
                    pe.wait_ge(acc_read, n - 7)
                elif n >= LAST + 2:
                    pe.wait_ge(acc_read, n - 1)

            def haar_weights():
                for j, (m, c0, nco) in enumerate(HAAR_UNITS):
                    if j == 0:
                        pe.wait_ge(ld_haar, 32)
                    elif j == 2:
                        pe.wait_ge(ld_third, 16)
                    for h in range(2):
                        last = mm(bank(j, nco * D), HAD[:, h, m * 128:(m + 1) * 128],
                                  W1K[:, h, c0:c0 + nco, :], h == 0, h == 1)
                    last.then_inc(acc_done, 1)

            def embed(c):
                n = first_unit[("e", c)]
                if c == 0:
                    pe.wait_ge(ld_plw, 16)
                    pe.wait_ge(ld_x_first, 16)
                else:
                    pe.wait_ge(ld_x[c], 16)
                for j, w0 in enumerate((0, DA, 2 * DA)):
                    if c == 0 and j == 1:
                        pe.wait_ge(acc_read, 4)
                    if c == 0 and j == 2:
                        pe.wait_ge(ld_plw_b, 16)
                    free_bank(n + j)
                    for k in range(KC):
                        if c == 0 and j == 0 and k == KC // 2:
                            pe.wait_ge(ld_x[0], 16)
                        last = mm(bank(n + j, CT), WE[:, k, w0:w0 + 128], X[:, c, k, :], k == 0, k == KC - 1)
                    last.then_inc(acc_done, 1)

            def pointwise(layer, i):
                w = LAYERS.index(layer) * LW
                wa, wb, wd = PW[:, w:w + D], PW[:, w + D:w + 2 * D], PW[:, w + 2 * D:w + 2 * D + 128]
                n = first_unit[(layer, i)]
                if layer in ("loc", "g"):
                    pe.wait_ge(tap, taps_done(("dw", 2 * i + 1)))
                    b = ("loc", "g").index(layer)
                    half = slice(DB * b, DB * b + DB)
                    a_in = [DWA[:, b, 2 * i + j, :] for j in range(2)]
                    b_in = [(half, DWM[half, 2 * i + j, :]) for j in range(2)]
                else:
                    if layer == "w2":
                        pe.wait_ge(acc_read, first_unit[("g", i)] + 3)
                        src = G2
                    else:
                        pe.wait_ge(tap, taps_done((layer, i)))
                        src = TAP
                    a_in = [src[:, 2 * i + j, :] for j in range(2)]
                    b_in = [(slice(DB * j, DB * j + DB), src[DB * j:DB * j + DB, 4 + i, :]) for j in range(2)]
                outs = [PSUM[DB * j:DB * j + DB, bank_of(n + 2), 0:CT] for j in range(2)]
                for j in range(2):
                    free_bank(n + j)
                    mm(bank(n + j, CT), wa[:, 0:DA], a_in[j], True, False)
                free_bank(n + 2)
                for j in range(2):
                    mm(outs[j], wa[:, DA:D], a_in[j], True, False)
                if layer[0] == "f" and on_pe((layer, i)):
                    pe.wait_ge(acc_read, first_unit[("p" + layer[1], i)] + 1)
                for j in range(2):
                    half, rhs = b_in[j]
                    mm(bank(n + j, CT), wb[half, 0:DA], rhs, False, True).then_inc(acc_done, 1)
                if layer in ("loc", "g"):
                    for j in range(2):
                        half, rhs = b_in[j]
                        last = mm(outs[j], wb[half, DA:D], rhs, False, True)
                else:
                    last = mm(bank(n + 2, CT), wd, src[:, 4 + i, :], False, True)
                last.then_inc(acc_done, 1)

            def depthwise(layer, i):
                n = first_unit[("p%d" % layer, i)]
                free_bank(n)
                pe.wait_ge(dg_ready, layer)
                if layer == 2:
                    pe.wait_ge(acc_read, first_unit[("f1", i)] + 3)
                else:
                    pe.wait_ge(fused, nfused[("w2" if layer == 1 else "f2", i)])
                src, acc = CUR[:, 4 + i, :], bank(n, CT)
                mm(acc, DG[:, layer - 1, 4, :], src, True, False)
                for j, (dy, dx) in enumerate(SHIFTS):
                    last = mm(shifted(acc, dy, dx, False), DG[:, layer - 1, (dy + 1) * 3 + dx + 1, :],
                              shifted(src, dy, dx, True), False, j == len(SHIFTS) - 1)
                last.then_inc(acc_done, 1)

            def f3_tiles(i, q, tiles=(0, 1)):
                w = LAYERS.index("f3") * LW
                wa, wb = PW[:, w:w + D], PW[:, w + D:w + 2 * D]
                n = first_unit[("f3", i)]
                if 0 in tiles:
                    free_bank(n + q)
                pe.wait_ge(d3_ready, 2 * i + q // 2 + 1)
                pe.wait_ge(acc_read, first_unit[("p3", i)] + 1)
                for u in tiles:
                    t = 8 * i + 2 * q + u
                    half = slice(DB * (q // 2), DB * (q // 2) + DB)
                    at = (8 * i + 2 * (t % 4)) * ROWS
                    out = PSUM[:, bank_of(n + q), u * D:(u + 1) * D]
                    mm(out, D3A[:, 2 * t * ROWS:(2 * t + 2) * ROWS], wa, True, False)
                    last = mm(out, D3P[half, at:at + 2 * ROWS], wb[half, :], False, True)
                if 1 in tiles:
                    last.then_inc(acc_done, 1)

            def step(kind, i):
                if kind == "w":
                    haar_weights()
                elif kind == "e":
                    embed(i)
                elif kind == "f3":
                    for q in range(4):
                        f3_tiles(i, q)
                elif kind[0] == "p":
                    depthwise(int(kind[1]), i)
                else:
                    if (kind, i) == ("g", 0):
                        pe.wait_ge(ld_pw, 16)
                    pointwise(kind, i)

            pe.wait_ge(warm, 1)
            for _ in range(3):
                mm(PSUM[:, 7, 0:256], cureg[:, 0:128], cureg[:, 0:256], True, True)
            for st in STEPS[:-1]:
                step(*st)

            def halves(n, cols):
                return PSUM[0:HD, n, 0:2 * cols].rearrange("p (k n) -> p k n", k=2)

            def transpose_in(src, n):
                out = halves(n, 2 * 128)
                for u in range(2):
                    for k in range(2):
                        last = nc.tensor.transpose(out[:, k, u * 128:(u + 1) * 128],
                                                   src[:, u * D + k * HD:u * D + (k + 1) * HD], IDN)
                return last

            def t1(g):
                wait(pe, xn_ready, times(g, 2, 2))
                if not isinstance(g, int) or g > 1:
                    wait(pe, h2_ready, times(g, 2, -2))
                transpose_in(XN, 1).then_inc(t1_done, 1)

            def t2(g, ahead):
                wait(pe, xn2_ready, times(g, 2, 2))
                if ahead:
                    wait(pe, k_ready, times(g, 1, 3))
                transpose_in(XN2, 1).then_inc(t2_done, 1)

            def q_or_k(g, which):
                wait(pe, xt_ready, times(g, 1, 1))
                for m, tile in enumerate(((0, 2), (1,))[which]):
                    for k in range(2):
                        w = k * 2 * D + tile * 128
                        last = mm(PSUM[:, which, m * GI * S:(m + 1) * GI * S], WQK[:, w:w + 128],
                                  XT[:, k * GI * S:(k + 1) * GI * S], k == 0, k == 1)
                last.then_inc((q_done, k_done)[which], 1)

            def kt(g):
                wait(pe, k_ready, times(g, 1, 1))
                wait(pe, q_ready, times(g, 1, 1))
                wait(pe, pt_lo, times(g, 2))
                wait(pe, pt_hi, times(g, 2))
                for n in range(2):
                    for i in range(2):
                        for k, (parts, _, h0) in enumerate(QK_PARTS):
                            at = i * D + h0 * DH
                            last = nc.tensor.transpose(PSUM[:, 4 + n, at:at + parts],
                                                       KT2[0:parts, k * GI + 2 * n + i, :, :], IDN[0:parts, 0:parts])
                    last.then_inc(kt_done, 1)

            def scores(g, u):
                wait(pe, d_ready, times(g, 2, u))
                if u == 0:
                    wait(pe, bd_ready, times(g, 1, 1))
                for k, (parts, heads, _) in enumerate(QK_PARTS):
                    for e in range(2):
                        last = mm(PSUM[ROWS * e:ROWS * e + ROWS, 2 + k, 0:heads * S], QT[0:parts, k, 2 * u + e, :],
                                  BD[k][:, 2 * u + e, :, :], True, True)
                last.then_inc(s_done, 1)

            def transpose_probs(g, u):
                wait(pe, p_ready, times(g, 2, u + 1))
                if u == 0:
                    wait(pe, kv_ready, times(g, 2, 2))
                else:
                    wait(pe, pt_lo, times(g, 2, 1))
                    wait(pe, pt_hi, times(g, 2, 1))
                for a in range(HP):
                    last = nc.tensor.transpose(PSUM[:, 4 + a // 3, (a % 3) * 128:(a % 3 + 1) * 128],
                                               P[:, u, 2 * a:2 * a + 2, :], IDN)
                last.then_inc(pt_done, 1)

            def attend(g, u, ahead):
                wait(pe, pt_lo, times(g, 2, u + 1))
                wait(pe, pt_hi, times(g, 2, u + 1))
                if u == 0 and ahead:
                    wait(pe, q_ready, times(g, 1, 2))
                elif u == 0:
                    wait(pe, ot_ready, times(g, 2))
                else:
                    wait(pe, o_ready, times(g, 2, 1))
                for a in range(HP):
                    for e in range(2):
                        last = mm(PSUM[ROWS * e:ROWS * e + ROWS, 0, a * 34:(a + 1) * 34],
                                  PT[:, a, ROWS * e:ROWS * e + ROWS], KV[:, 2 * u + e, 2 * a:2 * a + 2, :], True, True)
                last.then_inc(av_done, 1)

            def transpose_out(g, u, ffn):
                wait(pe, o_ready, times(g, 2, u + 1))
                if u == 0 and ffn:
                    wait(pe, x2_ready, times(g, 1))
                elif u == 0:
                    wait(pe, k_ready, times(g, 1, 2))
                n = 1 - u
                for k in range(2):
                    last = nc.tensor.transpose(PSUM[0:HD, n, k * 128:(k + 1) * 128], OTOK[:, k * HD:(k + 1) * HD], IDN)
                last.then_inc(ot_done, 1)

            def project(g, u):
                wait(pe, ot_ready, times(g, 2, u + 1))
                if u == 1:
                    wait(pe, h2_ready, times(g, 2, 1))
                for k in range(2):
                    last = mm(PSUM[:, 1, 0:D], OT[:, k * 128:(k + 1) * 128], WOUT[:, k * D:(k + 1) * D], k == 0, k == 1)
                last.then_inc(proj_done, 1)

            def ffn_up(g, j):
                if j == 0:
                    wait(pe, x2_ready, times(g, 1, 1))
                    wait(pe, gelu_done, times(g, 3))
                elif j == 1:
                    wait(pe, y_ready, times(g, 1))
                else:
                    wait(pe, gelu_done, times(g, 3, 1))
                x2 = X2T[:, :].rearrange("p (k i j) -> p k i j", k=2, i=GI)
                for c in (2 * j, 2 * j + 1):
                    for k in range(2):
                        last = mm(PSUM[:, 6 + j % 2, (c % 2) * GI * NMAIN:(c % 2 + 1) * GI * NMAIN],
                                  MW1[:, k * HID + c * 128:k * HID + (c + 1) * 128], x2[:, k, :, 0:NMAIN],
                                  k == 0, k == 1)
                last.then_inc(f1_done, 1)

            def ffn_down(g, u):
                if u == 0:
                    wait(pe, gelu_done, times(g, 3, 3))
                for c in range(HC):
                    last = mm(PSUM[:, 7, u * D:(u + 1) * D], HIDT[:, c, 2 * u:2 * u + 2, :],
                              MW2[:, c * D:(c + 1) * D], c == 0, c == HC - 1)
                if u == 1:
                    last.then_inc(f2_done, 1)

            def body(g, ahead, ffn, down):
                scores(g, 0)
                if ahead:
                    t1(g + 1)
                if down:
                    ffn_down(g - 2, 1)
                elif ffn:
                    f3_tiles(NPAIR - 1, 3)
                if not ffn:
                    f3_tiles(NPAIR - 1, 1, (0,))
                if ahead:
                    q_or_k(g + 1, 1)
                scores(g, 1)
                if ffn:
                    t2(g - 1, ahead)
                if ahead:
                    q_or_k(g + 1, 0)
                transpose_probs(g, 0)
                if ffn:
                    if not down:
                        pe.wait_ge(acc_read, NUNITS)
                    ffn_up(g - 1, 0)
                    ffn_up(g - 1, 1)
                attend(g, 0, ahead)
                transpose_probs(g, 1)
                if ffn:
                    ffn_up(g - 1, 2)
                else:
                    f3_tiles(NPAIR - 1, 1, (1,))
                transpose_out(g, 0, ffn)
                attend(g, 1, ahead)
                if ahead:
                    kt(g + 1)
                project(g, 0)
                transpose_out(g, 1, ffn)
                if ffn:
                    ffn_down(g - 1, 0)
                else:
                    f3_tiles(NPAIR - 1, 2)
                project(g, 1)

            pe.wait_ge(ld_cst, 16)
            pe.wait_ge(ld_attn, 32)
            pe.wait_ge(ld_moe, 32)
            pe.wait_ge(acc_read, LAST - 1)
            t1(0)
            q_or_k(0, 1)
            q_or_k(0, 0)
            f3_tiles(NPAIR - 1, 0)
            kt(0)
            pe.wait_ge(pads_zero, 2)
            body(0, True, False, False)
            body(1, True, True, False)
            with pe.Fori(2, NG - 1) as g:
                body(g, True, True, True)
            body(NG - 1, False, True, True)
            ffn_down(NG - 2, 1)
            t2(NG - 1, False)

            ffn_up(NG - 1, 0)
            ffn_up(NG - 1, 1)
            ffn_up(NG - 1, 2)

            pe.wait_ge(tok_ready, NG)
            pe.wait_ge(ld_gw, 16)
            gwv = GW[:, :].rearrange("p (k r a n) -> p k r a n", k=2, r=2, a=3)
            for r in range(2):
                for a in range(3):
                    for k in range(2):
                        last = mm(PSUM[B * a:B * a + B, 0, 2 * r:2 * r + 2], TOKv[:, k, r, a, :], gwv[:, k, r, a, :],
                                  k == 0, k == 1)
            last.then_inc(gate_done, 1)
            pe.wait_ge(ld_a1, 16)
            a2v = A2[:, :].rearrange("p (c e n) -> p c e n", c=HC, e=NEXP)

            def second_layer(r):
                if r == 0:
                    pe.wait_ge(ld_a2, 16)
                    pe.wait_ge(e1_read, 3)
                    pe.wait_ge(gate_max, 1)
                for c in range(HC):
                    last = mm(PSUM[0:96, 0, r * D:(r + 1) * D], HE[0][:, c, r, :], a2v[:, c, 3 + r, :], c == 0, c == HC - 1)
                if r == 1:
                    last.then_inc(e2_done, 1)

            for n, (a, c0, c1) in enumerate(((0, 0, 6), (1, 0, 6), (2, 0, 6), (3, 0, 3), (3, 3, 6), (4, 0, 3), (4, 3, 6))):
                w = 64 if a < 3 else 96
                nb = 1 + n if n < 5 else n - 4
                if n >= 5:
                    pe.wait_ge(e1_read, n - 4)
                for c in range(c0, c1):
                    for k in range(2):
                        rhs = TOKv[:, k, :, a, :] if a < 3 else TOKv[:, k, a - 3, :, :]
                        last = mm(PSUM[:, nb, (c - c0) * w:(c - c0 + 1) * w],
                                  A1[:, k, a, c * 128:(c + 1) * 128], rhs, k == 0, k == 1)
                last.then_inc(e1_done, 1)
                if n < 2:
                    ffn_down(NG - 1, n)
                elif n in (4, 6):
                    second_layer(n // 2 - 2)
            pe.wait_ge(e1_read, 7)
            for r in range(2):
                for c in range(HC):
                    for a in range(3):
                        last = mm(PSUM[B * a:B * a + B, 3 + r, 0:D], HE[1][:, c, r, B * a:B * a + B],
                                  a2v[:, c, a, :], c == 0, c == HC - 1)
                last.then_inc(e2_done, 1)

        @block.scalar
        def _(act):
            def read(n, done=1):
                act.wait_ge(acc_done, n + 1)

            def centre_taps(b, ready=None, value=0):
                units = batch_units(b)
                for j, (src, dst, f) in enumerate(units):
                    if ready is not None:
                        act.wait_ge(ready, value + j + 1)
                    nc.scalar.activation(dst, src, ACT.Copy, scale=v(f, 4)).then_inc(centre, 1)

            def haar_evict():
                for j, (m, c0, nco) in enumerate(HAAR_UNITS):
                    read(j)
                    src = bank(j, nco * D).rearrange("p (c o) -> p c o", o=D)
                    dst = WE[:, 2 * c0 + m:2 * (c0 + nco - 1) + m + 1:2, :]
                    nc.scalar.activation(dst[:, :, DA:2 * DA], src[:, :, 0:DA], ACT.Copy)
                    nc.scalar.activation(dst[:, :, 2 * DA + DB:], src[:, :, DA:D], ACT.Copy).then_inc(acc_read, 1)

            def embed_evict(c):
                n = first_unit[("e", c)]
                for j, (dst, bias) in enumerate(((GA[:, 0, c, :], "bias_loc"), (GA[:, 1, c, :], "bias_g"),
                                                 (GM[:, c, :], "bias_mixed"))):
                    read(n + j)
                    nc.scalar.activation(dst, bank(n + j, CT), ACT.Gelu, bias=v(bias)).then_inc(acc_read, 1)
                centre_taps(("dw", c), acc_read, n)

            def pointwise_evict(layer, i):
                n = first_unit[(layer, i)]
                for j, u in enumerate(units_of_pair(i)):
                    part = "_P" if j == 2 else "_A"
                    p = (j == 2)
                    read(n + j)
                    src = bank(n + j, CT)
                    if layer == "loc":
                        nc.scalar.activation(LOC[:, u, :], src, ACT.Identity, bias=v("plb" + part))
                        if i == 0 and j == 0:
                            act.wait_ge(gate_step, 8)
                        nc.scalar.activation(LM[:, u, :], src, ACT.Identity, bias=TH[:, 8 + p:9 + p],
                                             scale=TH[:, 4 + p:5 + p]).then_inc(acc_read, 1)
                    elif layer == "g":
                        nc.scalar.activation(G2[:, u, :], src, ACT.Gelu, bias=v("pgb" + part)).then_inc(acc_read, 1)
                    elif layer == "w2":
                        nc.scalar.activation(CUR[:, u, :], src, ACT.Copy, scale=TH[:, 2 + p:3 + p]).then_inc(acc_read, 1)
                    else:
                        nc.scalar.activation(CUR[:, u, :], src, ACT.Relu, bias=v(layer + "b" + part)).then_inc(acc_read, 1)


            def by_image(src, dst):
                s = src.rearrange("p (t i) -> p i t", i=CI)
                d = dst.rearrange("p (i r) -> p i r", r=ROWS)
                nc.scalar.activation(d[:, :, 0:NMAIN], s[:, :, 4:NTOK], ACT.Copy)
                return nc.scalar.activation(d[:, :, NMAIN:NTOK], s[:, :, 0:4], ACT.Copy)

            def d3(i):
                act.wait_ge(tap, taps_done(("f3", i)))
                act.wait_ge(d3_zero, 1)
                for j in range(2):
                    c = 2 * i + j
                    by_image(TAP[:, c, :], D3A[:, c * CI * ROWS:(c + 1) * CI * ROWS]).then_inc(d3_ready, 1)

            def depthwise_evict(layer, i):
                n = first_unit[("p%d" % layer, i)]
                read(n)
                if layer == 3:
                    act.wait_ge(d3_zero, 1)
                    by_image(bank(n, CT), D3P[:, i * CI * ROWS:(i + 1) * CI * ROWS]).then_inc(acc_read, 1)
                else:
                    nc.scalar.activation(TAP[:, 4 + i, :], bank(n, CT), ACT.Copy).then_inc(acc_read, 1)

            def f3_evict(i, q):
                n = first_unit[("f3", i)] + q
                read(n)
                nc.scalar.activation(T3[:, (4 * i + q) * 2 * D:(4 * i + q + 1) * 2 * D], bank(n, 2 * D),
                                     ACT.Copy).then_inc(acc_read, 1)

            act.wait_ge(ld_vec, 16)
            a0 = VEC["alpha_A"][0]
            nc.scalar.activation(TH[:, 0:2], V[:, a0:a0 + 2], ACT.Tanh).then_inc(tanh_done, 1)
            haar_evict()
            for c in range(NCH):
                embed_evict(c)
            for i in range(NPAIR):
                pointwise_evict("g", i)
                pointwise_evict("loc", i)
                pointwise_evict("w2", i)
                centre_taps(("f1", i), fused, nfused[("w2", i)] - 3)
            for i in range(NPAIR):
                if on_pe(("f1", i)):
                    depthwise_evict(1, i)
                pointwise_evict("f1", i)
                centre_taps(("f2", i), acc_read, first_unit[("f1", i)])
            depthwise_evict(2, 0)
            pointwise_evict("f2", 0)
            centre_taps(("f3", 0), fused, nfused[("f2", 0)] - 3)
            depthwise_evict(2, 1)
            pointwise_evict("f2", 1)
            centre_taps(("f3", 1), fused, nfused[("f2", 1)] - 3)
            d3(0)
            depthwise_evict(3, 0)
            for q in range(4):
                f3_evict(0, q)
            depthwise_evict(3, 1)

            def halves(n, cols):
                return PSUM[0:HD, n, 0:2 * cols].rearrange("p (k n) -> p k n", k=2)

            def xt(g):
                wait(act, t1_done, times(g, 1, 1))
                src = PSUM[0:HD, 1, :].rearrange("p (m j) -> p m j", j=ROWS)
                wait(act, q_done, times(g, 1))
                nc.scalar.activation(XT[:, :].rearrange("p (m j) -> p m j", j=S), src[:, :, 0:S], ACT.Copy).then_inc(xt_ready, 1)

            def x2t(g):
                wait(act, t2_done, times(g, 1, 1))
                wait(act, tok_ready, times(g, 1))
                wait(act, f1_done, times(g, 3))
                nc.scalar.activation(X2T[:, :], PSUM[0:HD, 1, :], ACT.Copy).then_inc(x2_ready, 1)

            def qt(g):
                wait(act, q_done, times(g, 1, 1))
                wait(act, s_done, times(g, 2))

                def tile(at, half):
                    return PSUM[half, 0, at:at + GI * S].rearrange("p (m j) -> p m j", j=S)

                nc.scalar.activation(QT[:, 0, :, 0:S], tile(0, slice(0, DA)), ACT.Copy)
                nc.scalar.activation(QT[0:DB, 1, :, 0:S], tile(GI * S, slice(0, DB)), ACT.Copy)
                keys = tile(GI * S, slice(DB, 2 * DB)).rearrange("p m (o j) -> p m o j", o=1)
                nc.scalar.activation(KT2[0:DB, GI:2 * GI, :, 0:S], keys.to_broadcast([DB, GI, 2, S]), ACT.Copy).then_inc(q_ready, 1)

            def kt2(g):
                wait(act, k_done, times(g, 1, 1))
                wait(act, kt_done, times(g, 2))
                wait(act, bd_ready, times(g, 1))
                keys = PSUM[:, 1, 0:GI * S].rearrange("p (m o j) -> p m o j", o=1, j=S)
                nc.scalar.activation(KT2[:, 0:GI, :, 0:S], keys.to_broadcast([128, GI, 2, S]), ACT.Copy).then_inc(k_ready, 1)

            def kv(g):
                for n in range(2):
                    wait(act, kt_done, times(g, 2, n + 1))
                    wait(act, av_done, times(g, 2))
                    for r in range(2):
                        half = slice(ROWS * r, ROWS * r + ROWS)
                        for i in range(2):
                            src = PSUM[half, 4 + n, i * D:(i + 1) * D].rearrange("p (a d) -> p a d", d=2 * DH)
                            dst = KV[half, 2 * n + i, r:NH:2, 0:DH]
                            last = nc.scalar.activation(dst, src[:, :, r * DH:(r + 1) * DH], ACT.Copy)
                    last.then_inc(kv_ready, 1)

            def exps(g, u):
                wait(act, d_ready, times(g, 2, u + 1))
                nc.scalar.activation(P[:, u, :, 0:S], P[:, u, :, 0:S], ACT.Exp, scale=SCALE).then_inc(p_ready, 1)

            def probs_lo(g, u):
                wait(act, pt_done, times(g, 2, u + 1))
                wait(act, av_done, times(g, 2, u))
                nc.scalar.activation(PT[:, 0:3, :].rearrange("p a i -> p (a i)"), PSUM[:, 4, 0:384], ACT.Copy).then_inc(pt_lo, 1)

            def ot(g, u):
                wait(act, ot_done, times(g, 2, u + 1))
                wait(act, proj_done, times(g, 2, u))
                nc.scalar.activation(OT[:, :], PSUM[0:HD, 1 - u, 0:256], ACT.Copy).then_inc(ot_ready, 1)

            def gelus(g, j):
                wait(act, f1_done, times(g, 3, j + 1))
                wait(act, f2_done, times(g, 1))
                for c in (2 * j, 2 * j + 1):
                    src = PSUM[:, 6 + j % 2, (c % 2) * GI * NMAIN:(c % 2 + 1) * GI * NMAIN].rearrange("p (i j) -> p i j", j=NMAIN)
                    last = nc.scalar.activation(HIDT[:, c, :, 0:NMAIN], src, ACT.Gelu, bias=v("moe_b1", c))
                last.then_inc(gelu_done, 1)

            def load_table(function):
                at = 1 + (function == ACT.Exp)
                nc.scalar.activation(NIL[:, at:at + 1], NIL[:, 0:1], function)

            def body(g, ahead, ffn, down=True):
                if ahead:
                    xt(g + 1)
                exps(g, 0)
                if ffn and not down:
                    f3_evict(NPAIR - 1, 3)
                if ahead:
                    kt2(g + 1)
                if ffn:
                    x2t(g - 1)
                if ahead:
                    qt(g + 1)
                probs_lo(g, 0)
                exps(g, 1)
                load_table(ACT.Gelu)
                if ffn:
                    gelus(g - 1, 0)
                    gelus(g - 1, 1)
                probs_lo(g, 1)
                if ffn:
                    gelus(g - 1, 2)
                else:
                    f3_evict(NPAIR - 1, 1)
                ot(g, 0)
                if ahead:
                    load_table(ACT.Exp)
                    kv(g + 1)
                ot(g, 1)
                if not ffn:
                    f3_evict(NPAIR - 1, 2)

            act.wait_ge(pads_zero, 2)
            xt(0)
            d3(1)
            kt2(0)
            qt(0)
            kv(0)
            f3_evict(NPAIR - 1, 0)
            load_table(ACT.Exp)
            body(0, True, False)
            body(1, True, True, False)
            with act.Fori(2, NG - 1) as g:
                body(g, True, True)
            body(NG - 1, False, True)
            x2t(NG - 1)
            for j in range(3):
                gelus(NG - 1, j)
            for n, (a, c0, c1) in enumerate(((0, 0, 6), (1, 0, 6), (2, 0, 6), (3, 0, 3), (3, 3, 6), (4, 0, 3), (4, 3, 6))):
                act.wait_ge(e1_done, n + 1)
                nb = 1 + n if n < 5 else n - 4
                w = 64 if a < 3 else 96
                for c in range(c0, c1):
                    src = PSUM[:, nb, (c - c0) * w:(c - c0 + 1) * w]
                    if a < 3:
                        src = src.rearrange("p (r n) -> p r n", r=2)
                        dst = HE[0][:, c, :, B * a:B * a + B]
                    else:
                        dst = HE[1][:, c, a - 3, :]
                    last = nc.scalar.activation(dst, src, ACT.Gelu, bias=v("exp_b1", a * HC + c))
                last.then_inc(e1_read, 1)
                if n == 0:
                    act.wait_ge(gate_max, 2)
                    nc.scalar.activation(GT[:, 4:8], GT[:, 4:8], ACT.Exp).then_inc(gate_exp, 1)
                    load_table(ACT.Gelu)

        @block.vector
        def _(dve):
            steps = [0]

            def step(ins):
                steps[0] += 1
                ins.then_inc(gate_step, 1)
                dve.wait_ge(gate_step, steps[0])

            nc.vector.memset(cureg[:, 0:CT], 0.0).then_inc(warm, 1)
            dve.sem_inc(y_free, 16)
            dve.wait_ge(tanh_done, 1)
            dve.wait_ge(ld_vec, 16)
            p0, q0 = VEC["plb_A"][0], VEC["b2_A"][0]
            step(nc.vector.tensor_scalar(TH[:, 2:4], TH[:, 0:2], 1.0, 0.5, ALU.add, ALU.mult))
            step(nc.vector.tensor_scalar(TH[:, 4:6], TH[:, 2:4], -1.0, 1.0, ALU.mult, ALU.add))
            step(nc.vector.tensor_tensor(TH[:, 6:8], TH[:, 2:4], V[:, q0:q0 + 2], ALU.mult))
            step(nc.vector.tensor_tensor(TH[:, 8:10], TH[:, 4:6], V[:, p0:p0 + 2], ALU.mult))
            step(nc.vector.tensor_tensor(TH[:, 8:10], TH[:, 8:10], TH[:, 6:8], ALU.add))
            nc.vector.memset(NIL[:, 0:1], 0.0)
            step(nc.vector.memset(NEG[:, :], -0.5))
            step(nc.vector.tensor_copy(TH[:, 0:2], TH[:, 2:4]))
            step(nc.vector.tensor_copy(TH[:, 6:8], TH[:, 4:6]))

            def taps(b, j0=0, j1=len(SHIFTS)):
                units = batch_units(b)
                before = taps_done(b) - 8 * len(units)
                for j in range(j0, j1):
                    dy, dx = SHIFTS[j]
                    for i, (src, dst, f) in enumerate(units):
                        if j == 0:
                            dve.wait_ge(centre, centres_done(b) - len(units) + i + 1)
                        else:
                            dve.wait_ge(tap, before + len(units) * (j - 1) + i + 1)
                        acc = shifted(dst, dy, dx, False)
                        nc.vector.scalar_tensor_tensor(out=acc, in0=shifted(src, dy, dx, True),
                                                       scalar=v(f, (dy + 1) * 3 + dx + 1), in1=acc,
                                                       op0=ALU.mult, op1=ALU.add).then_inc(tap, 1)

            def fuse(layer, i, other):
                n = first_unit[(layer, i)]
                for j, u in enumerate(units_of_pair(i)):
                    dve.wait_ge(acc_read, n + j + 1)
                    nc.vector.tensor_tensor(CUR[:, u, :], CUR[:, u, :], other[:, u, :], ALU.add).then_inc(fused, 1)

            for c in range(NCH):
                taps(("dw", c))
            for i in range(NPAIR):
                fuse("w2", i, LM)
                taps(("f1", i))
            for i in range(NPAIR):
                taps(("f2", i))
            fuse("f2", 0, LOC)
            taps(("f3", 0))
            fuse("f2", 1, LOC)

            def wait_bn(s, value):
                wait(dve, s, value)
                if not isinstance(value, int):
                    dve.sem_inc(passed, 1)

            def statistics(i, src, u):
                nc.vector.bn_stats(ST[:, (2 * i + u) * 6:(2 * i + u + 1) * 6], src).then_inc(stats[i], 1)

            def aggregate(i, u):
                return nc.vector.bn_aggr(MV[:, (2 * i + u) * 2:(2 * i + u + 1) * 2], ST[:, (2 * i + u) * 6:(2 * i + u + 1) * 6])

            def add_eps(i, u0, n):
                var = MV[:, (2 * i + u0) * 2:(2 * i + u0 + n) * 2].rearrange("p (u m) -> p u m", m=2)[:, :, 1]
                return nc.vector.tensor_scalar(VE[:, 2 * i + u0:2 * i + u0 + n], var, EPS, None, ALU.add)

            def mean(i, u):
                return MV[:, (2 * i + u) * 2:(2 * i + u) * 2 + 1]

            def both(row):
                return row.rearrange("p (o c) -> p o c", o=1).to_broadcast([128, 2, D])

            T3B2 = T3B.rearrange("p (u c) -> p u c", u=2)

            def tokens_a(g):
                t3 = T3[:, bass.ds(times(g, 2 * D), 2 * D)].rearrange("p (u c) -> p u c", u=2)
                nc.vector.tensor_tensor(T3B2, t3, both(BF3), ALU.add).then_inc(biased, 1)
                wait_bn(biased, times(g, 1, 1))
                for u in range(2):
                    statistics(0, T3B[:, u * D:(u + 1) * D], u)
                for u in range(2):
                    wait_bn(stats[0], times(g, 2, u + 1))
                    aggregate(0, u).then_inc(meanvar[0], 1)
                wait(dve, meanvar[0], times(g, 2, 2))
                add_eps(0, 0, 2).then_inc(var_eps[0], 1)

            def tokens_b(g):
                for u in range(2):
                    tile = T3B[:, u * D:(u + 1) * D]
                    nc.vector.scalar_tensor_tensor(out=tile, in0=tile, scalar=mean(0, u), in1=LNG,
                                                   op0=ALU.subtract, op1=ALU.mult).then_inc(norm3, 1)
                wait(dve, rstd_masked, times(g, 1, 1))
                for u in range(2):
                    wait(dve, norm3, times(g, 2, u + 1))
                    last = nc.vector.scalar_tensor_tensor(out=H[:, bass.ds(times(g, 2 * D, u * D), D)], in0=T3B[:, u * D:(u + 1) * D],
                                                          scalar=RS[:, 6 + u:7 + u], in1=LNB, op0=ALU.mult, op1=ALU.add)
                last.then_inc(h_ready, 1)

            def tokens_c(g):
                wait_bn(h_ready, times(g, 1, 1))
                for u in range(2):
                    statistics(1, H[:, bass.ds(times(g, 2 * D, u * D), D)], u)
                for u in range(2):
                    wait_bn(stats[1], times(g, 2, u + 1))
                    aggregate(1, u).then_inc(meanvar[1], 1)
                wait(dve, meanvar[1], times(g, 2, 2))
                add_eps(1, 0, 2).then_inc(var_eps[1], 1)

            def tokens_d(g):
                wait(dve, rstd[1], times(g, 1, 1))
                wait(dve, t1_done, times(g, 1))
                for u in range(2):
                    nc.vector.tensor_scalar(XN[:, u * D:(u + 1) * D], H[:, bass.ds(times(g, 2 * D, u * D), D)], mean(1, u),
                                            RS[:, 2 + u:3 + u], ALU.subtract, ALU.mult).then_inc(xn_ready, 1)

            def tokens(g):
                tokens_a(g)
                tokens_b(g)
                tokens_c(g)
                tokens_d(g)

            def block_diagonal(g, k):
                wait(dve, (k_ready, q_ready)[k], times(g, 1, 1))
                if k == 0:
                    wait(dve, s_done, times(g, 2))
                parts, heads, _ = QK_PARTS[k]
                for h in range(heads):
                    last = nc.vector.tensor_scalar(BD[k][:, :, h, :], KT2[0:parts, k * GI:(k + 1) * GI, 0, 0:S],
                                                   HMASK[0:parts, h:h + 1], None, ALU.mult)
                if k == 1:
                    last.then_inc(bd_ready, 1)

            def minus_max(g, u):
                wait(dve, s_done, times(g, 2, u + 1))
                for k, (_, heads, h0) in enumerate(QK_PARTS):
                    s = PSUM[:, 2 + k, 0:heads * S].rearrange("p (h j) -> p h j", j=S)
                    last = nc.vector.tensor_reduce(MX[:, u * NH + h0:u * NH + h0 + heads], s, AXX, ALU.max)
                last.then_inc(smax, 1)
                wait(dve, smax, times(g, 2, u + 1))
                wait(dve, pt_done, times(g, 2, u - 1))
                for k, (_, heads, h0) in enumerate(QK_PARTS):
                    s = PSUM[:, 2 + k, 0:heads * S].rearrange("p (h j) -> p h j", j=S)
                    m = MX[:, u * NH + h0:u * NH + h0 + heads].rearrange("p (h o) -> p h o", o=1).to_broadcast([128, heads, S])
                    last = nc.vector.tensor_tensor(P[:, u, h0:h0 + heads, 0:S], s, m, ALU.subtract)
                last.then_inc(d_ready, 1)

            def probs_hi(g, u):
                wait(dve, pt_done, times(g, 2, u + 1))
                wait(dve, av_done, times(g, 2, u))
                nc.vector.tensor_copy(PT[:, 3:6, :].rearrange("p a i -> p (a i)"), PSUM[:, 5, 0:384]).then_inc(pt_hi, 1)

            def normalise(g, u):
                wait(dve, av_done, times(g, 2, u + 1))
                av = PSUM[:, 0, 0:NH * 17].rearrange("p (h d) -> p h d", d=17)
                nc.vector.reciprocal(RD[:, :], av[:, :, DH]).then_inc(rden, 1)
                wait(dve, rden, times(g, 2, u + 1))
                wait(dve, ot_done, times(g, 2, u))
                r = RD[:, :].rearrange("p (h o) -> p h o", o=1).to_broadcast([128, NH, DH])
                nc.vector.tensor_tensor(OTOK[:, :].rearrange("p (h d) -> p h d", d=DH), av[:, :, 0:DH], r, ALU.mult).then_inc(o_ready, 1)

            def residual(g, u):
                wait(dve, proj_done, times(g, 2, u + 1))
                at = bass.ds(times(g, 2 * D, u * D), D)
                nc.vector.tensor_tensor(H2[:, at], PSUM[:, 1, 0:D], H[:, at], ALU.add).then_inc(h2_ready, 1)
                wait_bn(h2_ready, times(g, 2, u + 1))
                statistics(2, H2[:, at], u)
                wait_bn(stats[2], times(g, 2, u + 1))
                aggregate(2, u).then_inc(meanvar[2], 1)
                wait(dve, meanvar[2], times(g, 2, u + 1))
                add_eps(2, u, 1).then_inc(var_eps[2], 1)

            def norm2(g, u):
                wait(dve, rstd[2], times(g, 2, u + 1))
                wait(dve, t2_done, times(g, 1))
                at = bass.ds(times(g, 2 * D, u * D), D)
                nc.vector.tensor_scalar(XN2[:, u * D:(u + 1) * D], H2[:, at], mean(2, u), RS[:, 4 + u:5 + u],
                                        ALU.subtract, ALU.mult).then_inc(xn2_ready, 1)

            def ffn_out(g):
                wait(dve, f2_done, times(g, 1, 1))
                wait(dve, h2b_ready, times(g, 1, 1))
                wait(dve, y_free, times(g, 16, 16))
                nc.vector.tensor_tensor(Y, PSUM[:, 7, 0:2 * D], H2B[:, bass.ds(times(g, 2 * D), 2 * D)], ALU.add).then_inc(y_ready, 1)

            def body(g, two_ahead, ahead, before, out):
                minus_max(g, 0)
                if before:
                    norm2(g - 1, 0)
                    norm2(g - 1, 1)
                if two_ahead:
                    tokens_a(g + 2)
                minus_max(g, 1)
                if out:
                    ffn_out(g - 2)
                probs_hi(g, 0)
                if two_ahead:
                    tokens_b(g + 2)
                if two_ahead:
                    tokens_c(g + 2)
                normalise(g, 0)
                probs_hi(g, 1)
                if ahead:
                    block_diagonal(g + 1, 0)
                normalise(g, 1)
                if ahead:
                    block_diagonal(g + 1, 1)
                if two_ahead:
                    tokens_d(g + 2)
                residual(g, 0)
                residual(g, 1)

            dve.wait_ge(ld_bc, 16)
            dve.wait_ge(ld_cst, 16)
            taps(("f3", 1), 0, 6)
            dve.wait_ge(acc_read, first_unit[("f3", 0)] + 1)
            tokens_a(0)
            taps(("f3", 1), 6, 7)
            tokens_b(0)
            tokens_c(0)
            dve.wait_ge(acc_read, first_unit[("f3", 0)] + 4)
            tokens_a(1)
            tokens_d(0)
            taps(("f3", 1), 7, 8)
            tokens_b(1)
            tokens_c(1)
            dve.wait_ge(pads_zero, 2)
            block_diagonal(0, 0)
            block_diagonal(0, 1)
            tokens_d(1)
            body(0, True, True, False, False)
            body(1, True, True, True, False)
            dve.wait_ge(acc_read, NUNITS)
            with dve.Fori(2, NG - 2) as g:
                body(g, True, True, True, True)
            body(NG - 2, False, True, True, True)
            body(NG - 1, False, False, True, True)
            norm2(NG - 1, 0)
            norm2(NG - 1, 1)
            ffn_out(NG - 2)

            dve.wait_ge(gate_done, 1)
            lg = PSUM[0:96, 0, 0:4].rearrange("p (r n) -> p r n", r=2)

            def pairs(at):
                return GT[:, at:at + 4].rearrange("p (r n) -> p r n", r=2)

            def one(at):
                return GT[:, at:at + 2].rearrange("p (r o) -> p r o", o=1).to_broadcast([96, 2, 2])

            nc.vector.tensor_reduce(GT[:, 0:2], lg, AXX, ALU.max).then_inc(gate_dve, 1)
            dve.wait_ge(gate_dve, 1)
            nc.vector.tensor_tensor(pairs(4), lg, one(0), ALU.subtract).then_inc(gate_max, 2)
            dve.wait_ge(gate_exp, 1)
            chain = [1]

            def link(ins):
                chain[0] += 1
                ins.then_inc(gate_dve, 1)
                dve.wait_ge(gate_dve, chain[0])

            link(nc.vector.tensor_reduce(GT[:, 8:10], pairs(4), AXX, ALU.add))
            link(nc.vector.reciprocal(GT[:, 10:12], GT[:, 8:10]))
            link(nc.vector.tensor_tensor(pairs(12), pairs(4), one(10), ALU.mult))
            link(nc.vector.tensor_reduce(GT[:, 16:18], pairs(12), AXX, ALU.min))
            link(nc.vector.tensor_tensor(pairs(20), pairs(12), one(16), ALU.is_gt))
            link(nc.vector.tensor_tensor(pairs(24), pairs(20), pairs(12), ALU.mult))
            link(nc.vector.tensor_reduce(GT[:, 28:30], pairs(24), AXX, ALU.add))
            link(nc.vector.tensor_scalar(GT[:, 30:32], GT[:, 28:30], 1e-6, None, ALU.max))
            link(nc.vector.reciprocal(GT[:, 32:34], GT[:, 30:32]))
            link(nc.vector.tensor_tensor(pairs(36), pairs(24), one(32), ALU.mult))
            ffn_out(NG - 1)
            dve.wait_ge(e2_done, 1)
            for r in range(2):
                cols = slice(r * D, (r + 1) * D)
                nc.vector.tensor_tensor(EU[:, cols], PSUM[0:96, 0, cols], (EB3, EB4)[r][0:96, :], ALU.add).then_inc(e_mix, 1)
            dve.wait_ge(hc_loaded, 16 * NCLS)
            for r in range(2):
                cols = slice(r * D, (r + 1) * D)
                dve.wait_ge(e_mix, 1 + r)
                nc.vector.scalar_tensor_tensor(out=ER[:, cols], in0=EU[:, cols], scalar=GT[:, 36 + 2 * r:37 + 2 * r],
                                               in1=HC2[:, cols], op0=ALU.mult, op1=ALU.add).then_inc(e_mix, 1)
            for r in range(2):
                cols = slice(r * D, (r + 1) * D)
                second = slice((2 + r) * D, (3 + r) * D)
                dve.wait_ge(e2_done, 2 + r)
                nc.vector.tensor_tensor(EU[:, second], PSUM[0:96, 3 + r, 0:D], EBK[0:96, :], ALU.add).then_inc(e_mix, 1)
                dve.wait_ge(e_mix, 5 + 2 * r)
                nc.vector.scalar_tensor_tensor(out=ER[:, second], in0=EU[:, second], scalar=GT[:, 37 + 2 * r:38 + 2 * r],
                                               in1=ER[:, cols], op0=ALU.mult, op1=ALU.add).then_inc(e_mix, 1)

        @block.gpsimd
        def _(gp):
            gp.wait_ge(ld_vec, 16)
            gp.wait_ge(ld_cst, 16)
            for k, f in enumerate(("f1_P", "f2_P", "f3_P")):
                w = V[:, VEC[f][0]:VEC[f][0] + 9].rearrange("p (t o) -> p t o", o=1).to_broadcast([128, 9, 128])
                gp.tensor_tensor(DG[:, k, :, :], IDN.rearrange("p (o n) -> p o n", o=1).to_broadcast([128, 9, 128]), w,
                                 ALU.mult).then_inc(dg_ready, 1)
            gp.wait_ge(acc_done, first_unit[("loc", 1)] + 3)
            gp.memset(mixreg[:, 0:(B + B // 2) * ROWS], 0.0).then_inc(d3_zero, 1)
            gp.wait_ge(acc_done, first_unit[("w2", 1)] + 3)
            gp.wait_ge(fused, 6)
            gp.memset(QT[:, :, :, S:ROWS], 0.0)
            gp.memset(KT2[:, :, :, S:ROWS], 0.0)
            gp.memset(P[:, :, :, S:ROWS], 0.0)
            gp.memset(HIDT[:, :, :, NMAIN:ROWS], 0.0)
            gp.memset(KV, 0.0).then_inc(consts, 1)
            gp.wait_ge(consts, 1)
            for r in range(2):
                gp.memset(KV[ROWS * r:ROWS * r + ROWS, :, r:NH:2, DH:DH + 1], 1.0).then_inc(pads_zero, 1)
                gp.wait_ge(pads_zero, r + 1)

            def power(i, at, n):
                return gp.tensor_tensor(RS[:, at:at + n], VE[:, 2 * i + at % 2:2 * i + at % 2 + n],
                                        NEG[:, :].to_broadcast([128, n]), ALU.pow)

            def norm3(g):
                wait(gp, var_eps[0], times(g, 1, 1))
                power(0, 0, 2).then_inc(rstd[0], 1)
                wait(gp, rstd[0], times(g, 1, 1))
                gp.tensor_tensor(RS[:, 6:8], RS[:, 0:2], PMASK.to_broadcast([128, 2]), ALU.mult).then_inc(rstd_masked, 1)

            def norm1(g):
                wait(gp, var_eps[1], times(g, 1, 1))
                power(1, 2, 2).then_inc(rstd[1], 1)

            def norm2(g):
                for u in range(2):
                    wait(gp, var_eps[2], times(g, 2, u + 1))
                    gp.tensor_tensor(RS[:, 4 + u:5 + u], VE[:, 4 + u:5 + u], NEG[:, :], ALU.pow).then_inc(rstd[2], 1)
                at = bass.ds(times(g, 2 * D), 2 * D)
                gp.tensor_tensor(H2B[:, at].rearrange("p (u c) -> p u c", u=2), H2[:, at].rearrange("p (u c) -> p u c", u=2),
                                 MB2.rearrange("p (o c) -> p o c", o=1).to_broadcast([128, 2, D]), ALU.add).then_inc(h2b_ready, 1)

            def class_tokens(g):
                wait(gp, x2_ready, times(g, 1, 1))
                x2 = X2T[:, :].rearrange("p (k u e j) -> p k u e j", k=2, u=2, e=2)
                for k in range(2):
                    for r in range(2):
                        for e in range(2):
                            dst = TOKv[:, k, r, :, bass.ds(times(g, 2, 16 * e), 2)]
                            gp.tensor_copy(dst[:, 1:3, :], x2[:, k, :, e, NMAIN + r:NMAIN + 4:2].rearrange("p u a -> p a u"))
                            last = gp.tensor_copy(dst[:, 0, :], x2[:, k, :, e, NTOK + r])
                last.then_inc(tok_ready, 1)

            gp.wait_ge(ld_cst, 16)
            gp.wait_ge(ld_bc, 16)
            gp.wait_ge(gate_step, 6)
            for g in range(2):
                norm3(g)
                norm1(g)

            def body(g, ffn, two_ahead):
                if two_ahead:
                    norm3(g + 2)
                if ffn:
                    class_tokens(g - 1)
                if two_ahead:
                    norm1(g + 2)
                norm2(g)

            body(0, False, True)
            with gp.Fori(1, NG - 2) as g:
                body(g, True, True)
            body(NG - 2, True, False)
            body(NG - 1, True, False)
            class_tokens(NG - 1)


def _haar():
    y, x = np.meshgrid(np.arange(PATCH), np.arange(PATCH), indexing="ij")
    m = np.ones((PIX, PATCH, PATCH), np.float32)
    for band in range(PIX):
        for level in range(4):
            d = (band >> (2 * (3 - level))) & 3
            if d & 2:
                m[band] *= 1 - 2 * ((x >> level) & 1)
            if d & 1:
                m[band] *= 1 - 2 * ((y >> level) & 1)
    return (m / 16.0).reshape(PIX, PIX).astype(np.float32)


def kernel(**inputs):
    import concourse.bacc as bacc
    from concourse.bass_utils import run_bass_kernel_spmd as run

    a = {k: np.asarray(w) for k, w in inputs.items()}
    t = {k[len("L0_tok_"):]: w for k, w in a.items() if k.startswith("L0_tok_")}
    f = {k[len("L0_ffn_"):]: w for k, w in a.items() if k.startswith("L0_ffn_")}
    z = np.zeros
    f32 = np.float32

    def rows(m, k):
        return m.reshape(k, m.shape[0] // k, -1).transpose(1, 0, 2)

    x = a["x"].reshape(NCH, CI, CIN, G, PATCH, G, PATCH).transpose(2, 4, 6, 0, 3, 5, 1)
    x = x.reshape(KC, 128, NCH, CT).transpose(1, 2, 0, 3)
    plw = rows(t["pl_w"].reshape(D, KPIX).T, KC)
    w1k = t["pg_w1"].reshape(D, PIX, CIN).transpose(1, 2, 0).reshape(2, 128, CIN, D).transpose(1, 0, 2, 3)
    had = rows(_haar(), 2)
    blocks = []
    for name in ("pl_pw", "pg_pw", "pg_w2", "f1_pw", "f2_pw", "f3_pw"):
        w = t[name].reshape(D, D).T
        bd = z((128, 128), f32)
        bd[:DB, :DB] = w[DA:, DA:]
        bd[DB:, DB:] = w[DA:, DA:]
        blocks += [w[:DA], np.concatenate([w[DA:], w[DA:]]), bd]
    pww = np.concatenate(blocks, 1)

    def part_a(w):
        return w.reshape(D, -1)[:DA]

    def part_p(w):
        return np.concatenate([w.reshape(D, -1)[DA:]] * 2)

    def mixed(p, q):
        return np.concatenate([p.reshape(D, -1)[DA:], q.reshape(D, -1)[DA:]])

    vec = np.concatenate([
        part_a(t["pl_b"]), part_a(t["pg_b1"]), mixed(t["pl_b"], t["pg_b1"]), part_a(t["alpha"]), part_p(t["alpha"]),
        part_a(t["pl_pwb"]), part_p(t["pl_pwb"]), part_a(t["pg_pwb"]), part_p(t["pg_pwb"]),
        part_a(t["pg_b2"]), part_p(t["pg_b2"]), part_a(t["f1_pwb"]), part_p(t["f1_pwb"]),
        part_a(t["f2_pwb"]), part_p(t["f2_pwb"]),
        part_a(t["pl_dw"]), part_a(t["pg_dw"]), mixed(t["pl_dw"], t["pg_dw"]),
        part_a(t["f1_dw"]), part_p(t["f1_dw"]), part_a(t["f2_dw"]), part_p(t["f2_dw"]),
        part_a(t["f3_dw"]), part_p(t["f3_dw"]),
        f["moe0_b1"].reshape(HC, 128).T, f["A1_b"].reshape(NEXP * HC, 128).T], 1)

    def wide(row, n=128):
        return np.broadcast_to(row.reshape(1, D), (n, D))

    lnb = z((128, D), f32)
    for e in range(2):
        lnb[ROWS * e:ROWS * e + NTOK] = wide(t["ln_b"], NTOK)
        lnb[ROWS * e + NTOK] = a["cls_tok"].reshape(D)
        lnb[ROWS * e + NTOK + 1] = t["cls"].reshape(D)
    ebk = np.concatenate([wide(f["A2_b"][k], B) for k in range(3)] + [z((128 - 3 * B, D), f32)])
    bcw = np.concatenate([wide(t["f3_pwb"]), wide(t["ln_g"]), lnb, wide(f["moe0_b2"]), wide(f["A2_b"][3]),
                          wide(f["A2_b"][4]), ebk], 1)
    cst = z((128, 128 + HMAX + 1), f32)
    cst[:, :128] = np.eye(128)
    for h in range(HMAX):
        cst[h * DH:(h + 1) * DH, 128 + h] = 1.0
    for e in range(2):
        cst[ROWS * e:ROWS * e + NTOK, 128 + HMAX] = 1.0
    qkv = a["L0_attn_w_qkv"]
    wqk = rows(np.concatenate([qkv[:, :DA], qkv[:, D:D + DA], qkv[:, DA:D], qkv[:, D + DA:2 * D]], 1), 2)
    wout = rows(a["L0_attn_w_out"], 2)
    mw1 = rows(f["moe0_W1"], 2)
    mw2 = rows(f["moe0_W2"], HC)
    a1 = f["A1_W"].reshape(NEXP, 2, HD, HID).transpose(2, 1, 0, 3)
    a2 = f["A2_W"].reshape(NEXP, HC, 128, D).transpose(2, 1, 0, 3)
    gw = f["G_W"].reshape(3, 2, 2, HD, 2).transpose(3, 2, 1, 0, 4)

    arrays = {
        "x": x, "plw": plw, "w1k": w1k, "had": had, "pww": pww, "vec": vec, "bcw": bcw, "cst": cst,
        "wqk": wqk.reshape(HD, -1), "wout": wout.reshape(HD, -1), "mw1": mw1.reshape(HD, -1), "mw2": mw2.reshape(128, -1),
        "a1": a1, "a2": a2.reshape(128, -1), "gw": gw.reshape(HD, -1)}
    arrays = {k: np.ascontiguousarray(w) for k, w in arrays.items()}

    nc = bacc.Bacc("TRN2", target_bir_lowering=False, num_devices=1)
    args = [nc.dram_tensor(k, w.shape, mybir.dt.from_np(w.dtype), kind="ExternalInput").ap() for k, w in arrays.items()]
    args.append(nc.dram_tensor("out_main", (128, NT * D), F32, kind="ExternalOutput").ap())
    args.append(nc.dram_tensor("out_cls", (96, 2 * D), F32, kind="ExternalOutput").ap())
    args.append(nc.dram_tensor("h2x", (NCLS, 2, NT, D), F32, kind="Internal").ap())
    vit_tower(nc, *args)
    r = run(nc, [arrays], core_ids=[0]).results[0]
    main = np.asarray(r["out_main"]).reshape(2, ROWS, NT, D)[:, :NMAIN].transpose(2, 0, 1, 3).reshape(B, NMAIN, D)
    cls = np.asarray(r["out_cls"]).reshape(3, 2, NT, 2, D).transpose(2, 1, 0, 3, 4).reshape(B, NCLS, D)
    return np.concatenate([cls, main], 1)
```
